# Optimizing a Trainium2 kernel written in Bass

```python
import numpy as np
import jax
import jax.numpy as jnp

def _softmax(x, axis=-1):
    return jax.nn.softmax(x, axis=axis)

def _gelu(x):
    return jax.nn.gelu(x, approximate=True)

def _silu(x):
    return jax.nn.silu(x)

def _sigmoid(x):
    return jax.nn.sigmoid(x)

def _layernorm(x, axis=-1, eps=1e-05):
    m = jnp.mean(x, axis=axis, keepdims=True)
    v = jnp.var(x, axis=axis, keepdims=True)
    return (x - m) / jnp.sqrt(v + eps)

def _scatter_add(tgt, idx, src, axis=0):
    return tgt.at[idx].add(src)

def _segment_sum(src, seg, n):
    return jax.ops.segment_sum(src, seg, n)
kernel_name = 'mk_xattn_ffn_d2_seqx_r8_90dff3'

def setup_inputs(seed: int=0):
    np.random.seed(seed)
    _w = jnp.asarray

    def _rec_inputs():
        import jax
        import jax.numpy as jnp
        _rk = jax.random.key(seed)
        x = 7.22e-05 + 1 * jax.random.normal(jax.random.fold_in(_rk, 1), (64, 64, 128), jnp.float32)
        _lenS = 64 - jax.random.randint(jax.random.fold_in(_rk, 7), (64,), 0, max(1, 64 // 4) + 1, jnp.int32)
        _lenS2 = 64 - jax.random.randint(jax.random.fold_in(_rk, 8), (64,), 0, max(1, 64 // 4) + 1, jnp.int32)
        _ctx_1024P = jax.random.normal(jax.random.fold_in(_rk, 11), (64, 16, 128), jnp.float32)
        _ctx_1024c = jax.random.dirichlet(jax.random.fold_in(_rk, 511), 0.3 * jnp.ones((16,), jnp.float32), (64, 64))
        _ctx_1024t = jnp.einsum('bsk,bkd->bsd', _ctx_1024c, _ctx_1024P)
        _ctx_1024t = _ctx_1024t * jax.lax.rsqrt(jnp.mean(jnp.square(_ctx_1024t)) + 1e-12) * 0.953939
        ctx_1024 = 4.13588e-05 + 0.999923 * (_ctx_1024t + 0.3 * jax.random.normal(jax.random.fold_in(_rk, 611), (64, 64, 128), jnp.float32))
        return (x, ctx_1024)
    x, ctx_1024 = _rec_inputs()

    def _L0_xattn_setup():
        import jax, jax.numpy as jnp
        import numpy as np
        B, L, D, H = (4, 256, 128, 16)
        DK = D // H
        key = jax.random.key(seed)
        ks = jax.random.split(key, 8)

        def n(k, shape, s=1.0):
            return jax.random.normal(k, shape, dtype=jnp.float32) * s
        return {'q': n(ks[0], (B, L, D)), 'k': n(ks[1], (B, L, D)), 'v': n(ks[2], (B, L, D)), 'Wq': n(ks[3], (D, D), 0.02), 'bq': jnp.zeros((D,), jnp.float32), 'Wk': n(ks[4], (D, D), 0.02), 'bk': jnp.zeros((D,), jnp.float32), 'Wv': n(ks[5], (D, D), 0.02), 'bv': jnp.zeros((D,), jnp.float32), 'Wo': n(ks[6], (D, D), 0.02), 'bo': jnp.zeros((D,), jnp.float32), 'w_rel': n(ks[7], (2 * L - 1, DK), 0.02)}
    _L0_xattn_all = _L0_xattn_setup()
    _L0_xattn_in = {k: v for k, v in _L0_xattn_all.items() if k in ('Wq', 'bq', 'Wk', 'bk', 'Wv', 'bv', 'Wo', 'bo', 'w_rel')}
    del _L0_xattn_all

    def _L0_ffn_setup():
        import jax, jax.numpy as jnp
        import numpy as np
        from jax import lax
        B, S, D = (4, 256, 128)
        E = 8
        K = 2
        F = 408
        NORM_TOPK = True
        key = jax.random.key(seed)
        ks = jax.random.split(key, 8)
        sd = 0.02
        return {'x': jax.random.normal(ks[0], (B, S, D), jnp.float32), 'gate_w': jax.random.normal(ks[1], (E, D), jnp.float32) * sd, 'gate_b': jnp.zeros((E,), jnp.float32), 'up_w': jax.random.normal(ks[2], (E, F, D), jnp.float32) * sd, 'up_b': jnp.zeros((E, F), jnp.float32), 'gp_w': jax.random.normal(ks[3], (E, F, D), jnp.float32) * sd, 'gp_b': jnp.zeros((E, F), jnp.float32), 'down_w': jax.random.normal(ks[4], (E, D, F), jnp.float32) * sd, 'down_b': jnp.zeros((E, D), jnp.float32)}
    _L0_ffn_all = _L0_ffn_setup()
    _L0_ffn_in = {k: v for k, v in _L0_ffn_all.items() if k in ('gate_w', 'gate_b', 'up_w', 'up_b', 'gp_w', 'gp_b', 'down_w', 'down_b')}
    del _L0_ffn_all

    def _L1_xattn_setup():
        import jax, jax.numpy as jnp
        import numpy as np
        D_MODEL = 128
        B, S = (4, 256)
        key = jax.random.key(seed)
        ks = jax.random.split(key, 10)
        s = 1.0 / np.sqrt(D_MODEL)
        return {'k': jax.random.normal(ks[0], (B, S, D_MODEL), jnp.float32), 'v': jax.random.normal(ks[1], (B, S, D_MODEL), jnp.float32), 'q': jax.random.normal(ks[2], (B, S, D_MODEL), jnp.float32), 'Wk': jax.random.normal(ks[3], (D_MODEL, D_MODEL), jnp.float32) * s, 'Wv': jax.random.normal(ks[4], (D_MODEL, D_MODEL), jnp.float32) * s, 'bv': jnp.zeros((D_MODEL,), jnp.float32), 'Wq': jax.random.normal(ks[5], (D_MODEL, D_MODEL), jnp.float32) * s, 'bq': jnp.zeros((D_MODEL,), jnp.float32), 'Wo': jax.random.normal(ks[6], (D_MODEL, D_MODEL), jnp.float32) * s, 'bo': jnp.zeros((D_MODEL,), jnp.float32)}
    _L1_xattn_all = _L1_xattn_setup()
    _L1_xattn_in = {k: v for k, v in _L1_xattn_all.items() if k in ('Wk', 'Wv', 'bv', 'Wq', 'bq', 'Wo', 'bo')}
    del _L1_xattn_all

    def _L1_ffn_setup():
        import jax, jax.numpy as jnp
        import numpy as np
        NUM_EXPERTS = 8
        EXPERT_CAPACITY = 2.0
        DIM = 128
        HIDDEN_DIM = 512
        key = jax.random.key(seed)
        k_x, k_g, k_w1, k_w2 = jax.random.split(key, 4)
        n, t, d, f, e = (8, 128, DIM, HIDDEN_DIM, NUM_EXPERTS)
        x = jax.random.normal(k_x, (n, t, d), dtype=jnp.float32)
        gate_w = jax.random.normal(k_g, (e, d), dtype=jnp.float32) * 0.02
        w1 = jax.random.normal(k_w1, (e, d, f), dtype=jnp.float32) * 0.02
        w2 = jax.random.normal(k_w2, (e, f, d), dtype=jnp.float32) * 0.02
        return {'x': x, 'gate_w': gate_w, 'w1': w1, 'w2': w2}
    _L1_ffn_all = _L1_ffn_setup()
    _L1_ffn_in = {k: v for k, v in _L1_ffn_all.items() if k in ('gate_w', 'w1', 'w2')}
    del _L1_ffn_all
    return {'x': x, 'ctx_1024': ctx_1024, 'L0_xattn_Wq': _L0_xattn_in['Wq'], 'L0_xattn_bq': _L0_xattn_in['bq'], 'L0_xattn_Wk': _L0_xattn_in['Wk'], 'L0_xattn_bk': _L0_xattn_in['bk'], 'L0_xattn_Wv': _L0_xattn_in['Wv'], 'L0_xattn_bv': _L0_xattn_in['bv'], 'L0_xattn_Wo': _L0_xattn_in['Wo'], 'L0_xattn_bo': _L0_xattn_in['bo'], 'L0_xattn_w_rel': _L0_xattn_in['w_rel'], 'L0_ffn_gate_w': _L0_ffn_in['gate_w'], 'L0_ffn_gate_b': _L0_ffn_in['gate_b'], 'L0_ffn_up_w': _L0_ffn_in['up_w'], 'L0_ffn_up_b': _L0_ffn_in['up_b'], 'L0_ffn_gp_w': _L0_ffn_in['gp_w'], 'L0_ffn_gp_b': _L0_ffn_in['gp_b'], 'L0_ffn_down_w': _L0_ffn_in['down_w'], 'L0_ffn_down_b': _L0_ffn_in['down_b'], 'L1_xattn_Wk': _L1_xattn_in['Wk'], 'L1_xattn_Wv': _L1_xattn_in['Wv'], 'L1_xattn_bv': _L1_xattn_in['bv'], 'L1_xattn_Wq': _L1_xattn_in['Wq'], 'L1_xattn_bq': _L1_xattn_in['bq'], 'L1_xattn_Wo': _L1_xattn_in['Wo'], 'L1_xattn_bo': _L1_xattn_in['bo'], 'L1_ffn_gate_w': _L1_ffn_in['gate_w'], 'L1_ffn_w1': _L1_ffn_in['w1'], 'L1_ffn_w2': _L1_ffn_in['w2']}

def reference(x, ctx_1024, L0_xattn_Wq, L0_xattn_bq, L0_xattn_Wk, L0_xattn_bk, L0_xattn_Wv, L0_xattn_bv, L0_xattn_Wo, L0_xattn_bo, L0_xattn_w_rel, L0_ffn_gate_w, L0_ffn_gate_b, L0_ffn_up_w, L0_ffn_up_b, L0_ffn_gp_w, L0_ffn_gp_b, L0_ffn_down_w, L0_ffn_down_b, L1_xattn_Wk, L1_xattn_Wv, L1_xattn_bv, L1_xattn_Wq, L1_xattn_bq, L1_xattn_Wo, L1_xattn_bo, L1_ffn_gate_w, L1_ffn_w1, L1_ffn_w2):
    import jax
    import jax.numpy as jnp

    def _L0_xattn_ref(q, k, v, Wq, bq, Wk, bk, Wv, bv, Wo, bo, w_rel):
        import jax, jax.numpy as jnp
        import numpy as np
        B, L, D, H = (4, 256, 128, 16)
        DK = D // H
        bs, Lq, _ = q.shape
        qh = (q @ Wq.T + bq).reshape(bs, Lq, H, DK).transpose(0, 2, 1, 3)
        kh = (k @ Wk.T + bk).reshape(bs, -1, H, DK).transpose(0, 2, 1, 3)
        vh = (v @ Wv.T + bv).reshape(bs, -1, H, DK).transpose(0, 2, 1, 3)
        scores = jnp.einsum('bhid,bhjd->bhij', qh, kh)
        t = jnp.einsum('bhid,rd->bhir', qh, w_rel)
        idx = jnp.arange(Lq)[:, None] + jnp.arange(Lq)[None, :]
        bias = jnp.take_along_axis(t, idx[None, None], axis=-1)
        attn = jax.nn.softmax((scores + bias) / jnp.sqrt(jnp.float32(DK)), axis=-1)
        out = jnp.einsum('bhij,bhjd->bhid', attn, vh)
        concat = out.transpose(0, 2, 1, 3).reshape(bs, Lq, D)
        return concat @ Wo.T + bo

    def _L0_ffn_ref(x, gate_w, gate_b, up_w, up_b, gp_w, gp_b, down_w, down_b):
        import jax, jax.numpy as jnp
        import numpy as np
        from jax import lax
        B, S, D = (4, 256, 128)
        E = 8
        K = 2
        F = 408
        NORM_TOPK = True
        bs, slen, dim = x.shape
        xf = x.reshape(-1, dim)
        N = xf.shape[0]
        scores = jax.nn.softmax(xf @ gate_w.T + gate_b, axis=-1)
        top_w, top_idx = lax.top_k(scores, K)
        if NORM_TOPK:
            top_w = top_w / (top_w.sum(-1, keepdims=True) + 1e-20)
        comb = jnp.zeros((N, E), xf.dtype).at[jnp.arange(N)[:, None], top_idx].add(top_w)

        def step(acc, p):
            uw, ub, gw, gb, dw, db, w = p
            h = jax.nn.silu((xf @ gw.T + gb) * (xf @ uw.T + ub))
            return (acc + w[:, None] * (h @ dw.T + db), None)
        y0 = jnp.zeros_like(xf)
        y, _ = lax.scan(step, y0, (up_w, up_b, gp_w, gp_b, down_w, down_b, comb.T))
        return y.reshape(bs, slen, dim)

    def _L1_xattn_ref(k, v, q, Wk, Wv, bv, Wq, bq, Wo, bo):
        import jax, jax.numpy as jnp
        import numpy as np
        D_MODEL = 128
        B, S = (4, 256)
        kp = jnp.einsum('bsd,ed->bse', k, Wk)
        vp = jnp.einsum('bsd,ed->bse', v, Wv) + bv
        qp = jnp.einsum('bsd,ed->bse', q, Wq) + bq
        scale = 1.0 / jnp.sqrt(jnp.float32(kp.shape[-1]))
        scores = jnp.einsum('bqd,bkd->bqk', qp, kp) * scale
        probs = jax.nn.softmax(scores, axis=-1)
        ctx = jnp.einsum('bqk,bkd->bqd', probs, vp)
        return jnp.einsum('bqd,ed->bqe', ctx, Wo) + bo

    def _L1_ffn_ref(x, gate_w, w1, w2):
        import jax, jax.numpy as jnp
        import numpy as np
        NUM_EXPERTS = 8
        EXPERT_CAPACITY = 2.0
        DIM = 128
        HIDDEN_DIM = 512
        n, t, d = x.shape
        e = gate_w.shape[0]
        k = int(EXPERT_CAPACITY * t / e)
        scores = jnp.einsum('ntd,ed->nte', x, gate_w)
        probs = jax.nn.softmax(scores, axis=-1)
        g, m = jax.lax.top_k(probs.transpose(0, 2, 1), k)
        batch_idx = jnp.arange(n)[:, None, None]
        xin = x[batch_idx, m]
        h = jnp.einsum('nekd,edf->nekf', xin, w1)
        h = jax.nn.gelu(h, approximate=False)
        h = jnp.einsum('nekf,efd->nekd', h, w2)
        out_tok = g[..., None] * h
        out = jnp.zeros((n, t, d), dtype=x.dtype).at[batch_idx, m].add(out_tok)
        return out
    x = x + _L0_xattn_ref(_layernorm(x, axis=-1), ctx_1024, ctx_1024, L0_xattn_Wq, L0_xattn_bq, L0_xattn_Wk, L0_xattn_bk, L0_xattn_Wv, L0_xattn_bv, L0_xattn_Wo, L0_xattn_bo, L0_xattn_w_rel)
    x = x + _L0_ffn_ref(_layernorm(x, axis=-1), L0_ffn_gate_w, L0_ffn_gate_b, L0_ffn_up_w, L0_ffn_up_b, L0_ffn_gp_w, L0_ffn_gp_b, L0_ffn_down_w, L0_ffn_down_b)
    x = x + _L1_xattn_ref(ctx_1024, ctx_1024, _layernorm(x, axis=-1), L1_xattn_Wk, L1_xattn_Wv, L1_xattn_bv, L1_xattn_Wq, L1_xattn_bq, L1_xattn_Wo, L1_xattn_bo)
    x = x + _L1_ffn_ref(_layernorm(x, axis=-1), L1_ffn_gate_w, L1_ffn_w1, L1_ffn_w2)
    return x

_drawn_inputs = setup_inputs


def setup_inputs(seed=0):
    import zlib

    import numpy as np

    out = dict(_drawn_inputs(seed))
    spreads = {'L0_xattn_bq': (0.0, 0.8),
     'L0_xattn_bk': (0.0, 2.0),
     'L0_xattn_bv': (0.0, 0.358),
     'L0_xattn_bo': (0.0, 0.1),
     'L0_ffn_gate_b': (0.0, 0.1),
     'L0_ffn_up_b': (0.0, 0.8),
     'L0_ffn_gp_b': (0.0, 0.8),
     'L0_ffn_down_b': (0.0, 0.502),
     'L1_xattn_bv': (0.0, 0.455),
     'L1_xattn_bq': (0.0, 1.458),
     'L1_xattn_bo': (0.0, 0.437)}
    factors = {'L0_xattn_Wq': 8.0,
     'L0_xattn_Wk': 8.0,
     'L0_xattn_w_rel': 8.0,
     'L0_ffn_up_w': 7.872,
     'L0_ffn_gp_w': 7.929,
     'L0_ffn_down_w': 7.195,
     'L1_ffn_gate_w': 6.259,
     'L1_ffn_w1': 5.532,
     'L1_ffn_w2': 5.466}
    for name, (base, spread) in spreads.items():
        noise = np.random.default_rng([zlib.crc32(name.encode()), seed]).standard_normal(out[name].shape)
        drawn = base * np.exp(spread * noise) if base else spread * noise
        out[name] = jnp.asarray(drawn.astype(out[name].dtype))
    for name, factor in factors.items():
        out[name] = (out[name] * factor).astype(out[name].dtype)
    return out
```

```python
from contextlib import ExitStack

import concourse.bass as bass
from concourse import mybir

F32 = mybir.dt.float32
BF16 = mybir.dt.bfloat16
I32 = mybir.dt.int32
U32 = mybir.dt.uint32
ALU = mybir.AluOpType
ACT = mybir.ActivationFunctionType
AX_X = mybir.AxisListType.X
ds = bass.ds

P = 128
BATCH, SEQ, D = 64, 64, 128
NT = BATCH * SEQ
TILES = NT // P
H, DK = 16, 8
HP = H // 2
E = 8
F0, C0 = 408, 4
R0 = F0 // C0
F1, C1 = 512, 4
R1 = F1 // C1
TOPK = 2
SLOT_TILES = (NT * TOPK + E * (P - 1)) // P + 1
SLOT_TILES += SLOT_TILES % 2
CAP = 2 * SEQ // E
G = 4
GT = G * P
GROUPS = NT // GT
LN_EPS = 1e-5
NEG = -1e38
TERM_HIGH = (0, 1, 0)
TERM_W = (0, 0, 1)
QROWS = 2 * 3 * 16


class Tensors:
    pass


def at_least(eng, sem, value):
    if not (isinstance(value, int) and value <= 0):
        eng.wait_ge(sem, value)


def rounds(eng, count, body):
    body(0)
    with eng.Fori(1, count) as it:
        body(it)


def flat2(ap):
    return ap.rearrange("p a d -> p (a d)")


class Alloc:

    def __init__(self, nc, ctx, stage):
        self.nc, self.ctx, self.stage = nc, ctx, stage

    def sb(self, name, shape, dt=F32):
        return self.ctx.enter_context(self.nc.sbuf_tensor(f"{self.stage}_{name}", shape, dt))

    def ps(self, name, shape, dt=F32):
        return self.ctx.enter_context(self.nc.psum_tensor(f"{self.stage}_{name}", shape, dt))

    def sem(self, name):
        sem = self.nc.alloc_semaphore(f"{self.stage}_{name}")
        HELD.append(sem)
        return sem


HELD = []


def clear_semaphores(nc):
    nc.clear_and_free_semaphores(list(HELD))
    HELD.clear()
    nc.all_engine_barrier()


def windows(row):
    return bass.AP(tensor=row.tensor, offset=row.offset, ap=[row.ap[0], (2, SEQ // 2), (1, SEQ)])


def prepare(nc, I, T):
    with ExitStack() as ctx:
        a = Alloc(nc, ctx, "prepare")
        small = a.sb("small", [P, 8, P])
        gates = a.sb("gates", [E, 2, P])
        wrel = a.sb("wrel", [P, DK])
        wrel_t = a.sb("wrel_t", [DK, 2, P], BF16)
        up = a.sb("up", [R0, E * C0, P])
        gp = a.sb("gp", [R0, E * C0, P])
        down = a.sb("down", [P, E, F0])
        ring = [a.ps(f"ring{i}", [P, 512]) for i in range(4)]
        small_in, rel_in, up_in, gp_in, down_in, row_in = (
            a.sem(n) for n in ("small_in", "rel_in", "up_in", "gp_in", "down_in", "row_in"))
        ident_set, ident_ready, zero_set, rel_zero, rel_out = (
            a.sem(n) for n in ("ident_set", "ident_ready", "zero_set", "rel_zero", "rel_out"))
        turned, high_done, low_done, owned = (
            a.sem(n) for n in ("turned", "high_done", "low_done", "owned"))

        jobs = []
        for h in range(2):
            jobs.append((small_in, 160, [small[:, 4 * h + j, :] for j in range(4)], "small", h))
        jobs.append((small_in, 160, [gates[:, j, :] for j in range(2)], "gates", 0))
        jobs.append((rel_in, 16, [wrel[:, :]], "wrel", 0))
        for e in range(E):
            jobs.append((up_in, 16, [up[:, e * C0 + c, :] for c in range(C0)], "up", e))
            jobs.append((gp_in, 16, [gp[:, e * C0 + c, :] for c in range(C0)], "gp", e))
            jobs.append((down_in, 16, [down[:, e, c * R0:(c + 1) * R0] for c in range(C0)], "down", e))

        lows = [sum(k not in ("small", "gates") for _, _, _, k, _ in jobs[:n + 1]) for n in range(len(jobs))]

        def result(kind, bank, e, half):
            if kind == "small":
                return T.WT[:, 4 * e:4 * e + 4, :], bank[:, :].rearrange("p (j d) -> p j d", j=4)
            if kind == "gates":
                return T.gateT[:, :, :], bank[:, 0:2 * E].rearrange("p (j e) -> p j e", j=2)
            if kind == "wrel":
                return wrel_t[:, half, :], bank[0:DK, 0:P]
            if kind == "down":
                return T.WD[:, half, e, :], bank[0:R0, :]
            return (T.WU if kind == "up" else T.WG)[:, half, e, :], bank[:, 0:F0]

        with nc.Block() as block:
            @block.sync
            def _(sp):
                for j, n in enumerate(("L0_xattn_Wq", "L0_xattn_Wk", "L0_xattn_Wv", "L0_xattn_Wo",
                                       "L1_xattn_Wq", "L1_xattn_Wk", "L1_xattn_Wv", "L1_xattn_Wo")):
                    sp.dma_start(small[:, j, :], I[n]).then_inc(small_in, 16)
                sp.dma_start(gates[:, 0, :], I["L0_ffn_gate_w"]).then_inc(small_in, 16)
                sp.dma_start(gates[:, 1, :], I["L1_ffn_gate_w"]).then_inc(small_in, 16)
                sp.dma_start(wrel[:, :], I["L0_xattn_w_rel"][0:P, :]).then_inc(rel_in, 16)
                sp.dma_start(up[:, :, :], I["L0_ffn_up_w"].rearrange("e (c r) d -> r (e c) d", r=R0)).then_inc(up_in, 16)
                sp.dma_start(gp[:, :, :], I["L0_ffn_gp_w"].rearrange("e (c r) d -> r (e c) d", r=R0)).then_inc(gp_in, 16)
                sp.dma_start(down[:, :, :], I["L0_ffn_down_w"].rearrange("e d f -> d e f")).then_inc(down_in, 16)
                sp.wait_ge(low_done, 1)
                sp.wait_ge(rel_zero, 1)
                for par in range(2):
                    for s in range(3):
                        for h2 in range(2):
                            row = par * 48 + s * 16 + h2 * DK
                            sp.dma_start(T.Wrel[row:row + DK, :, h2 * SEQ:(h2 + 1) * SEQ],
                                         windows(wrel_t[:, TERM_W[s], par:P])).then_inc(rel_out, 16)
                sp.wait_ge(rel_out, 12 * 16)

            @block.gpsimd
            def _(pool):
                def row(out, name, n):
                    pool.dma_start(out, I[name].partition_broadcast(P)).then_inc(row_in, 16)
                row(T.bv0[:, :], "L0_xattn_bv", D)
                row(T.bo0[:, :], "L0_xattn_bo", D)
                row(T.bv1[:, :], "L1_xattn_bv", D)
                row(T.bo1[:, :], "L1_xattn_bo", D)
                row(T.gb0[:, :], "L0_ffn_gate_b", E)
                pool.dma_start(T.db0[:, :, :], I["L0_ffn_down_b"].partition_broadcast(P)).then_inc(row_in, 16)
                for j, n in enumerate(("L0_xattn_bq", "L0_xattn_bk", "L1_xattn_bq")):
                    pool.dma_start(T.bcol[:, j:j + 1], I[n].rearrange("(p a) -> p a", a=1)).then_inc(row_in, 16)
                for out, n in ((T.ub, "L0_ffn_up_b"), (T.gb, "L0_ffn_gp_b")):
                    for c in range(C0):
                        pool.dma_start(out[:, :, c], I[n][:, c * R0:(c + 1) * R0].rearrange("e r -> r e"),
                                       allow_slow_non_contiguous=True).then_inc(row_in, 16)
                pool.memset(T.identF[:, :], 0.0).then_inc(ident_set, 1)
                pool.memset(T.identB[:, :], 0.0).then_inc(ident_set, 1)
                pool.memset(T.sel[:, :, :, :], 0.0).then_inc(ident_set, 1)
                pool.memset(T.before[:, :], 0.0).then_inc(ident_set, 1)
                pool.wait_ge(ident_set, 4)
                for m in (T.identF, T.identB):
                    pool.affine_select(out=m[:, :], in_=m[:, :], compare_op=ALU.not_equal, fill=1.0, base=0,
                                       pattern=[[-1, P]], channel_multiplier=1).then_inc(ident_ready, 1)
                pool.affine_select(out=T.before[:, :], in_=T.before[:, :], compare_op=ALU.is_ge, fill=1.0, base=0,
                                   pattern=[[-1, P]], channel_multiplier=1).then_inc(ident_ready, 1)
                for base in (0, -32):
                    pool.affine_select(out=T.sel[:, :, :, :], in_=T.sel[:, :, :, :], compare_op=ALU.not_equal,
                                       fill=1.0, base=base, pattern=[[-2, HP], [-1, 2], [0, SEQ]],
                                       channel_multiplier=1).then_inc(ident_ready, 1)
                    pool.wait_ge(ident_ready, 4 if base == 0 else 5)
                pool.iota(T.row_i[:, :], pattern=[[0, 2]], base=0, channel_multiplier=1).then_inc(zero_set, 1)
                pool.iota(T.iota_i[:, :], pattern=[[1, 512]], base=0, channel_multiplier=0).then_inc(zero_set, 1)
                pool.iota(T.iota_p[:, :], pattern=[[0, 1]], base=0, channel_multiplier=1).then_inc(zero_set, 1)
                pool.wait_ge(row_in, 16 * 17)

            @block.tensor
            def _(pe):
                pe.wait_ge(ident_ready, 2)
                for n, (load, count, sources, kind, e) in enumerate(jobs):
                    pe.wait_ge(load, count)
                    if n >= 4:
                        pe.wait_ge(high_done, n - 3)
                        at_least(pe, low_done, lows[n - 4])
                    for j, src in enumerate(sources):
                        k, m = src.shape
                        w = {"small": P, "gates": E, "wrel": P, "down": P}.get(kind, R0)
                        last = pe.transpose(ring[n % 4][0:m, j * w:j * w + k], src, T.identF[0:k, 0:k])
                    last.then_inc(turned, 1)

            @block.scalar
            def _(act):
                for n, (_, _, _, kind, e) in enumerate(jobs):
                    act.wait_ge(turned, n + 1)
                    out, src = result(kind, ring[n % 4], e, 0)
                    act.copy(out, src).then_inc(high_done, 1)

            @block.vector
            def _(dve):
                dve.memset(T.Wrel[:, :, :], 0.0).then_inc(rel_zero, 1)
                dve.memset(T.ones[:, :], 1.0)
                dve.memset(T.half[:, :], -0.5).then_inc(owned, 1)
                dve.wait_ge(owned, 1)
                dve.memset(T.eps[:, :], LN_EPS)
                for a0, b0 in ((0, 0), (0, 64), (64, 0), (64, 64)):
                    dve.memset(T.mask[a0:a0 + 64, b0:b0 + 64], 0.0 if a0 == b0 else NEG)
                for n, (_, _, _, kind, e) in enumerate(jobs):
                    if kind in ("small", "gates"):
                        continue
                    dve.wait_ge(high_done, n + 1)
                    out, src = result(kind, ring[n % 4], e, 1)
                    high, _ = result(kind, ring[n % 4], e, 0)
                    dve.tensor_tensor(out, src, high, ALU.subtract).then_inc(low_done, 1)
                dve.wait_ge(zero_set, 3)
                dve.tensor_scalar(T.row_i[:, :], T.row_i[:, :], DK, None, ALU.bitwise_and).then_inc(owned, 1)
                dve.wait_ge(owned, 2)
                dve.tensor_scalar(T.owns[:, 0:1], T.row_i[:, 0:1], 0.0, None, ALU.is_equal)
                dve.tensor_scalar(T.owns[:, 1:2], T.row_i[:, 1:2], 0.0, None, ALU.is_gt)
                dve.tensor_copy(T.iotaB[:, :], T.iota_i[:, :])
                dve.tensor_copy(T.iotaP[:, :], T.iota_p[:, :])


class Norm:

    def __init__(self, a, T, name="ln"):
        self.T = T
        self.scratch = a.sb(f"{name}_scratch", [P, 1])
        self.stats = [a.sb(f"{name}_stats{v}", [P, G, 6]) for v in range(2)]
        self.mv = [a.sb(f"{name}_mv{v}", [P, G, 2]) for v in range(2)]
        self.var = [a.sb(f"{name}_var{v}", [P, G]) for v in range(2)]
        self.rstd = [a.sb(f"{name}_rstd{v}", [P, G]) for v in range(2)]
        self.xn = [a.sb(f"{name}_xn{v}", [P, G, D]) for v in range(2)]
        self.summed, self.mv_ready, self.var_ready, self.rstd_ready, self.xn_ready = (
            a.sem(f"{name}_{n}") for n in ("summed", "mv_ready", "var_ready", "rstd_ready", "xn_ready"))

    def sums(self, dve, g, v):
        for t in range(G):
            last = dve.bn_stats(self.stats[v][:, t, :], flat2(self.T.X[:, ds(g * G + t, 1), :]))
        last.then_inc(self.summed, 1)
        dve.wait_ge(self.summed, g + 1)
        dve.tensor_copy(self.scratch[:, 0:1], self.stats[v][:, G - 1, 0:1])
        for t in range(G):
            last = dve.bn_aggr(self.mv[v][:, t, :], self.stats[v][:, t, :])
        last.then_inc(self.mv_ready, 1)

    def root(self, pool, g, v):
        pool.wait_ge(self.mv_ready, g + 1)
        pool.tensor_tensor(self.var[v][:, :], self.mv[v][:, :, 1], self.T.eps[:, 0:G], ALU.add)\
            .then_inc(self.var_ready, 1)
        pool.wait_ge(self.var_ready, g + 1)
        pool.tensor_tensor(self.rstd[v][:, :], self.var[v][:, :], self.T.half[:, 0:G], ALU.pow)\
            .then_inc(self.rstd_ready, 1)

    def apply(self, dve, g, v):
        dve.wait_ge(self.rstd_ready, g + 1)
        for t in range(G):
            last = dve.tensor_scalar(self.xn[v][:, t, :], flat2(self.T.X[:, ds(g * G + t, 1), :]),
                                     self.mv[v][:, t, 0:1], self.rstd[v][:, t:t + 1], ALU.subtract, ALU.mult)
        last.then_inc(self.xn_ready, 1)


def project0(nc, I, T):
    with ExitStack() as ctx:
        a = Alloc(nc, ctx, "project0")
        ln = Norm(a, T)
        cx = [a.sb(f"cx{v}", [P, G, D]) for v in range(2)]
        xnT = [a.sb(f"xnT{v}", [P, GT]) for v in range(2)]
        q_split = [a.sb(f"q_split{v}", [P, 4, GT], BF16) for v in range(2)]
        k_full = [a.sb(f"k_full{v}", [P, GT]) for v in range(2)]
        k_split = [a.sb(f"k_split{v}", [P, 2, 2 * G, 2, SEQ], BF16) for v in range(2)]
        xt_ps = [a.ps(f"xt_ps{v}", [P, GT]) for v in range(2)]
        ct_ps = [a.ps(f"ct_ps{v}", [P, GT]) for v in range(2)]
        q_ps = [a.ps(f"q_ps{v}", [P, GT]) for v in range(2)]
        k_ps = [a.ps(f"k_ps{v}", [P, GT]) for v in range(2)]
        x_in = [a.sem(f"x_in{v}") for v in range(2)]
        c_in = [a.sem(f"c_in{v}") for v in range(2)]
        planes_out = [a.sem(f"planes_out{v}") for v in range(2)]
        zeroed, xt_done, ct_done, xt_copied, ct_copied, q_done, k_done, q_high, k_high, low, biased = (
            a.sem(n) for n in ("zeroed", "xt_done", "ct_done", "xt_copied", "ct_copied", "q_done", "k_done",
                               "q_high", "k_high", "low", "biased"))
        k_copied = a.sem("k_copied")
        x_d = I["x"].rearrange("b s d -> (b s) d").rearrange("(n p) d -> p n d", p=P)
        c_d = I["ctx_1024"].rearrange("b s d -> (b s) d").rearrange("(n p) d -> p n d", p=P)

        with nc.Block() as block:
            @block.sync
            def _(sp):
                def load(it):
                    for v in range(2):
                        g = 2 * it + v
                        at_least(sp, ct_done, g - 1)
                        sp.dma_start(T.X[:, ds(g * G, G), :], x_d[:, ds(g * G, G), :]).then_inc(x_in[v], 16)
                        sp.dma_start(cx[v][:, :, :], c_d[:, ds(g * G, G), :]).then_inc(c_in[v], 16)
                rounds(sp, GROUPS // 2, load)

            @block.gpsimd
            def _(pool):
                for v in range(2):
                    pool.memset(q_split[v][:, :, :], 0.0).then_inc(zeroed, 1)

                def body(it):
                    for v in range(2):
                        g = 2 * it + v
                        ln.root(pool, g, v)
                        pool.wait_ge(ln.xn_ready, g + 1)
                        pool.tensor_tensor(T.X[:, ds(g * G, G), :], T.X[:, ds(g * G, G), :],
                                           T.bo0[:, :].unsqueeze(1).to_broadcast([P, G, D]), ALU.add).then_inc(biased, 1)
                rounds(pool, GROUPS // 2, body)

            @block.vector
            def _(dve):
                dve.wait_ge(zeroed, 2)

                def body(it):
                    for v in range(2):
                        g = 2 * it + v
                        dve.wait_ge(x_in[v], 16 * (it + 1))
                        ln.sums(dve, g, v)
                        at_least(dve, xt_done, g - 1)
                        ln.apply(dve, g, v)
                        dve.wait_ge(ct_done, g + 1)
                        dve.tensor_copy(T.ctxT[:, ds(g * GT, GT)], ct_ps[v][:, :]).then_inc(ct_copied, 1)
                        dve.wait_ge(q_high, 2 * g + 2)
                        at_least(dve, planes_out[v], 32 * it)
                        for par in range(2):
                            dve.scalar_tensor_tensor(q_split[v][:, 2 + par, par::2], q_ps[v][:, par::2], T.bcol[:, 0:1],
                                                     q_split[v][:, par, par::2], ALU.add, ALU.subtract)
                        dve.wait_ge(k_high, 2 * g + 2)
                        for h2 in range(2):
                            last = dve.scalar_tensor_tensor(
                                k_split[v][:, 1, :, h2, :], k_full[v][:, :].rearrange("p (b j) -> p b j", j=SEQ),
                                T.owns[:, h2:h2 + 1], k_split[v][:, 0, :, h2, :], ALU.mult, ALU.subtract)
                        last.then_inc(low, 1)
                rounds(dve, GROUPS // 2, body)

            @block.tensor
            def _(pe):
                def body(it):
                    for v in range(2):
                        g = 2 * it + v
                        pe.wait_ge(c_in[v], 16 * (it + 1))
                        at_least(pe, ct_copied, g - 1)
                        for t in range(G):
                            last = pe.transpose(ct_ps[v][:, t * P:(t + 1) * P], cx[v][:, t, :], T.identF[:, :])
                        last.then_inc(ct_done, 1)
                        pe.wait_ge(ln.xn_ready, g + 1)
                        at_least(pe, xt_copied, g - 1)
                        for t in range(G):
                            last = pe.transpose(xt_ps[v][:, t * P:(t + 1) * P], ln.xn[v][:, t, :], T.identF[:, :])
                        last.then_inc(xt_done, 1)
                        at_least(pe, low, g - 1)
                        pe.wait_ge(ct_copied, g + 1)
                        pe.matmul(k_ps[v][:, :], T.WT[:, 1, :], T.ctxT[:, ds(g * GT, GT)], start=True, stop=True)\
                            .then_inc(k_done, 1)
                        pe.wait_ge(xt_copied, g + 1)
                        pe.matmul(q_ps[v][:, :], T.WT[:, 0, :], xnT[v][:, :], start=True, stop=True).then_inc(q_done, 1)
                rounds(pe, GROUPS // 2, body)

            @block.scalar
            def _(act):
                act.wait_ge(zeroed, 2)

                def body(it):
                    for v in range(2):
                        g = 2 * it + v
                        act.wait_ge(xt_done, g + 1)
                        at_least(act, q_done, g - 1)
                        act.copy(xnT[v][:, :], xt_ps[v][:, :]).then_inc(xt_copied, 1)
                        at_least(act, planes_out[v], 32 * it)
                        act.wait_ge(k_done, g + 1)
                        at_least(act, low, g - 1)
                        act.activation(k_full[v][:, :], k_ps[v][:, :], ACT.Identity, bias=T.bcol[:, 1:2])\
                            .then_inc(k_copied, 1)
                        act.wait_ge(k_copied, g + 1)
                        for h2 in range(2):
                            act.activation(k_split[v][:, 0, :, h2, :],
                                           k_full[v][:, :].rearrange("p (b j) -> p b j", j=SEQ),
                                           ACT.Identity, scale=T.owns[:, h2:h2 + 1]).then_inc(k_high, 1)
                        act.wait_ge(q_done, g + 1)
                        for par in range(2):
                            act.activation(q_split[v][:, par, par::2], q_ps[v][:, par::2], ACT.Identity,
                                           bias=T.bcol[:, 0:1]).then_inc(q_high, 1)
                        act.wait_ge(low, g + 1)
                        act.dma_start(T.q_dram[:, :, ds(g * GT, GT)].rearrange("n p t -> p n t"), q_split[v][:, :, :])\
                            .then_inc(planes_out[v], 16)
                        act.dma_start(T.k_dram[:, :, ds(g * 2 * GT, 2 * GT)].rearrange("n p t -> p n t"),
                                      k_split[v][:, :, :, :, :].rearrange("p n b h j -> p n (b h j)"))\
                            .then_inc(planes_out[v], 16)
                rounds(act, GROUPS // 2, body)
                for v in range(2):
                    act.wait_ge(planes_out[v], 32 * (GROUPS // 2))


def attend0(nc, I, T):
    with ExitStack() as ctx:
        a = Alloc(nc, ctx, "attend0")
        Q = [a.sb(f"Q{v}", [QROWS, HP, GT], BF16) for v in range(2)]
        K = [a.sb(f"K{v}", [QROWS, HP, 2 * GT], BF16) for v in range(2)]
        cg = [a.sb(f"cg{v}", [P, 2 * G, 2, SEQ]) for v in range(2)]
        scores = [a.sb(f"scores{v}", [P, HP * P]) for v in range(2)]
        probs = [a.sb(f"probs{v}", [P, HP * P]) for v in range(2)]
        V = [a.sb(f"V{v}", [P, HP, 2, 2, DK + 1]) for v in range(2)]
        maxes = a.sb("maxes", [P, P])
        shift = a.sb("shift", [48, P], BF16)
        rsum = a.sb("rsum", [P, HP, 2])
        heads = a.sb("heads", [P, HP, 2, DK])
        headsT = a.sb("headsT", [P, P])
        st = [a.ps(f"st{v}", [P, 2, 512]) for v in range(2)]
        turned_ps = a.ps("turned_ps", [P, 2, 512])
        v_ps = a.ps("v_ps", [P, 512])
        outp = a.ps("outp", [P, 512])
        mt_ps, ht_ps = turned_ps[:, 0, 0:P], turned_ps[:, 1, 0:P]
        o_ps, y_ps = outp[:, 0:HP * 36], outp[:, 384:512]
        planes_in = [a.sem(f"planes_in{v}") for v in range(2)]
        (set0, cg_ready, st_ready, copied, turned, maxed, m_copied, mt_ready, hi_set, shift_ready, shifted,
         exped, v_done, v_ready, pv_done, recip, heads_ready, ht_done, ht_copied, y_done, x_done) = (
            a.sem(n) for n in ("set0", "cg_ready", "st_ready", "copied", "turned", "maxed", "m_copied", "mt_ready",
                               "hi_set", "shift_ready", "shifted", "exped", "v_done", "v_ready", "pv_done", "recip",
                               "heads_ready", "ht_done", "ht_copied", "y_done", "x_done"))
        LOADS = 6 + 6
        PAIRS = 2 * G

        def steps(eng, step):
            for u in range(PAIRS):
                step(u, u)
            with eng.Fori(1, TILES // PAIRS) as it:
                for u in range(PAIRS):
                    step(it * PAIRS + u, u)
            for u in range(2):
                step(TILES + u, u)

        def live(p):
            return not isinstance(p, int) or 0 <= p < TILES

        with nc.Block() as block:
            @block.sync
            def _(sp):
                def load(it):
                    for v in range(2):
                        g = 2 * it + v
                        at_least(sp, st_ready, 2 * G * (g - 1))
                        for par in range(2):
                            for s in range(3):
                                row = par * 48 + s * 16
                                sp.dma_start(Q[v][row:row + 16, :, :],
                                             T.q_dram[2 * TERM_HIGH[s] + par, :, ds(g * GT, GT)]
                                             .rearrange("(hp r) t -> r hp t", r=16)).then_inc(planes_in[v], 16)
                                sp.dma_start(K[v][row:row + 16, :, :],
                                             T.k_dram[TERM_W[s], :, ds(g * 2 * GT, 2 * GT)]
                                             .rearrange("(hp r) t -> r hp t", r=16)).then_inc(planes_in[v], 16)
                rounds(sp, GROUPS // 2, load)

            @block.gpsimd
            def _(pool):
                for v in range(2):
                    pool.memset(V[v][:, :, :, :, :], 0.0).then_inc(set0, 1)
                pool.memset(maxes[:, :], 0.0).then_inc(set0, 1)
                pool.wait_ge(set0, 3)
                for v in range(2):
                    pool.memset(V[v][0:64, :, :, 0, DK:DK + 1], 1.0).then_inc(set0, 1)
                    pool.memset(V[v][64:P, :, :, 1, DK:DK + 1], 1.0).then_inc(set0, 1)
                pool.wait_ge(set0, 7)

                def body(it):
                    for v in range(2):
                        g = 2 * it + v
                        at_least(pool, v_done, G * (g - 1))
                        for dup in range(2):
                            pool.tensor_copy(cg[v][:, :, dup, :], T.ctxT[:, ds(g * GT, GT)]
                                             .rearrange("p (b t) -> p b t", t=SEQ)).then_inc(cg_ready, 1)
                rounds(pool, GROUPS // 2, body)

            @block.tensor
            def _(pe):
                def score(p, u, bank):
                    v, w = (u // G) % 2, u % 2
                    if bank == 0:
                        at_least(pe, exped, p - 1)
                        if u % G == 0:
                            pe.wait_ge(planes_in[v], 16 * LOADS * 1 if isinstance(p, int) else
                                       (p - u) * (2 * LOADS) + 16 * LOADS)
                    t0 = (u % G) * P
                    out = st[w][:, bank, :].rearrange("p (h b i) -> p h b i", h=4, b=2)
                    for h in range(4):
                        for b in range(2):
                            hp, t = bank * 4 + h, t0 + b * SEQ
                            pe.matmul(out[:, h, b, :], K[v][:, hp, 2 * t:2 * t + P], Q[v][:, hp, t:t + SEQ],
                                      start=(h == 0 and b == 0), stop=False, skip_group_check=True)
                    q4 = Q[v][:, bank * 4:bank * 4 + 4, t0:t0 + P].rearrange("r h (b i) -> r h b i", b=2)
                    for i in range(0, SEQ, 2):
                        last = pe.matmul(out[:, :, :, i:i + 2], T.Wrel[:, i // 2, :], q4[:, :, :, i:i + 2],
                                         start=False, stop=(i == SEQ - 2), skip_group_check=True)
                    last.then_inc(st_ready, 1)

                def turn(p, u):
                    w = u % 2
                    at_least(pe, shift_ready, p)
                    at_least(pe, ht_copied, p - 1)
                    for bank in range(2):
                        pe.wait_ge(copied, 2 * p + 1 + bank)
                        for h in range(4):
                            c = (bank * 4 + h) * P
                            last = pe.transpose(turned_ps[:, bank, h * P:(h + 1) * P], scores[w][:, c:c + P],
                                                T.identF[:, :])
                        last.then_inc(turned, 1)

                def subtract_max(p, u):
                    w = u % 2
                    pe.wait_ge(shift_ready, p + 1)
                    for hp in range(HP):
                        last = pe.matmul(st[w][:, hp // 4, (hp % 4) * P:(hp % 4 + 1) * P],
                                         T.sel[:, hp, :, :], shift[:, :],
                                         start=False, stop=True, skip_group_check=True)
                    last.then_inc(shifted, 1)

                def weigh(p, u):
                    w = u % 2
                    pe.wait_ge(exped, p + 1)
                    pe.wait_ge(v_ready, 2 * p + 2)
                    at_least(pe, x_done, p)
                    for hp in range(HP):
                        last = pe.matmul(o_ps[:, hp * 36:hp * 36 + 36], probs[w][:, hp * P:(hp + 1) * P],
                                         V[w][:, hp, :, :, :].rearrange("p b h d -> p (b h d)"),
                                         start=True, stop=True)
                    last.then_inc(pv_done, 1)

                def values(p, u):
                    v = (u // G) % 2
                    if u % G == 0:
                        pe.wait_ge(cg_ready, 2 * (1 + v) if isinstance(p, int) else (p - u) // G * 2 + 2 * (1 + v))
                    at_least(pe, v_ready, 2 * p)
                    for b in range(2):
                        last = pe.matmul(v_ps[:, b * P:(b + 1) * P],
                                         cg[v][:, (u % G) * 2 + b, :, :], T.WT[:, 2, :], start=True, stop=True)
                    last.then_inc(v_done, 1)

                def step(p, u):
                    u1, u2 = (u - 1) % PAIRS, (u - 2) % PAIRS
                    if live(p):
                        score(p, u, 0)
                    if live(p - 1):
                        turn(p - 1, u1)
                    if live(p - 2):
                        weigh(p - 2, u2)
                    if live(p):
                        score(p, u, 1)
                    if live(p - 1):
                        pe.wait_ge(m_copied, p)
                        pe.transpose(mt_ps, maxes[:, :], T.identF[:, :]).then_inc(mt_ready, 1)
                    if live(p - 2):
                        pe.wait_ge(heads_ready, 2 * (p - 2) + 2)
                        pe.wait_ge(maxed, 2 * TILES if isinstance(p, int) and p > TILES else 2 * p)
                        pe.transpose(ht_ps, heads[:, :, :, :].rearrange("p a b d -> p (a b d)"), T.identF[:, :])\
                            .then_inc(ht_done, 1)
                    if live(p - 1):
                        subtract_max(p - 1, u1)
                    if live(p):
                        values(p, u)
                    if live(p - 2):
                        pe.wait_ge(ht_copied, p - 1)
                        pe.matmul(y_ps, headsT[:, :], T.WT[:, 3, :], start=True, stop=True).then_inc(y_done, 1)
                steps(pe, step)

            @block.scalar
            def _(act):
                def step(p, u):
                    if live(p):
                        at_least(act, turned, 2 * (p - 1))
                        for bank in range(2):
                            act.wait_ge(st_ready, 2 * p + 1 + bank)
                            act.copy(scores[u % 2][:, bank * 512:(bank + 1) * 512], st[u % 2][:, bank, :])\
                                .then_inc(copied, 1)
                    if live(p - 2):
                        act.wait_ge(ht_done, p - 1)
                        at_least(act, y_done, p - 2)
                        act.copy(headsT[:, :], ht_ps).then_inc(ht_copied, 1)
                    if live(p - 1):
                        act.wait_ge(shifted, p)
                        at_least(act, pv_done, p - 2)
                        act.activation(probs[(u - 1) % 2][:, :], st[(u - 1) % 2][:, :, :].rearrange("p a n -> p (a n)"),
                                       ACT.Exp, scale=DK ** -0.5).then_inc(exped, 1)
                steps(act, step)

            @block.vector
            def _(dve):
                dve.wait_ge(set0, 7)

                def step(p, u):
                    if live(p - 1):
                        q = p - 1
                        at_least(dve, mt_ready, q)
                        for bank in range(2):
                            dve.wait_ge(turned, 2 * q + 1 + bank)
                            dve.tensor_reduce(maxes[:, bank * 8:bank * 8 + 8],
                                              turned_ps[:, bank, :].rearrange("p (h j) -> p h j", j=SEQ),
                                              AX_X, ALU.max).then_inc(maxed, 1)
                        dve.wait_ge(maxed, 2 * q + 2)
                        dve.tensor_copy(maxes[:, 32:48], maxes[:, 0:16]).then_inc(m_copied, 1)
                    if live(p - 2):
                        q = p - 2
                        dve.wait_ge(pv_done, q + 1)
                        at_least(dve, ht_done, q)
                        o = o_ps.rearrange("p (hp b h d) -> p hp b h d", hp=HP, b=2, h=2)
                        for b in range(2):
                            rows = slice(64 * b, 64 * b + 64)
                            dve.reciprocal(rsum[rows, :, :], o[rows, :, b, :, DK]).then_inc(recip, 1)
                        for b in range(2):
                            rows = slice(64 * b, 64 * b + 64)
                            dve.wait_ge(recip, 2 * q + 1 + b)
                            dve.tensor_tensor(heads[rows, :, :, :], o[rows, :, b, :, 0:DK],
                                              rsum[rows, :, :].unsqueeze(3).to_broadcast([64, HP, 2, DK]), ALU.mult)\
                                .then_inc(heads_ready, 1)
                    if live(p - 1):
                        q = p - 1
                        dve.wait_ge(mt_ready, q + 1)
                        at_least(dve, shifted, q)
                        dve.tensor_scalar(shift[:, :], mt_ps[0:48, :], -1.0, None, ALU.mult).then_inc(hi_set, 1)
                        dve.wait_ge(hi_set, q + 1)
                        dve.scalar_tensor_tensor(shift[32:48, :], mt_ps[32:48, :], -1.0, shift[32:48, :],
                                                 ALU.mult, ALU.subtract).then_inc(shift_ready, 1)
                    if live(p):
                        dve.wait_ge(v_done, p + 1)
                        at_least(dve, pv_done, p - 1)
                        for h2 in range(2):
                            rows = slice(64 * h2, 64 * h2 + 64)
                            for b in range(2):
                                last = dve.tensor_tensor(
                                    V[u % 2][rows, :, b, h2, 0:DK],
                                    v_ps[rows, b * P:(b + 1) * P].rearrange("p (hp h d) -> p hp h d", hp=HP, h=2)[:, :, h2, :],
                                    T.bv0[rows, :].rearrange("p (hp h d) -> p hp h d", hp=HP, h=2)[:, :, h2, :], ALU.add)
                            last.then_inc(v_ready, 1)
                    if live(p - 2):
                        q = p - 2
                        dve.wait_ge(y_done, q + 1)
                        x = flat2(T.X[:, ds(q, 1), :])
                        dve.tensor_tensor(x, y_ps, x, ALU.add).then_inc(x_done, 1)
                steps(dve, step)


class Scores:

    def __init__(self, a, T, gate):
        self.T, self.gate = T, gate
        self.ln = Norm(a, T)
        self.SC = a.sb("SC", [P, TILES, E])
        self.xnT = [a.sb(f"xnT{v}", [P, GT]) for v in range(2)]
        self.xt_ps = [a.ps(f"xt_ps{v}", [P, GT]) for v in range(2)]
        self.s_ps = [a.ps(f"s_ps{v}", [P, G * E]) for v in range(2)]
        self.xt_done, self.xt_copied, self.s_done, self.s_ready, self.high, self.low = (
            a.sem(n) for n in ("xt_done", "xt_copied", "s_done", "s_ready", "high", "low"))

    def pool(self, pool):
        def body(it):
            for v in range(2):
                g = 2 * it + v
                self.ln.root(pool, g, v)
                pool.wait_ge(self.ln.xn_ready, g + 1)
                pool.tensor_copy(self.T.XHL[:, ds(g * G, G), 0, :], self.ln.xn[v][:, :, :]).then_inc(self.high, 1)
        rounds(pool, GROUPS // 2, body)

    def vector(self, dve):
        def body(it):
            for v in range(2):
                g = 2 * it + v
                self.ln.sums(dve, g, v)
                at_least(dve, self.xt_done, g - 1)
                self.ln.apply(dve, g, v)
                dve.wait_ge(self.high, g + 1)
                dve.tensor_tensor(self.T.XHL[:, ds(g * G, G), 1, :], self.ln.xn[v][:, :, :],
                                  self.T.XHL[:, ds(g * G, G), 0, :], ALU.subtract).then_inc(self.low, 1)
                dve.wait_ge(self.s_done, g + 1)
                out = self.SC[:, ds(g * G, G), :]
                s = self.s_ps[v][:, :].rearrange("p (t e) -> p t e", e=E)
                if self.gate == 0:
                    dve.tensor_tensor(out, s, self.T.gb0[:, :].unsqueeze(1).to_broadcast([P, G, E]), ALU.add)\
                        .then_inc(self.s_ready, 1)
                else:
                    dve.tensor_copy(out, s).then_inc(self.s_ready, 1)
        rounds(dve, GROUPS // 2, body)

    def tensor(self, pe):
        def body(it):
            for v in range(2):
                g = 2 * it + v
                pe.wait_ge(self.ln.xn_ready, g + 1)
                at_least(pe, self.xt_copied, g - 1)
                for t in range(G):
                    last = pe.transpose(self.xt_ps[v][:, t * P:(t + 1) * P], self.ln.xn[v][:, t, :],
                                        self.T.identF[:, :])
                last.then_inc(self.xt_done, 1)
                pe.wait_ge(self.xt_copied, g + 1)
                at_least(pe, self.s_ready, g - 1)
                for t in range(G):
                    last = pe.matmul(self.s_ps[v][:, t * E:(t + 1) * E], self.xnT[v][:, t * P:(t + 1) * P],
                                     self.T.gateT[:, self.gate, :], start=True, stop=True)
                last.then_inc(self.s_done, 1)
        rounds(pe, GROUPS // 2, body)

    def scalar(self, act):
        def body(it):
            for v in range(2):
                g = 2 * it + v
                act.wait_ge(self.xt_done, g + 1)
                at_least(act, self.s_done, g - 1)
                act.copy(self.xnT[v][:, :], self.xt_ps[v][:, :]).then_inc(self.xt_copied, 1)
        rounds(act, GROUPS // 2, body)


class Chain:

    def __init__(self, eng, sem):
        self.eng, self.sem, self.n = eng, sem, 0

    def __call__(self, ins):
        self.n += 1
        ins.then_inc(self.sem, 1)
        self.eng.wait_ge(self.sem, self.n)


def spread(ap, n):
    return ap.unsqueeze(2).to_broadcast([ap.shape[0], ap.shape[1], n])


def softmax_first(dve, chain, sc, SC, peak, shifted_ready):
    dve.wait_ge(sc.s_ready, GROUPS)
    chain(dve.tensor_reduce(peak, SC, AX_X, ALU.max))
    dve.tensor_tensor(SC, SC, spread(peak, E), ALU.subtract).then_inc(shifted_ready, 1)


def softmax_last(dve, chain, PR, total, exp_ready):
    dve.wait_ge(exp_ready, 1)
    chain(dve.tensor_reduce(total, PR, AX_X, ALU.add))
    chain(dve.reciprocal(total, total))
    chain(dve.tensor_tensor(PR, PR, spread(total, E), ALU.mult))


def route0(nc, I, T):
    with ExitStack() as ctx:
        a = Alloc(nc, ctx, "route0")
        sc = Scores(a, T, 0)
        PR, eq, rest, A, one1, one2 = (a.sb(n, [P, TILES, E]) for n in ("PR", "eq", "rest", "A", "one1", "one2"))
        peak, total, p1, p2, top = (a.sb(n, [P, TILES]) for n in ("peak", "total", "p1", "p2", "top"))
        rank8, count, padded, begin, adjust, ones8 = (a.sb(n, [P, E]) for n in ("rank8", "count", "padded", "begin",
                                                                              "adjust", "ones8"))
        padded_i = a.sb("padded_i", [P, E], I32)
        chosen = a.sb("chosen", [P, E, TILES], BF16)
        onesf, csum, pre, tot = (a.sb(n, [P, E * TILES]) for n in ("onesf", "csum", "pre", "tot"))
        slot_f = a.sb("slot_f", [P, TOPK, TILES])
        reach = a.sb("reach", [P, SLOT_TILES, E])
        first = a.sb("first", [P, SLOT_TILES])
        owner = a.sb("owner", [P, SLOT_TILES])
        zeros = a.sb("zeros", [P, 8, 2 * D], BF16)
        pre_ps = a.ps("pre_ps", [P, 512])
        tot_ps = a.ps("tot_ps", [P, 512])
        zset, zero_out, shifted_ready, exp_ready, chosen_ready, counted, step, slots_ready, sent = (
            a.sem(n) for n in ("zset", "zero_out", "shifted_ready", "exp_ready", "chosen_ready", "counted", "step",
                               "slots_ready", "sent"))
        with nc.Block() as block:
            @block.sync
            def _(sp):
                sp.wait_ge(zset, 1)
                for c in range(SLOT_TILES // 8):
                    sp.dma_start(T.xs_dram[c * 8 * P:(c + 1) * 8 * P, :].rearrange("(n p) d -> p n d", p=P),
                                 zeros[:, :, :]).then_inc(zero_out, 16)
                sp.wait_ge(zero_out, 16 * (SLOT_TILES // 8))

            @block.gpsimd
            def _(pool):
                pool.memset(zeros[:, :, :], 0.0).then_inc(zset, 1)
                sc.pool(pool)
                pool.wait_ge(zero_out, 16 * (SLOT_TILES // 8))
                pool.wait_ge(sc.low, GROUPS)
                pool.wait_ge(slots_ready, 1)
                for t in range(TILES):
                    for k in range(TOPK):
                        pool.indirect_dma_start(
                            T.xs_dram[:, :], bass.IndirectOffsetOnAxis(ap=T.slot[:, k, t:t + 1].bitcast(U32), axis=0),
                            T.XHL[:, t, :, :].rearrange("p a d -> p (a d)"), None).then_inc(sent, 16)
                pool.wait_ge(sent, 16 * TILES * TOPK)

            @block.tensor
            def _(pe):
                sc.tensor(pe)
                pe.wait_ge(chosen_ready, 1)
                m = chosen[:, :, :].rearrange("p e t -> p (e t)")
                pe.matmul(pre_ps[:, 0:E * TILES], T.before[:, :], m, start=True, stop=True)
                pe.matmul(tot_ps[:, 0:E * TILES], T.ones[:, :], m, start=True, stop=True).then_inc(counted, 1)

            @block.scalar
            def _(act):
                sc.scalar(act)
                act.wait_ge(shifted_ready, 1)
                act.activation(PR[:, :, :], sc.SC[:, :, :], ACT.Exp).then_inc(exp_ready, 1)

            @block.vector
            def _(dve):
                chain = Chain(dve, step)
                dve.memset(onesf[:, :], 1.0)
                dve.memset(ones8[:, :], 1.0)
                dve.tensor_scalar(first[:, :], T.iotaB[:, 0:SLOT_TILES], float(P), None, ALU.mult)
                chain(dve.tensor_scalar(rank8[:, :], T.iotaB[:, 0:E], -1.0, float(E), ALU.mult, ALU.add))
                sc.vector(dve)
                softmax_first(dve, chain, sc, sc.SC[:, :, :], peak[:, :], shifted_ready)
                softmax_last(dve, chain, PR[:, :, :], total[:, :], exp_ready)
                ranks = rank8[:, :].unsqueeze(1).to_broadcast([P, TILES, E])
                src = PR
                for value, one in ((p1, one1), (p2, one2)):
                    chain(dve.tensor_reduce(value[:, :], src[:, :, :], AX_X, ALU.max))
                    chain(dve.tensor_tensor(eq[:, :, :], src[:, :, :], spread(value[:, :], E), ALU.is_equal))
                    chain(dve.tensor_tensor(eq[:, :, :], eq[:, :, :], ranks, ALU.mult))
                    chain(dve.tensor_reduce(top[:, :], eq[:, :, :], AX_X, ALU.max))
                    chain(dve.tensor_tensor(one[:, :, :], eq[:, :, :], spread(top[:, :], E), ALU.is_equal))
                    if one is one1:
                        chain(dve.scalar_tensor_tensor(rest[:, :, :], one1[:, :, :], -2.0, PR[:, :, :], ALU.mult, ALU.add))
                    src = rest
                chain(dve.tensor_tensor(chosen[:, :, :].rearrange("p e t -> p t e"), one1[:, :, :], one2[:, :, :], ALU.add))
                dve.sem_inc(chosen_ready, 1)
                chain(dve.tensor_tensor(total[:, :], p1[:, :], p2[:, :], ALU.add))
                chain(dve.tensor_scalar(total[:, :], total[:, :], 1e-20, None, ALU.add))
                chain(dve.reciprocal(total[:, :], total[:, :]))
                dve.tensor_tensor(T.share[:, 0, :], p1[:, :], total[:, :], ALU.mult)
                dve.tensor_tensor(T.share[:, 1, :], p2[:, :], total[:, :], ALU.mult)
                dve.wait_ge(counted, 1)
                chain(dve.tensor_copy(tot[:, :], tot_ps[:, 0:E * TILES]))
                chain(dve.tensor_copy(pre[:, :], pre_ps[:, 0:E * TILES]))
                chain(dve.tensor_reduce(count[:, :], tot[:, :].rearrange("p (e t) -> p e t", e=E), AX_X, ALU.add))
                chain(dve.tensor_scalar(padded[:, :], count[:, :], float(P - 1), None, ALU.add))
                chain(dve.tensor_copy(padded_i[:, :], padded[:, :]))
                chain(dve.tensor_scalar(padded_i[:, :], padded_i[:, :], -P, None, ALU.bitwise_and))
                chain(dve.tensor_copy(padded[:, :], padded_i[:, :]))
                chain(dve.tensor_tensor_scan(begin[:, :], ones8[:, :], padded[:, :], 0.0, ALU.mult, ALU.add))
                chain(dve.tensor_tensor(begin[:, :], begin[:, :], padded[:, :], ALU.subtract))
                chain(dve.tensor_tensor_scan(adjust[:, :], ones8[:, :], count[:, :], 0.0, ALU.mult, ALU.add))
                chain(dve.tensor_tensor(adjust[:, :], adjust[:, :], count[:, :], ALU.subtract))
                chain(dve.tensor_tensor(adjust[:, :], begin[:, :], adjust[:, :], ALU.subtract))
                chain(dve.tensor_tensor_scan(csum[:, :], onesf[:, :], tot[:, :], 0.0, ALU.mult, ALU.add))
                chain(dve.tensor_tensor(csum[:, :], csum[:, :], tot[:, :], ALU.subtract))
                chain(dve.tensor_tensor(csum[:, :], csum[:, :], pre[:, :], ALU.add))
                c3 = csum[:, :].rearrange("p (e t) -> p e t", e=E)
                chain(dve.tensor_tensor(c3, c3, spread(adjust[:, :], TILES), ALU.add))
                for k, one in ((0, one1), (1, one2)):
                    chain(dve.tensor_tensor(A[:, :, :], one[:, :, :], c3.rearrange("p e t -> p t e"), ALU.mult))
                    chain(dve.tensor_reduce(slot_f[:, k, :], A[:, :, :], AX_X, ALU.add))
                dve.tensor_copy(T.slot[:, :, :], slot_f[:, :, :]).then_inc(slots_ready, 1)
                chain(dve.tensor_tensor(reach[:, :, :], spread(first[:, :], E),
                                        begin[:, :].unsqueeze(1).to_broadcast([P, SLOT_TILES, E]), ALU.is_ge))
                chain(dve.tensor_reduce(owner[:, :], reach[:, :, :], AX_X, ALU.add))
                chain(dve.tensor_scalar(owner[:, :], owner[:, :], -1.0, None, ALU.add))
                dve.tensor_copy(T.owner[:, :], owner[:, :])


def experts0(nc, I, T):
    with ExitStack() as ctx:
        a = Alloc(nc, ctx, "experts0")
        xs = [a.sb(f"xs{v}", [P, 2, D], BF16) for v in range(2)]
        xt = [a.sb(f"xt{v}", [P, 2, P], BF16) for v in range(2)]
        gated = [a.sb(f"gated{v}", [R0, C0 * P]) for v in range(2)]
        z = [a.sb(f"z{v}", [R0, C0 * P]) for v in range(2)]
        hidden = [a.sb(f"hidden{v}", [R0, C0 * P]) for v in range(2)]
        hh = [a.sb(f"hh{v}", [R0, 2, C0 * P], BF16) for v in range(2)]
        ys = [a.sb(f"ys{v}", [P, D]) for v in range(2)]
        xt_ps = [a.ps(f"xt_ps{v}", [P, 2, P], BF16) for v in range(2)]
        g_ps = [a.ps(f"g_ps{v}", [P, C0 * P]) for v in range(2)]
        u_ps = [a.ps(f"u_ps{v}", [P, C0 * P]) for v in range(2)]
        y_ps = [a.ps(f"y_ps{v}", [P, D]) for v in range(2)]
        xs_in = [a.sem(f"xs_in{v}") for v in range(2)]
        ys_out = [a.sem(f"ys_out{v}") for v in range(2)]
        xt_done, xt_copied, g_done, u_done, gate_ready, z_ready, silu_ready, high, low, y_done, y_ready = (
            a.sem(n) for n in ("xt_done", "xt_copied", "g_done", "u_done", "gate_ready", "z_ready", "silu_ready",
                               "high", "low", "y_done", "y_ready"))

        def live(p):
            return not isinstance(p, int) or 0 <= p < SLOT_TILES

        def steps(step):
            def run(eng):
                for p in range(4):
                    step(p, p % 2)
                with eng.Fori(2, SLOT_TILES // 2) as it:
                    for u in range(2):
                        step(it * 2 + u, u)
                for u in range(2):
                    step(SLOT_TILES + u, u)
            return run

        def expert(eng, p):
            return eng.value_load(T.owner[0:1, ds(p, 1)], min_val=0, max_val=E - 1)

        def one(ap):
            return ap.rearrange("p a n -> p (a n)")

        with nc.Block() as block:
            @block.sync
            def _(sp):
                def step(p, u):
                    if live(p):
                        at_least(sp, xt_done, p - 1)
                        sp.dma_start(xs[u][:, :, :], T.xs_dram[ds(p * P, P), :].rearrange("p (a d) -> p a d", a=2))\
                            .then_inc(xs_in[u], 16)
                    if live(p - 2):
                        sp.wait_ge(y_ready, p - 1)
                        sp.dma_start(T.ys_dram[ds((p - 2) * P, P), :], ys[u][:, :]).then_inc(ys_out[u], 16)
                steps(step)(sp)
                for v in range(2):
                    sp.wait_ge(ys_out[v], 8 * SLOT_TILES)

            @block.tensor
            def _(pe):
                TERMS = ((0, 0), (0, 1), (1, 0))

                def step(p, u):
                    if live(p):
                        pe.wait_ge(xs_in[u], (p - u) * 8 + 16)
                        at_least(pe, xt_copied, p - 1)
                        for half in range(2):
                            last = pe.transpose(xt_ps[u][:, half, :], xs[u][:, half, :], T.identB[:, :])
                        last.then_inc(xt_done, 1)
                    if live(p - 1):
                        v = 1 - u
                        e = expert(pe, p - 1)
                        pe.wait_ge(xt_copied, p)
                        at_least(pe, gate_ready, p - 2)
                        at_least(pe, z_ready, p - 2)
                        for ps, W, done in ((g_ps, T.WG, g_done), (u_ps, T.WU, u_done)):
                            for c in range(C0):
                                for n, (wh, xh) in enumerate(TERMS):
                                    last = pe.matmul(ps[v][0:R0, c * P:(c + 1) * P],
                                                     one(W[:, wh, ds(e, 1), c * R0:(c + 1) * R0]), xt[v][:, xh, :],
                                                     start=(n == 0), stop=(n == 2))
                            last.then_inc(done, 1)
                    if live(p - 2):
                        e = expert(pe, p - 2)
                        pe.wait_ge(high, p - 1)
                        pe.wait_ge(low, p - 1)
                        at_least(pe, y_ready, p - 3)
                        for c in range(C0):
                            for n, (wh, xh) in enumerate(TERMS):
                                last = pe.matmul(y_ps[u][:, :], hh[u][:, xh, c * P:(c + 1) * P],
                                                 one(T.WD[:, wh, ds(e, 1), c * P:(c + 1) * P]),
                                                 start=(c == 0 and n == 0), stop=(c == C0 - 1 and n == 2))
                        last.then_inc(y_done, 1)
                steps(step)(pe)

            @block.scalar
            def _(act):
                def step(p, u):
                    if live(p - 1):
                        v = 1 - u
                        e = expert(act, p - 1)
                        act.wait_ge(g_done, p)
                        at_least(act, z_ready, p - 2)
                        for c in range(C0):
                            last = act.activation(gated[v][:, c * P:(c + 1) * P], g_ps[v][0:R0, c * P:(c + 1) * P],
                                                  ACT.Identity, bias=one(T.gb[:, ds(e, 1), c:c + 1]))
                        last.then_inc(gate_ready, 1)
                        act.wait_ge(z_ready, p)
                        at_least(act, y_done, p - 2)
                        act.activation(hh[v][:, 0, :], z[v][:, :], ACT.Silu).then_inc(high, 1)
                        at_least(act, low, p - 2)
                        act.activation(hidden[v][:, :], z[v][:, :], ACT.Silu).then_inc(silu_ready, 1)
                steps(step)(act)

            @block.vector
            def _(dve):
                def step(p, u):
                    if live(p):
                        dve.wait_ge(xt_done, p + 1)
                        at_least(dve, u_done, p - 1)
                        dve.tensor_copy(xt[u][:, :, :], xt_ps[u][:, :, :]).then_inc(xt_copied, 1)
                    if live(p - 2):
                        dve.wait_ge(silu_ready, p - 1)
                        at_least(dve, y_done, p - 3)
                        dve.tensor_tensor(hh[u][:, 1, :], hidden[u][:, :], hh[u][:, 0, :], ALU.subtract).then_inc(low, 1)
                    if live(p - 1):
                        v = 1 - u
                        e = expert(dve, p - 1)
                        dve.wait_ge(u_done, p)
                        dve.wait_ge(gate_ready, p)
                        at_least(dve, silu_ready, p - 2)
                        for c in range(C0):
                            last = dve.scalar_tensor_tensor(z[v][:, c * P:(c + 1) * P], u_ps[v][0:R0, c * P:(c + 1) * P],
                                                            one(T.ub[:, ds(e, 1), c:c + 1]),
                                                            gated[v][:, c * P:(c + 1) * P], ALU.add, ALU.mult)
                        last.then_inc(z_ready, 1)
                    if live(p - 2):
                        e = expert(dve, p - 2)
                        dve.wait_ge(y_done, p - 1)
                        at_least(dve, ys_out[u], 8 * (p - u) - 16)
                        dve.tensor_tensor(ys[u][:, :], y_ps[u][:, :], flat2(T.db0[:, ds(e, 1), :]), ALU.add)\
                            .then_inc(y_ready, 1)
                steps(step)(dve)


def combine0(nc, I, T):
    with ExitStack() as ctx:
        a = Alloc(nc, ctx, "combine0")
        rows = a.sb("rows", [P, TILES, TOPK, D])
        rows_in = [a.sem(f"rows_in{t}") for t in range(GROUPS)]
        added = a.sem("added")
        with nc.Block() as block:
            @block.gpsimd
            def _(pool):
                for t in range(TILES):
                    for k in range(TOPK):
                        pool.indirect_dma_start(
                            rows[:, t, k, :], None, T.ys_dram[:, :],
                            bass.IndirectOffsetOnAxis(ap=T.slot[:, k, t:t + 1].bitcast(U32), axis=0))\
                            .then_inc(rows_in[t // G], 16)

            @block.vector
            def _(dve):
                for t in range(TILES):
                    dve.wait_ge(rows_in[t // G], 16 * TOPK * G)
                    for k in range(TOPK):
                        dve.scalar_tensor_tensor(T.X[:, t, :], rows[:, t, k, :], T.share[:, k, t:t + 1], T.X[:, t, :],
                                                 ALU.mult, ALU.add).then_inc(added, 1)
                        dve.wait_ge(added, 2 * t + k + 1)


def attend1(nc, I, T):
    with ExitStack() as ctx:
        a = Alloc(nc, ctx, "attend1")
        SCALE = D ** -0.5
        ln = Norm(a, T)
        cg, qT, kT, V = ([a.sb(f"{n}{v}", [P, GT]) for v in range(2)] for n in ("cg", "qT", "kT", "V"))
        xnT, sm, probs, pT, oT = (a.sb(n, [P, GT]) for n in ("xnT", "sm", "probs", "pT", "oT"))
        peak, nmax, total, inverse = (a.sb(n, [P, G]) for n in ("peak", "nmax", "total", "inverse"))
        xt_ps, q_ps, k_ps, v_ps, s_ps, p_ps, o_ps, y_ps = (
            a.ps(n, [P, GT]) for n in ("xt_ps", "q_ps", "k_ps", "v_ps", "s_ps", "p_ps", "o_ps", "y_ps"))
        (cg_ready, xt_done, xt_copied, q_done, q_ready, k_done, k_ready, v_done, v_ready, s_done, masked, peaked,
         nmax_ready, exped, p_done, p_copied, o_done, o_copied, y_done, inverted, x_done, biased) = (
            a.sem(n) for n in ("cg_ready", "xt_done", "xt_copied", "q_done", "q_ready", "k_done", "k_ready", "v_done",
                               "v_ready", "s_done", "masked", "peaked", "nmax_ready", "exped", "p_done", "p_copied",
                               "o_done", "o_copied", "y_done", "inverted", "x_done", "biased"))

        def tile(t):
            return slice(t * P, (t + 1) * P)

        def live(g):
            return not isinstance(g, int) or 0 <= g < GROUPS

        def steps(eng, step):
            for g in range(2):
                step(g, g)
            with eng.Fori(1, GROUPS // 2) as it:
                for v in range(2):
                    step(it * 2 + v, v)
            step(GROUPS, 0)

        with nc.Block() as block:
            @block.gpsimd
            def _(pool):
                def body(it):
                    for v in range(2):
                        g = 2 * it + v
                        at_least(pool, v_done, g - 1)
                        pool.tensor_copy(cg[v][:, :], T.ctxT[:, ds(g * GT, GT)]).then_inc(cg_ready, 1)
                        ln.root(pool, g, v)
                        pool.wait_ge(ln.xn_ready, g + 1)
                        pool.tensor_tensor(T.X[:, ds(g * G, G), :], T.X[:, ds(g * G, G), :],
                                           T.bo1[:, :].unsqueeze(1).to_broadcast([P, G, D]), ALU.add).then_inc(biased, 1)
                rounds(pool, GROUPS // 2, body)

            @block.tensor
            def _(pe):
                def step(g, v):
                    w, b = 1 - v, g - 1
                    if live(g):
                        pe.wait_ge(ln.xn_ready, g + 1)
                        at_least(pe, xt_copied, g)
                        for t in range(G):
                            last = pe.transpose(xt_ps[:, tile(t)], ln.xn[v][:, t, :], T.identF[:, :])
                        last.then_inc(xt_done, 1)
                    if live(b):
                        pe.wait_ge(q_ready, b + 1)
                        pe.wait_ge(k_ready, b + 1)
                        at_least(pe, masked, b)
                        for t in range(G):
                            last = pe.matmul(s_ps[:, tile(t)], qT[w][:, tile(t)], kT[w][:, tile(t)],
                                             start=True, stop=True)
                        last.then_inc(s_done, 1)
                    if live(g):
                        pe.wait_ge(cg_ready, g + 1)
                        at_least(pe, k_ready, g)
                        pe.matmul(k_ps[:, :], T.WT[:, 5, :], cg[v][:, :], start=True, stop=True).then_inc(k_done, 1)
                        at_least(pe, v_ready, g)
                        for t in range(G):
                            last = pe.matmul(v_ps[:, tile(t)], cg[v][:, tile(t)], T.WT[:, 6, :], start=True, stop=True)
                        last.then_inc(v_done, 1)
                    if live(b):
                        pe.wait_ge(exped, b + 1)
                        at_least(pe, p_copied, b)
                        for t in range(G):
                            last = pe.transpose(p_ps[:, tile(t)], probs[:, tile(t)], T.identF[:, :])
                        last.then_inc(p_done, 1)
                    if live(g):
                        pe.wait_ge(xt_copied, g + 1)
                        at_least(pe, q_ready, g)
                        pe.matmul(q_ps[:, :], T.WT[:, 4, :], xnT[:, :], start=True, stop=True).then_inc(q_done, 1)
                    if live(b):
                        pe.wait_ge(p_copied, b + 1)
                        at_least(pe, o_copied, b)
                        for t in range(G):
                            last = pe.matmul(o_ps[:, tile(t)], V[w][:, tile(t)], pT[:, tile(t)], start=True, stop=True)
                        last.then_inc(o_done, 1)
                        pe.wait_ge(o_copied, b + 1)
                        at_least(pe, x_done, b)
                        for t in range(G):
                            last = pe.matmul(y_ps[:, tile(t)], oT[:, tile(t)], T.WT[:, 7, :], start=True, stop=True)
                        last.then_inc(y_done, 1)
                steps(pe, step)

            @block.scalar
            def _(act):
                def step(g, v):
                    b = g - 1
                    if live(b):
                        act.wait_ge(nmax_ready, b + 1)
                        at_least(act, p_done, b)
                        at_least(act, inverted, b)
                        for t in range(G):
                            last = act.activation(probs[:, tile(t)], sm[:, tile(t)], ACT.Exp, bias=nmax[:, t:t + 1],
                                                  scale=SCALE, accum_out=total[:, t:t + 1])
                        last.then_inc(exped, 1)
                    if live(g):
                        act.wait_ge(xt_done, g + 1)
                        at_least(act, q_done, g)
                        act.copy(xnT[:, :], xt_ps[:, :]).then_inc(xt_copied, 1)
                        act.wait_ge(k_done, g + 1)
                        at_least(act, s_done, g - 1)
                        act.copy(kT[v][:, :], k_ps[:, :]).then_inc(k_ready, 1)
                    if live(b):
                        act.wait_ge(p_done, b + 1)
                        at_least(act, o_done, b)
                        act.copy(pT[:, :], p_ps[:, :]).then_inc(p_copied, 1)
                    if live(g):
                        act.wait_ge(q_done, g + 1)
                        act.activation(qT[v][:, :], q_ps[:, :], ACT.Identity, bias=T.bcol[:, 2:3]).then_inc(q_ready, 1)
                steps(act, step)

            @block.vector
            def _(dve):
                def norm(g, v):
                    ln.sums(dve, g, v)
                    at_least(dve, xt_done, g - 1)
                    ln.apply(dve, g, v)

                def step(g, v):
                    b = g - 1
                    if live(g):
                        norm(g, v)
                    if live(b):
                        dve.wait_ge(s_done, b + 1)
                        at_least(dve, exped, b)
                        s4 = sm[:, :].rearrange("p (t n) -> p t n", t=G)
                        dve.tensor_tensor(s4, s_ps[:, :].rearrange("p (t n) -> p t n", t=G),
                                          T.mask[:, :].unsqueeze(1).to_broadcast([P, G, P]), ALU.add).then_inc(masked, 1)
                        dve.wait_ge(masked, b + 1)
                        dve.tensor_reduce(peak[:, :], s4, AX_X, ALU.max).then_inc(peaked, 1)
                        dve.wait_ge(peaked, b + 1)
                        dve.tensor_scalar(nmax[:, :], peak[:, :], -SCALE, None, ALU.mult).then_inc(nmax_ready, 1)
                    if live(g):
                        dve.wait_ge(v_done, g + 1)
                        at_least(dve, o_done, g - 1)
                        dve.tensor_tensor(V[v][:, :].rearrange("p (t n) -> p t n", t=G),
                                          v_ps[:, :].rearrange("p (t n) -> p t n", t=G),
                                          T.bv1[:, :].unsqueeze(1).to_broadcast([P, G, P]), ALU.add).then_inc(v_ready, 1)
                    if live(b):
                        dve.wait_ge(exped, b + 1)
                        dve.reciprocal(inverse[:, :], total[:, :]).then_inc(inverted, 1)
                        dve.wait_ge(o_done, b + 1)
                        at_least(dve, y_done, b)
                        dve.tensor_copy(oT[:, :], o_ps[:, :]).then_inc(o_copied, 1)
                        dve.wait_ge(y_done, b + 1)
                        dve.wait_ge(biased, b + 1)
                        dve.wait_ge(inverted, b + 1)
                        for t in range(G):
                            x = flat2(T.X[:, ds(b * G + t, 1), :])
                            last = dve.scalar_tensor_tensor(x, y_ps[:, tile(t)], inverse[:, t:t + 1], x, ALU.mult, ALU.add)
                        last.then_inc(x_done, 1)
                steps(dve, step)


def route1(nc, I, T):
    with ExitStack() as ctx:
        a = Alloc(nc, ctx, "route1")
        sc = Scores(a, T, 1)
        PR = a.sb("PR", [P, TILES, E])
        peak, total = (a.sb(n, [P, TILES]) for n in ("peak", "total"))
        byexp = a.sb("byexp", [P, 4, SEQ])
        rest = a.sb("rest", [P, 4, SEQ])
        best = a.sb("best", [P, 4, CAP])
        where = a.sb("where", [P, 4, CAP], U32)
        where_f = a.sb("where_f", [P, 4, CAP])
        rows_i = a.sb("rows_i", [64, 1], I32)
        b2_i = a.sb("b2_i", [64, 1], I32)
        b2 = a.sb("b2", [64, 1])
        tile_i = a.sb("tile_i", [64, 16, E], I32)
        in4 = a.sb("in4", [64, 16, E])
        in_pair = a.sb("in_pair", [64, P], BF16)
        in_eight = a.sb("in_eight", [64, P])
        gain = a.sb("gain", [64, P])
        w1 = [a.sb(f"w1{v}", [P, F1]) for v in range(2)]
        w2 = [a.sb(f"w2{v}", [P, C1, P]) for v in range(2)]
        e_ps = a.ps("e_ps", [P, 2, P])
        i_ps = a.ps("i_ps", [64, P])
        v_ps = a.ps("v_ps", [64, P])
        w_in = [a.sem(f"w_in{v}") for v in range(2)]
        (shifted_ready, exp_ready, probs_ready, turned, step, found, back, cols_ready, sent, loaded, iotas, whigh, wlow,
         fenced) = (
            a.sem(n) for n in ("shifted_ready", "exp_ready", "probs_ready", "turned", "step", "found", "back",
                               "cols_ready", "sent", "loaded", "iotas", "whigh", "wlow", "fenced"))
        w1_d = I["L1_ffn_w1"]
        w2_d = I["L1_ffn_w2"].rearrange("e (c p) d -> e p c d", p=P)
        with nc.Block() as block:
            @block.sync
            def _(sp):
                for e in range(E):
                    at_least(sp, wlow, 2 * (e - 1))
                    at_least(sp, w_in[e % 2], 32 * (e // 2))
                    sp.dma_start(w1[e % 2][:, :], w1_d[e, :, :]).then_inc(w_in[e % 2], 16)
                    sp.dma_start(w2[e % 2][:, :, :], w2_d[e, :, :, :]).then_inc(w_in[e % 2], 16)
                sp.wait_ge(cols_ready, 1)
                for d, src in ((T.pair_dram, in_pair), (T.eight_dram, in_eight), (T.gain_dram, gain)):
                    to = d.rearrange("(q p b k e) -> q b k p e", q=2, p=16, b=2, k=CAP)
                    for q in range(2):
                        for b in range(2):
                            r = (q * 2 + b) * CAP
                            sp.dma_start(to[q, b, :, :, :], src[r:r + CAP, :].rearrange("k (p e) -> k p e", e=E))\
                                .then_inc(sent, 16)
                sp.wait_ge(sent, 12 * 16)
                sp.dma_start(T.pair_row[:, :], T.pair_dram.partition_broadcast(P)).then_inc(loaded, 16)
                for d, dst in ((T.eight_dram, T.eight_col), (T.gain_dram, T.gain_col)):
                    sp.dma_start(dst[:, :, :], d.rearrange("(g q e) -> q g e", q=P, e=E)).then_inc(loaded, 16)
                sp.wait_ge(loaded, 48)

            @block.gpsimd
            def _(pool):
                pool.iota(rows_i[:, :], pattern=[[0, 1]], base=0, channel_multiplier=1).then_inc(iotas, 1)
                pool.iota(tile_i[:, :, :], pattern=[[0, 4], [P, 4], [0, E]], base=0, channel_multiplier=0)\
                    .then_inc(iotas, 1)
                sc.pool(pool)
                for e in range(E):
                    pool.wait_ge(whigh, 2 * e + 2)
                    pool.tensor_tensor(T.W1[:, 1, e, :], w1[e % 2][:, :], T.W1[:, 0, e, :], ALU.subtract).then_inc(wlow, 1)
                    pool.tensor_tensor(T.W2[:, 1, e, :], flat2(w2[e % 2][:, :, :]), T.W2[:, 0, e, :], ALU.subtract)\
                        .then_inc(wlow, 1)

            @block.tensor
            def _(pe):
                sc.tensor(pe)
                pe.wait_ge(probs_ready, 1)
                for q in range(2):
                    last = pe.transpose(e_ps[:, q, :], PR[:, q * 16:(q + 1) * 16, :].rearrange("p t e -> p (t e)"),
                                        T.identF[:, :])
                last.then_inc(turned, 1)
                pe.wait_ge(found, 1)
                pe.transpose(i_ps[:, :], where_f[:, :, :].rearrange("p s k -> p (s k)"), T.identF[:, :])
                pe.transpose(v_ps[:, :], best[:, :, :].rearrange("p s k -> p (s k)"), T.identF[:, :]).then_inc(back, 1)

            @block.scalar
            def _(act):
                sc.scalar(act)
                act.wait_ge(shifted_ready, 1)
                act.activation(PR[:, :, :], sc.SC[:, :, :], ACT.Exp).then_inc(exp_ready, 1)
                for e in range(E):
                    act.wait_ge(w_in[e % 2], 32 * (e // 2 + 1))
                    act.copy(T.W1[:, 0, e, :], w1[e % 2][:, :]).then_inc(whigh, 1)
                    act.copy(T.W2[:, 0, e, :], flat2(w2[e % 2][:, :, :])).then_inc(whigh, 1)

            @block.vector
            def _(dve):
                chain = Chain(dve, step)
                sc.vector(dve)
                softmax_first(dve, chain, sc, sc.SC[:, :, :], peak[:, :], shifted_ready)
                softmax_last(dve, chain, PR[:, :, :], total[:, :], exp_ready)
                dve.sem_inc(probs_ready, 1)
                dve.wait_ge(turned, 1)
                chain(dve.tensor_copy(byexp[:, :, :].rearrange("p s t -> p (s t)"), e_ps[:, :, :].rearrange("p q t -> p (q t)")))
                for s in range(4):
                    chain(dve.max(best[:, s, 0:8], byexp[:, s, :]))
                    chain(dve.max_index(where[:, s, 0:8], best[:, s, 0:8], byexp[:, s, :]))
                    chain(dve.match_replace(rest[:, s, :], best[:, s, 0:8], byexp[:, s, :], -1.0))
                    chain(dve.max(best[:, s, 8:16], rest[:, s, :]))
                    chain(dve.max_index(where[:, s, 8:16], best[:, s, 8:16], rest[:, s, :]))
                chain(dve.tensor_copy(where_f[:, :, :], where[:, :, :]))
                dve.sem_inc(found, 1)
                dve.wait_ge(iotas, 2)
                chain(dve.tensor_scalar(b2_i[:, :], rows_i[:, :], CAP, None, ALU.bitwise_and))
                chain(dve.tensor_copy(b2[:, :], b2_i[:, :]))
                chain(dve.tensor_scalar(b2[:, :], b2[:, :], float(SEQ // CAP), None, ALU.mult))
                chain(dve.tensor_copy(in4[:, :, :], tile_i[:, :, :]))
                dve.wait_ge(back, 1)
                chain(dve.tensor_scalar(in_pair[:, :], i_ps[:, :], b2[:, 0:1], None, ALU.add))
                chain(dve.scalar_tensor_tensor(in_eight[:, :], i_ps[:, :], b2[:, 0:1],
                                               in4[:, :, :].rearrange("p t e -> p (t e)"), ALU.add, ALU.add))
                chain(dve.tensor_copy(gain[:, :], v_ps[:, :]))
                dve.sem_inc(cols_ready, 1)


def experts1(nc, I, T):
    with ExitStack() as ctx:
        a = Alloc(nc, ctx, "experts1")
        XG = [a.sb(f"XG{h}", [P, E, BATCH, CAP], BF16) for h in range(2)]
        Y = a.sb("Y", [P, 2, GROUPS, E, D], BF16)
        pick = [a.sb(f"pick{v}", [P, 2 * P], BF16) for v in range(2)]
        place = [a.sb(f"place{v}", [P, GT], BF16) for v in range(2)]
        hidden = [a.sb(f"hidden{v}", [P, GT]) for v in range(2)]
        hh = [a.sb(f"hh{v}", [P, 2, C1, GT], BF16) for v in range(2)]
        bank = [a.ps(f"bank{i}", [P, 512]) for i in range(8)]
        out_d = T.out.rearrange("b s d -> (b s) d").rearrange("(n p) d -> p n d", p=P)
        (picked, g_done, g_high, g_low) = (a.sem(n) for n in ("picked", "g_done", "g_high", "g_low"))
        (h_done, gelu_ready, high, low, y_done, y_high, y_low) = (
            a.sem(n) for n in ("h_done", "gelu_ready", "high", "low", "y_done", "y_high", "y_low"))
        placed, sum_done, x_done, stored = (a.sem(n) for n in ("placed", "sum_done", "x_done", "stored"))
        TERMS = ((0, 0), (0, 1), (1, 0))
        STEPS = 2 * E

        def flat3(ap):
            return ap.rearrange("p a b c -> p (a b c)")

        def live(s):
            return not isinstance(s, int) or 0 <= s < STEPS

        def steps(eng, step):
            for s in range(2):
                step(s, 0, s)
            with eng.Fori(1, E) as e:
                for j in range(2):
                    step(2 * e + j, e, j)
            step(STEPS, E, 0)

        with nc.Block() as block:
            @block.sync
            def _(sp):
                def body(g):
                    sp.wait_ge(x_done, g + 1)
                    sp.dma_start(out_d[:, ds(g * G, G), :], T.X[:, ds(g * G, G), :]).then_inc(stored, 16)
                rounds(sp, GROUPS, body)
                sp.wait_ge(stored, 16 * GROUPS)

            @block.tensor
            def _(pe):
                def gather(it):
                    for v in range(2):
                        p = 2 * it + v
                        pe.wait_ge(picked, p + 1)
                        at_least(pe, g_high, p - 1)
                        at_least(pe, g_low, p - 1)
                        for h in range(2):
                            last = pe.matmul(bank[2 * v + h][:, 0:2 * P], T.XHL[:, ds(p, 1), h, :].rearrange("p a d -> p (a d)"),
                                             pick[v][:, :], start=True, stop=True)
                        last.then_inc(g_done, 1)
                rounds(pe, TILES // 2, gather)

                def step(s, e, j):
                    if live(s):
                        if isinstance(s, int) and s == 0:
                            pe.wait_ge(g_high, TILES)
                            pe.wait_ge(g_low, TILES)
                        for c in range(C1):
                            at_least(pe, gelu_ready, 4 * (s - 1) + c + 1)
                            for n, (wh, xh) in enumerate(TERMS):
                                last = pe.matmul(bank[c][:, :],
                                                 flat2(T.W1[:, wh, ds(e, 1), c * P:(c + 1) * P]),
                                                 flat3(XG[xh][:, ds(e, 1), 32 * j:32 * j + 32, :]),
                                                 start=(n == 0), stop=(n == 2))
                            last.then_inc(h_done, 1)
                    if live(s - 1):
                        r, w = s - 1, 1 - j
                        ee = e if j else e - 1
                        pe.wait_ge(high, 4 * r + 4)
                        pe.wait_ge(low, 4 * r + 4)
                        at_least(pe, y_low, r - 1)
                        for m in range(4):
                            for c in range(C1):
                                for n, (wh, xh) in enumerate(TERMS):
                                    last = pe.matmul(bank[4 + w][:, m * P:(m + 1) * P], hh[w][:, xh, c, m * P:(m + 1) * P],
                                                     flat2(T.W2[:, wh, ds(ee, 1), c * P:(c + 1) * P]),
                                                     start=(c == 0 and n == 0), stop=(c == C1 - 1 and n == 2))
                        last.then_inc(y_done, 1)
                steps(pe, step)

                def scatter(g):
                    b = bank[6]
                    at_least(pe, x_done, g)
                    for e in range(E):
                        pe.wait_ge(placed, g * E + e + 1)
                        for t in range(G):
                            for h in range(2):
                                last = pe.matmul(b[:, t * P:(t + 1) * P], place[e % 2][:, t * P:(t + 1) * P],
                                                 flat2(Y[:, h, ds(g, 1), e, :]),
                                                 start=(e == 0 and t == 0 and h == 0), stop=(e == E - 1 and h == 1),
                                                 skip_group_check=True)
                        last.then_inc(sum_done, 1)
                pe.wait_ge(y_low, STEPS)
                rounds(pe, GROUPS, scatter)

            @block.scalar
            def _(act):
                def gather(it):
                    for v in range(2):
                        p = 2 * it + v
                        act.wait_ge(g_done, p + 1)
                        act.copy(XG[0][:, :, ds(2 * p, 2), :].rearrange("p e b k -> p b k e"),
                                 bank[2 * v][:, 0:2 * P].rearrange("p (b k e) -> p b k e", b=2, e=E)).then_inc(g_high, 1)
                rounds(act, TILES // 2, gather)

                def step(s, e, j):
                    if live(s):
                        for c in range(C1):
                            act.wait_ge(h_done, 4 * s + c + 1)
                            at_least(act, low, 4 * s + c - 1)
                            act.activation(hidden[c % 2][:, :], bank[c][:, :], ACT.Gelu).then_inc(gelu_ready, 1)
                            at_least(act, y_done, s - 1)
                            act.wait_ge(gelu_ready, 4 * s + c + 1)
                            act.copy(hh[j][:, 0, c, :], hidden[c % 2][:, :]).then_inc(high, 1)
                    if live(s - 1):
                        r, w = s - 1, 1 - j
                        ee = e if j else e - 1
                        act.wait_ge(y_done, r + 1)
                        for m in range(4):
                            last = act.activation(flat2(Y[:, 0, 4 * w + m, ds(ee, 1), :]),
                                                  bank[4 + w][:, m * P:(m + 1) * P], ACT.Identity,
                                                  scale=T.gain_col[:, 4 * w + m, ds(ee, 1)])
                        last.then_inc(y_high, 1)
                steps(act, step)

            @block.vector
            def _(dve):
                def gather(it):
                    for v in range(2):
                        p = 2 * it + v
                        at_least(dve, g_done, p - 1)
                        dve.tensor_scalar(pick[v][:, :], T.pair_row[:, ds(p * 2 * P, 2 * P)], T.iotaP[:, 0:1], None,
                                          ALU.is_equal).then_inc(picked, 1)
                        dve.wait_ge(g_done, p + 1)
                        dve.tensor_copy(XG[1][:, :, ds(2 * p, 2), :].rearrange("p e b k -> p b k e"),
                                        bank[2 * v + 1][:, 0:2 * P].rearrange("p (b k e) -> p b k e", b=2, e=E))\
                            .then_inc(g_low, 1)
                rounds(dve, TILES // 2, gather)

                def step(s, e, j):
                    if live(s):
                        for c in range(C1):
                            dve.wait_ge(high, 4 * s + c + 1)
                            dve.tensor_tensor(hh[j][:, 1, c, :], hidden[c % 2][:, :], hh[j][:, 0, c, :], ALU.subtract)\
                                .then_inc(low, 1)
                    if live(s - 1):
                        r, w = s - 1, 1 - j
                        ee = e if j else e - 1
                        dve.wait_ge(y_high, r + 1)
                        for m in range(4):
                            last = dve.scalar_tensor_tensor(flat2(Y[:, 1, 4 * w + m, ds(ee, 1), :]),
                                                            bank[4 + w][:, m * P:(m + 1) * P],
                                                            T.gain_col[:, 4 * w + m, ds(ee, 1)],
                                                            flat2(Y[:, 0, 4 * w + m, ds(ee, 1), :]),
                                                            ALU.mult, ALU.subtract)
                        last.then_inc(y_low, 1)
                steps(dve, step)

                def scatter(g):
                    for e in range(E):
                        at_least(dve, sum_done, g * E + e - 1)
                        dve.tensor_scalar(place[e % 2][:, :], T.iotaB[:, :], flat2(T.eight_col[:, ds(g, 1), e:e + 1]), None,
                                          ALU.is_equal).then_inc(placed, 1)
                    dve.wait_ge(sum_done, g * E + E)
                    x = T.X[:, ds(g * G, G), :]
                    dve.tensor_tensor(x, bank[6][:, :].rearrange("p (t d) -> p t d", t=G), x, ALU.add).then_inc(x_done, 1)
                rounds(dve, GROUPS, scatter)


def build(nc, I, out, stages):
    HELD.clear()
    with ExitStack() as ctx:
        a = Alloc(nc, ctx, "build")
        T = Tensors()
        T.X = a.sb("X", [P, TILES, D])
        T.ctxT = a.sb("ctxT", [P, NT])
        T.WT = a.sb("WT", [P, 8, P])
        T.gateT = a.sb("gateT", [P, 2, E])
        T.owns = a.sb("owns", [P, 2])
        T.row_i = a.sb("row_i", [P, 2], I32)
        T.bv0, T.bo0, T.bv1, T.bo1 = (a.sb(n, [P, D]) for n in ("bv0", "bo0", "bv1", "bo1"))
        T.gb0 = a.sb("gb0", [P, E])
        T.bcol = a.sb("bcol", [P, 3])
        T.identF = a.sb("identF", [P, P])
        T.identB = a.sb("identB", [P, P], BF16)
        T.before = a.sb("before", [P, P], BF16)
        T.ones = a.sb("ones", [P, P], BF16)
        T.half = a.sb("half", [P, 8])
        T.eps = a.sb("eps", [P, 8])
        T.mask = a.sb("mask", [P, P])
        T.iota_i = a.sb("iota_i", [P, 512], I32)
        T.iota_p = a.sb("iota_p", [P, 1], I32)
        T.iotaB = a.sb("iotaB", [P, 512])
        T.iotaP = a.sb("iotaP", [P, 1])
        T.q_dram = nc.dram_tensor("q_dram", [4, P, NT], BF16, kind="Internal").ap()
        T.k_dram = nc.dram_tensor("k_dram", [2, P, 2 * NT], BF16, kind="Internal").ap()
        T.xs_dram = nc.dram_tensor("xs_dram", [SLOT_TILES * P, 2 * D], BF16, kind="Internal").ap()
        T.ys_dram = nc.dram_tensor("ys_dram", [SLOT_TILES * P, D], F32, kind="Internal").ap()
        with ExitStack() as first:
            b = Alloc(nc, first, "layer0")
            T.WU = b.sb("WU", [P, 2, E, F0], BF16)
            T.WG = b.sb("WG", [P, 2, E, F0], BF16)
            T.WD = b.sb("WD", [R0, 2, E, C0 * P], BF16)
            T.Wrel = b.sb("Wrel", [QROWS, SEQ // 2, P], BF16)
            T.sel = b.sb("sel", [48, HP, 2, SEQ], BF16)
            T.XHL = b.sb("XHL", [P, TILES, 2, D], BF16)
            T.slot = b.sb("slot", [P, TOPK, TILES], I32)
            T.share = b.sb("share", [P, TOPK, TILES])
            T.owner = b.sb("owner", [P, SLOT_TILES], I32)
            T.db0 = b.sb("db0", [P, E, D])
            T.ub = b.sb("ub", [R0, E, C0])
            T.gb = b.sb("gb", [R0, E, C0])
            for stage in stages[0]:
                stage(nc, I, T)
        clear_semaphores(nc)
        T.W1 = a.sb("W1", [P, 2, E, F1], BF16)
        T.W2 = a.sb("W2", [P, 2, E, C1 * P], BF16)
        T.XHL = a.sb("XHL1", [P, TILES, 2, D], BF16)
        T.pair_row = a.sb("pair_row", [P, BATCH * CAP * E], BF16)
        T.eight_col = a.sb("eight_col", [P, GROUPS, E])
        T.gain_col = a.sb("gain_col", [P, GROUPS, E])
        T.pair_dram = nc.dram_tensor("pair_dram", [BATCH * CAP * E], BF16, kind="Internal").ap()
        T.eight_dram = nc.dram_tensor("eight_dram", [BATCH * CAP * E], F32, kind="Internal").ap()
        T.gain_dram = nc.dram_tensor("gain_dram", [BATCH * CAP * E], F32, kind="Internal").ap()
        T.out = out
        for stage in stages[1]:
            stage(nc, I, T)


STAGES = ((prepare, project0, attend0, route0, experts0, combine0),
          (attend1, route1, experts1))

_INS = ["x", "ctx_1024", "L0_xattn_Wq", "L0_xattn_bq", "L0_xattn_Wk", "L0_xattn_bk", "L0_xattn_Wv", "L0_xattn_bv",
        "L0_xattn_Wo", "L0_xattn_bo", "L0_xattn_w_rel", "L0_ffn_gate_w", "L0_ffn_gate_b", "L0_ffn_up_w",
        "L0_ffn_up_b", "L0_ffn_gp_w", "L0_ffn_gp_b", "L0_ffn_down_w", "L0_ffn_down_b", "L1_xattn_Wk",
        "L1_xattn_Wv", "L1_xattn_bv", "L1_xattn_Wq", "L1_xattn_bq", "L1_xattn_Wo", "L1_xattn_bo",
        "L1_ffn_gate_w", "L1_ffn_w1", "L1_ffn_w2"]


def kernel(**inputs):
    import numpy as _np
    import concourse.bacc as _bacc
    from concourse import mybir as _mybir
    from concourse.bass_utils import run_bass_kernel_spmd as _run

    nc = _bacc.Bacc("TRN2", target_bir_lowering=False, num_devices=1)
    arrays, args = {}, {}
    for name in _INS:
        a = _np.ascontiguousarray(inputs[name])
        arrays[f"in_{name}_dram"] = a
        args[name] = nc.dram_tensor(f"in_{name}_dram", a.shape, _mybir.dt.from_np(a.dtype), kind="ExternalInput").ap()
    out = nc.dram_tensor("out_0_dram", (BATCH, SEQ, D), _mybir.dt.float32, kind="ExternalOutput").ap()
    build(nc, args, out, STAGES)
    r = _run(nc, [arrays], core_ids=[0])
    return r.results[0]["out_0_dram"]
```

```python
from contextlib import ExitStack

import concourse.bass as bass
from concourse import mybir

F32 = mybir.dt.float32
BF16 = mybir.dt.bfloat16
I32 = mybir.dt.int32
U32 = mybir.dt.uint32
ALU = mybir.AluOpType
ACT = mybir.ActivationFunctionType
AX_X = mybir.AxisListType.X
ds = bass.ds

P = 128
BATCH, SEQ, D = 64, 64, 128
NT = BATCH * SEQ
TILES = NT // P
H, DK = 16, 8
HP = H // 2
E = 8
F0, C0 = 408, 4
R0 = F0 // C0
F1, C1 = 512, 4
R1 = F1 // C1
TOPK = 2
ST = 2 * P
SLOT_TILES = -(-(NT * TOPK + E * (ST - 1)) // ST)
CAP = 2 * SEQ // E
G = 4
GT = G * P
GROUPS = NT // GT
LN_EPS = 1e-5
NEG = -1e38
TERM_HIGH = (0, 1, 0)
TERM_W = (0, 0, 1)
QROWS = 2 * 3 * 16


class Tensors:
    pass


def at_least(eng, sem, value):
    if not (isinstance(value, int) and value <= 0):
        eng.wait_ge(sem, value)


def rounds(eng, count, body):
    body(0)
    with eng.Fori(1, count) as it:
        body(it)


def flat2(ap):
    return ap.rearrange("p a d -> p (a d)")


class Alloc:

    def __init__(self, nc, ctx, stage):
        self.nc, self.ctx, self.stage = nc, ctx, stage

    def sb(self, name, shape, dt=F32):
        return self.ctx.enter_context(self.nc.sbuf_tensor(f"{self.stage}_{name}", shape, dt))

    def ps(self, name, shape, dt=F32):
        return self.ctx.enter_context(self.nc.psum_tensor(f"{self.stage}_{name}", shape, dt))

    def sem(self, name):
        sem = self.nc.alloc_semaphore(f"{self.stage}_{name}")
        HELD.append(sem)
        return sem


HELD = []


def clear_semaphores(nc):
    nc.clear_and_free_semaphores(list(HELD))
    HELD.clear()
    nc.all_engine_barrier()


def windows(row):
    return bass.AP(tensor=row.tensor, offset=row.offset, ap=[row.ap[0], (2, SEQ // 2), (1, SEQ)])


def prepare(nc, I, T):
    with ExitStack() as ctx:
        a = Alloc(nc, ctx, "prepare")
        small = a.sb("small", [P, 8, P])
        gates = a.sb("gates", [E, 2, P])
        wrel = a.sb("wrel", [P, DK])
        wrel_t = a.sb("wrel_t", [DK, 2, P], BF16)
        up = a.sb("up", [R0, E * C0, P])
        gp = a.sb("gp", [R0, E * C0, P])
        down = a.sb("down", [P, E, F0])
        bv_t = a.sb("bv_t", [P, P])
        ring = [a.ps(f"ring{i}", [P, 512]) for i in range(4)]
        fold = a.ps("fold", [P, 512])
        small_in, rel_in, up_in, gp_in, down_in, row_in = (
            a.sem(n) for n in ("small_in", "rel_in", "up_in", "gp_in", "down_in", "row_in"))
        ident_set, ident_ready, zero_set, rel_zero, rel_out = (
            a.sem(n) for n in ("ident_set", "ident_ready", "zero_set", "rel_zero", "rel_out"))
        turned, high_done, low_done, owned, fold_turned, fold_copied, folded = (
            a.sem(n) for n in ("turned", "high_done", "low_done", "owned", "fold_turned", "fold_copied", "folded"))

        jobs = []
        for h in range(2):
            jobs.append((small_in, 160, [small[:, 4 * h + j, :] for j in range(4)], "small", h))
        jobs.append((small_in, 160, [gates[:, j, :] for j in range(2)], "gates", 0))
        jobs.append((rel_in, 16, [wrel[:, :]], "wrel", 0))
        for e in range(E):
            jobs.append((up_in, 16, [up[:, e * C0 + c, :] for c in range(C0)], "up", e))
            jobs.append((gp_in, 16, [gp[:, e * C0 + c, :] for c in range(C0)], "gp", e))
            jobs.append((down_in, 16, [down[:, e, c * R0:(c + 1) * R0] for c in range(C0)], "down", e))

        lows = [sum(k not in ("small", "gates") for _, _, _, k, _ in jobs[:n + 1]) for n in range(len(jobs))]

        def result(kind, bank, e, half):
            if kind == "small":
                return T.WT[:, 4 * e:4 * e + 4, :], bank[:, :].rearrange("p (j d) -> p j d", j=4)
            if kind == "gates":
                return T.gateT[:, :, :], bank[:, 0:2 * E].rearrange("p (j e) -> p j e", j=2)
            if kind == "wrel":
                return wrel_t[:, half, :], bank[0:DK, 0:P]
            if kind == "down":
                return T.WD[:, half, e, :], bank[0:R0, :]
            return (T.WU if kind == "up" else T.WG)[:, half, e, :], bank[:, 0:F0]

        with nc.Block() as block:
            @block.sync
            def _(sp):
                for j, n in enumerate(("L0_xattn_Wq", "L0_xattn_Wk", "L0_xattn_Wv", "L0_xattn_Wo",
                                       "L1_xattn_Wq", "L1_xattn_Wk", "L1_xattn_Wv", "L1_xattn_Wo")):
                    sp.dma_start(small[:, j, :], I[n]).then_inc(small_in, 16)
                sp.dma_start(gates[:, 0, :], I["L0_ffn_gate_w"]).then_inc(small_in, 16)
                sp.dma_start(gates[:, 1, :], I["L1_ffn_gate_w"]).then_inc(small_in, 16)
                sp.dma_start(wrel[:, :], I["L0_xattn_w_rel"][0:P, :]).then_inc(rel_in, 16)
                sp.dma_start(up[:, :, :], I["L0_ffn_up_w"].rearrange("e (c r) d -> r (e c) d", r=R0)).then_inc(up_in, 16)
                sp.dma_start(gp[:, :, :], I["L0_ffn_gp_w"].rearrange("e (c r) d -> r (e c) d", r=R0)).then_inc(gp_in, 16)
                sp.dma_start(down[:, :, :], I["L0_ffn_down_w"].rearrange("e d f -> d e f")).then_inc(down_in, 16)
                sp.wait_ge(low_done, 1)
                sp.wait_ge(rel_zero, 1)
                for par in range(2):
                    for s in range(3):
                        for h2 in range(2):
                            row = par * 48 + s * 16 + h2 * DK
                            sp.dma_start(T.Wrel[row:row + DK, :, h2 * SEQ:(h2 + 1) * SEQ],
                                         windows(wrel_t[:, TERM_W[s], par:P])).then_inc(rel_out, 16)
                sp.wait_ge(rel_out, 12 * 16)

            @block.gpsimd
            def _(pool):
                def row(out, name, n):
                    pool.dma_start(out, I[name].partition_broadcast(P)).then_inc(row_in, 16)
                row(T.bv0[:, :], "L0_xattn_bv", D)
                row(T.bo0[:, :], "L0_xattn_bo", D)
                row(T.bv1[:, :], "L1_xattn_bv", D)
                row(T.bo1[:, :], "L1_xattn_bo", D)
                row(T.gb0[:, :], "L0_ffn_gate_b", E)
                pool.dma_start(T.db0[:, :, :], I["L0_ffn_down_b"].partition_broadcast(P)).then_inc(row_in, 16)
                for j, n in enumerate(("L0_xattn_bq", "L0_xattn_bk", "L1_xattn_bq")):
                    pool.dma_start(T.bcol[:, j:j + 1], I[n].rearrange("(p a) -> p a", a=1)).then_inc(row_in, 16)
                for out, n in ((T.ub, "L0_ffn_up_b"), (T.gb, "L0_ffn_gp_b")):
                    for c in range(C0):
                        pool.dma_start(out[:, :, c], I[n][:, c * R0:(c + 1) * R0].rearrange("e r -> r e"),
                                       allow_slow_non_contiguous=True).then_inc(row_in, 16)
                pool.memset(T.identF[:, :], 0.0).then_inc(ident_set, 1)
                pool.memset(T.identB[:, :], 0.0).then_inc(ident_set, 1)
                pool.memset(T.sel[:, :, :, :], 0.0).then_inc(ident_set, 1)
                pool.memset(T.before[:, :], 0.0).then_inc(ident_set, 1)
                pool.wait_ge(ident_set, 4)
                for m in (T.identF, T.identB):
                    pool.affine_select(out=m[:, :], in_=m[:, :], compare_op=ALU.not_equal, fill=1.0, base=0,
                                       pattern=[[-1, P]], channel_multiplier=1).then_inc(ident_ready, 1)
                pool.affine_select(out=T.before[:, :], in_=T.before[:, :], compare_op=ALU.is_ge, fill=1.0, base=0,
                                   pattern=[[-1, P]], channel_multiplier=1).then_inc(ident_ready, 1)
                for base in (0, -32):
                    pool.affine_select(out=T.sel[:, :, :, :], in_=T.sel[:, :, :, :], compare_op=ALU.not_equal,
                                       fill=1.0, base=base, pattern=[[-2, HP], [-1, 2], [0, SEQ]],
                                       channel_multiplier=1).then_inc(ident_ready, 1)
                    pool.wait_ge(ident_ready, 4 if base == 0 else 5)
                pool.iota(T.row_i[:, :], pattern=[[0, 2]], base=0, channel_multiplier=1).then_inc(zero_set, 1)
                pool.iota(T.iota_i[:, :], pattern=[[1, 512]], base=0, channel_multiplier=0).then_inc(zero_set, 1)
                pool.iota(T.iota_p[:, :], pattern=[[0, 1]], base=0, channel_multiplier=1).then_inc(zero_set, 1)
                pool.wait_ge(row_in, 16 * 17)

            @block.tensor
            def _(pe):
                pe.wait_ge(ident_ready, 2)
                for n, (load, count, sources, kind, e) in enumerate(jobs):
                    pe.wait_ge(load, count)
                    if n >= 4:
                        pe.wait_ge(high_done, n - 3)
                        at_least(pe, low_done, lows[n - 4])
                    for j, src in enumerate(sources):
                        k, m = src.shape
                        w = {"small": P, "gates": E, "wrel": P, "down": P}.get(kind, R0)
                        last = pe.transpose(ring[n % 4][0:m, j * w:j * w + k], src, T.identF[0:k, 0:k])
                    last.then_inc(turned, 1)
                pe.wait_ge(row_in, 16 * 17)
                pe.transpose(fold[:, 0:P], T.bv0[:, :], T.identF[:, :]).then_inc(fold_turned, 1)
                pe.wait_ge(fold_copied, 1)
                pe.matmul(fold[:, P:2 * P], bv_t[:, :], T.WT[:, 3, :], start=True, stop=True).then_inc(folded, 1)

            @block.scalar
            def _(act):
                for n, (_, _, _, kind, e) in enumerate(jobs):
                    act.wait_ge(turned, n + 1)
                    out, src = result(kind, ring[n % 4], e, 0)
                    act.copy(out, src).then_inc(high_done, 1)

            @block.vector
            def _(dve):
                dve.memset(T.Wrel[:, :, :], 0.0).then_inc(rel_zero, 1)
                dve.memset(T.ones[:, :], 1.0)
                dve.memset(T.half[:, :], -0.5).then_inc(owned, 1)
                dve.wait_ge(owned, 1)
                dve.memset(T.eps[:, :], LN_EPS)
                for a0, b0 in ((0, 0), (0, 64), (64, 0), (64, 64)):
                    dve.memset(T.mask[a0:a0 + 64, b0:b0 + 64], 0.0 if a0 == b0 else NEG)
                for n, (_, _, _, kind, e) in enumerate(jobs):
                    if kind in ("small", "gates"):
                        continue
                    dve.wait_ge(high_done, n + 1)
                    out, src = result(kind, ring[n % 4], e, 1)
                    high, _ = result(kind, ring[n % 4], e, 0)
                    dve.tensor_tensor(out, src, high, ALU.subtract).then_inc(low_done, 1)
                dve.wait_ge(zero_set, 3)
                dve.tensor_scalar(T.row_i[:, :], T.row_i[:, :], DK, None, ALU.bitwise_and).then_inc(owned, 1)
                dve.wait_ge(owned, 2)
                dve.tensor_scalar(T.owns[:, 0:1], T.row_i[:, 0:1], 0.0, None, ALU.is_equal)
                dve.tensor_scalar(T.owns[:, 1:2], T.row_i[:, 1:2], 0.0, None, ALU.is_gt)
                dve.tensor_copy(T.iotaB[:, :], T.iota_i[:, :])
                dve.tensor_copy(T.iotaP[:, :], T.iota_p[:, :])
                dve.wait_ge(fold_turned, 1)
                dve.tensor_copy(bv_t[:, :], fold[:, 0:P]).then_inc(fold_copied, 1)
                dve.wait_ge(folded, 1)
                dve.tensor_tensor(T.bo0[:, :], T.bo0[:, :], fold[:, P:2 * P], ALU.add)


class Norm:

    def __init__(self, a, T, name="ln"):
        self.T = T
        self.scratch = a.sb(f"{name}_scratch", [P, 1])
        self.stats = [a.sb(f"{name}_stats{v}", [P, G, 6]) for v in range(2)]
        self.mv = [a.sb(f"{name}_mv{v}", [P, G, 2]) for v in range(2)]
        self.var = [a.sb(f"{name}_var{v}", [P, G]) for v in range(2)]
        self.rstd = [a.sb(f"{name}_rstd{v}", [P, G]) for v in range(2)]
        self.xn = [a.sb(f"{name}_xn{v}", [P, G, D]) for v in range(2)]
        self.summed, self.mv_ready, self.var_ready, self.rstd_ready, self.xn_ready = (
            a.sem(f"{name}_{n}") for n in ("summed", "mv_ready", "var_ready", "rstd_ready", "xn_ready"))

    def sums(self, dve, g, v):
        for t in range(G):
            last = dve.bn_stats(self.stats[v][:, t, :], flat2(self.T.X[:, ds(g * G + t, 1), :]))
        last.then_inc(self.summed, 1)
        dve.wait_ge(self.summed, g + 1)
        dve.tensor_copy(self.scratch[:, 0:1], self.stats[v][:, G - 1, 0:1])
        for t in range(G):
            last = dve.bn_aggr(self.mv[v][:, t, :], self.stats[v][:, t, :])
        last.then_inc(self.mv_ready, 1)

    def root(self, pool, g, v):
        pool.wait_ge(self.mv_ready, g + 1)
        pool.tensor_tensor(self.var[v][:, :], self.mv[v][:, :, 1], self.T.eps[:, 0:G], ALU.add)\
            .then_inc(self.var_ready, 1)
        pool.wait_ge(self.var_ready, g + 1)
        pool.tensor_tensor(self.rstd[v][:, :], self.var[v][:, :], self.T.half[:, 0:G], ALU.pow)\
            .then_inc(self.rstd_ready, 1)

    def apply(self, dve, g, v):
        dve.wait_ge(self.rstd_ready, g + 1)
        for t in range(G):
            last = dve.tensor_scalar(self.xn[v][:, t, :], flat2(self.T.X[:, ds(g * G + t, 1), :]),
                                     self.mv[v][:, t, 0:1], self.rstd[v][:, t:t + 1], ALU.subtract, ALU.mult)
        last.then_inc(self.xn_ready, 1)


def project0(nc, I, T):
    with ExitStack() as ctx:
        a = Alloc(nc, ctx, "project0")
        ln = Norm(a, T)
        cx = [a.sb(f"cx{v}", [P, G, D]) for v in range(2)]
        xnT = [a.sb(f"xnT{v}", [P, GT]) for v in range(2)]
        q_split = [a.sb(f"q_split{v}", [P, 4, GT], BF16) for v in range(2)]
        k_full = [a.sb(f"k_full{v}", [P, GT]) for v in range(2)]
        k_split = [a.sb(f"k_split{v}", [P, 2, 2 * G, 2, SEQ], BF16) for v in range(2)]
        xt_ps = [a.ps(f"xt_ps{v}", [P, GT]) for v in range(2)]
        ct_ps = [a.ps(f"ct_ps{v}", [P, GT]) for v in range(2)]
        q_ps = [a.ps(f"q_ps{v}", [P, GT]) for v in range(2)]
        k_ps = [a.ps(f"k_ps{v}", [P, GT]) for v in range(2)]
        x_in = [a.sem(f"x_in{v}") for v in range(2)]
        c_in = [a.sem(f"c_in{v}") for v in range(2)]
        planes_out = [a.sem(f"planes_out{v}") for v in range(2)]
        zeroed, xt_done, ct_done, xt_copied, ct_copied, q_done, k_done, q_high, k_high, low, biased = (
            a.sem(n) for n in ("zeroed", "xt_done", "ct_done", "xt_copied", "ct_copied", "q_done", "k_done",
                               "q_high", "k_high", "low", "biased"))
        k_copied = a.sem("k_copied")
        x_d = I["x"].rearrange("b s d -> (b s) d").rearrange("(n p) d -> p n d", p=P)
        c_d = I["ctx_1024"].rearrange("b s d -> (b s) d").rearrange("(n p) d -> p n d", p=P)

        with nc.Block() as block:
            @block.sync
            def _(sp):
                def load(it):
                    for v in range(2):
                        g = 2 * it + v
                        at_least(sp, ct_done, g - 1)
                        sp.dma_start(T.X[:, ds(g * G, G), :], x_d[:, ds(g * G, G), :]).then_inc(x_in[v], 16)
                        sp.dma_start(cx[v][:, :, :], c_d[:, ds(g * G, G), :]).then_inc(c_in[v], 16)
                rounds(sp, GROUPS // 2, load)

            @block.gpsimd
            def _(pool):
                for v in range(2):
                    pool.memset(q_split[v][:, :, :], 0.0).then_inc(zeroed, 1)

                def body(it):
                    for v in range(2):
                        g = 2 * it + v
                        ln.root(pool, g, v)
                        pool.wait_ge(ln.xn_ready, g + 1)
                        pool.tensor_tensor(T.X[:, ds(g * G, G), :], T.X[:, ds(g * G, G), :],
                                           T.bo0[:, :].unsqueeze(1).to_broadcast([P, G, D]), ALU.add).then_inc(biased, 1)
                rounds(pool, GROUPS // 2, body)

            @block.vector
            def _(dve):
                dve.wait_ge(zeroed, 2)

                def body(it):
                    for v in range(2):
                        g = 2 * it + v
                        dve.wait_ge(x_in[v], 16 * (it + 1))
                        ln.sums(dve, g, v)
                        at_least(dve, xt_done, g - 1)
                        ln.apply(dve, g, v)
                        dve.wait_ge(ct_done, g + 1)
                        dve.tensor_copy(T.ctxT[:, ds(g * GT, GT)], ct_ps[v][:, :]).then_inc(ct_copied, 1)
                        dve.wait_ge(q_high, 2 * g + 2)
                        at_least(dve, planes_out[v], 32 * it)
                        for par in range(2):
                            dve.scalar_tensor_tensor(q_split[v][:, 2 + par, par::2], q_ps[v][:, par::2], T.bcol[:, 0:1],
                                                     q_split[v][:, par, par::2], ALU.add, ALU.subtract)
                        dve.wait_ge(k_high, 2 * g + 2)
                        for h2 in range(2):
                            last = dve.scalar_tensor_tensor(
                                k_split[v][:, 1, :, h2, :], k_full[v][:, :].rearrange("p (b j) -> p b j", j=SEQ),
                                T.owns[:, h2:h2 + 1], k_split[v][:, 0, :, h2, :], ALU.mult, ALU.subtract)
                        last.then_inc(low, 1)
                rounds(dve, GROUPS // 2, body)

            @block.tensor
            def _(pe):
                def body(it):
                    for v in range(2):
                        g = 2 * it + v
                        pe.wait_ge(c_in[v], 16 * (it + 1))
                        at_least(pe, ct_copied, g - 1)
                        for t in range(G):
                            last = pe.transpose(ct_ps[v][:, t * P:(t + 1) * P], cx[v][:, t, :], T.identF[:, :])
                        last.then_inc(ct_done, 1)
                        pe.wait_ge(ln.xn_ready, g + 1)
                        at_least(pe, xt_copied, g - 1)
                        for t in range(G):
                            last = pe.transpose(xt_ps[v][:, t * P:(t + 1) * P], ln.xn[v][:, t, :], T.identF[:, :])
                        last.then_inc(xt_done, 1)
                        at_least(pe, low, g - 1)
                        pe.wait_ge(ct_copied, g + 1)
                        pe.matmul(k_ps[v][:, :], T.WT[:, 1, :], T.ctxT[:, ds(g * GT, GT)], start=True, stop=True)\
                            .then_inc(k_done, 1)
                        pe.wait_ge(xt_copied, g + 1)
                        pe.matmul(q_ps[v][:, :], T.WT[:, 0, :], xnT[v][:, :], start=True, stop=True).then_inc(q_done, 1)
                rounds(pe, GROUPS // 2, body)

            @block.scalar
            def _(act):
                act.wait_ge(zeroed, 2)

                def body(it):
                    for v in range(2):
                        g = 2 * it + v
                        act.wait_ge(xt_done, g + 1)
                        at_least(act, q_done, g - 1)
                        act.copy(xnT[v][:, :], xt_ps[v][:, :]).then_inc(xt_copied, 1)
                        at_least(act, planes_out[v], 32 * it)
                        act.wait_ge(k_done, g + 1)
                        at_least(act, low, g - 1)
                        act.activation(k_full[v][:, :], k_ps[v][:, :], ACT.Identity, bias=T.bcol[:, 1:2])\
                            .then_inc(k_copied, 1)
                        act.wait_ge(k_copied, g + 1)
                        for h2 in range(2):
                            act.activation(k_split[v][:, 0, :, h2, :],
                                           k_full[v][:, :].rearrange("p (b j) -> p b j", j=SEQ),
                                           ACT.Identity, scale=T.owns[:, h2:h2 + 1]).then_inc(k_high, 1)
                        act.wait_ge(q_done, g + 1)
                        for par in range(2):
                            act.activation(q_split[v][:, par, par::2], q_ps[v][:, par::2], ACT.Identity,
                                           bias=T.bcol[:, 0:1]).then_inc(q_high, 1)
                        act.wait_ge(low, g + 1)
                        act.dma_start(T.q_dram[:, :, ds(g * GT, GT)].rearrange("n p t -> p n t"), q_split[v][:, :, :])\
                            .then_inc(planes_out[v], 16)
                        act.dma_start(T.k_dram[:, :, ds(g * 2 * GT, 2 * GT)].rearrange("n p t -> p n t"),
                                      k_split[v][:, :, :, :, :].rearrange("p n b h j -> p n (b h j)"))\
                            .then_inc(planes_out[v], 16)
                rounds(act, GROUPS // 2, body)
                for v in range(2):
                    act.wait_ge(planes_out[v], 32 * (GROUPS // 2))


def attend0(nc, I, T):
    with ExitStack() as ctx:
        a = Alloc(nc, ctx, "attend0")
        Q = [a.sb(f"Q{v}", [QROWS, HP, GT], BF16) for v in range(2)]
        K = [a.sb(f"K{v}", [QROWS, HP, 2 * GT], BF16) for v in range(2)]
        cg = [a.sb(f"cg{v}", [P, 2, 2, SEQ]) for v in range(2)]
        scores = [a.sb(f"scores{v}", [P, HP * P]) for v in range(2)]
        probs = a.sb("probs", [P, 2, 512])
        split = [a.sb(f"split{v}", [P, 2, HP * P], BF16) for v in range(2)]
        V = [a.sb(f"V{v}", [P, 2, HP, 2, 2, DK + 1], BF16) for v in range(2)]
        maxes = a.sb("maxes", [P, P])
        shift = a.sb("shift", [48, P], BF16)
        rsum = a.sb("rsum", [P, HP, 2])
        heads = a.sb("heads", [P, HP, 2, DK])
        headsT = a.sb("headsT", [P, P])
        st = [a.ps(f"st{v}", [P, 2, 512]) for v in range(2)]
        turned_ps = a.ps("turned_ps", [P, 2, 512])
        v_ps = a.ps("v_ps", [P, 512])
        outp = a.ps("outp", [P, 512])
        mt_ps, o_ps, ht_ps, y_ps = turned_ps[:, 0, 0:P], outp[:, 0:HP * 36], outp[:, 384:512], outp[:, 384:512]
        planes_in = [a.sem(f"planes_in{v}") for v in range(2)]
        (set0, cg_ready, st_ready, copied, turned, maxed, m_copied, mt_ready, hi_set, shift_ready, shifted,
         probs_high, exped, probs_low, v_done, v_high, v_ready, pv_done, recip, heads_ready, ht_done, ht_copied, y_done, x_done) = (
            a.sem(n) for n in ("set0", "cg_ready", "st_ready", "copied", "turned", "maxed", "m_copied", "mt_ready",
                               "hi_set", "shift_ready", "shifted", "probs_high", "exped", "probs_low", "v_done", "v_high", "v_ready", "pv_done", "recip",
                               "heads_ready", "ht_done", "ht_copied", "y_done", "x_done"))
        LOADS = 6 + 6
        PAIRS = 2 * G

        def steps(eng, step):
            for u in range(PAIRS):
                step(u, u)
            with eng.Fori(1, TILES // PAIRS) as it:
                for u in range(PAIRS):
                    step(it * PAIRS + u, u)
            for u in range(3):
                step(TILES + u, u)

        def live(p):
            return not isinstance(p, int) or 0 <= p < TILES

        with nc.Block() as block:
            @block.sync
            def _(sp):
                def load(it):
                    for v in range(2):
                        g = 2 * it + v
                        at_least(sp, st_ready, 2 * G * (g - 1))
                        for par in range(2):
                            for s in range(3):
                                row = par * 48 + s * 16
                                sp.dma_start(Q[v][row:row + 16, :, :],
                                             T.q_dram[2 * TERM_HIGH[s] + par, :, ds(g * GT, GT)]
                                             .rearrange("(hp r) t -> r hp t", r=16)).then_inc(planes_in[v], 16)
                                sp.dma_start(K[v][row:row + 16, :, :],
                                             T.k_dram[TERM_W[s], :, ds(g * 2 * GT, 2 * GT)]
                                             .rearrange("(hp r) t -> r hp t", r=16)).then_inc(planes_in[v], 16)
                rounds(sp, GROUPS // 2, load)

            @block.gpsimd
            def _(pool):
                for v in range(2):
                    pool.memset(V[v][:, :, :, :, :, :], 0.0).then_inc(set0, 1)
                pool.memset(maxes[:, :], 0.0).then_inc(set0, 1)
                pool.wait_ge(set0, 3)
                for v in range(2):
                    pool.memset(V[v][0:64, 0, :, :, 0, DK:DK + 1], 1.0).then_inc(set0, 1)
                    pool.memset(V[v][64:P, 0, :, :, 1, DK:DK + 1], 1.0).then_inc(set0, 1)
                pool.wait_ge(set0, 7)

                def step(p, u):
                    if live(p):
                        at_least(pool, v_done, p - 1)
                        pool.tensor_copy(cg[u % 2][:, :, :, :],
                                         T.ctxT[:, ds(p * P, P)].rearrange("p (b t) -> p b t", t=SEQ).unsqueeze(2)
                                         .to_broadcast([P, 2, 2, SEQ])).then_inc(cg_ready, 1)
                    if live(p - 2):
                        q, w = p - 2, u % 2
                        for bank in range(2):
                            pool.wait_ge(exped, 2 * q + 1 + bank)
                            at_least(pool, pv_done, q - 1)
                            cols = slice(bank * 512, bank * 512 + 512)
                            pool.tensor_tensor(split[w][:, 1, cols], probs[:, bank, :], split[w][:, 0, cols],
                                               ALU.subtract).then_inc(probs_low, 1)
                steps(pool, step)

            @block.tensor
            def _(pe):
                def score(p, u, bank):
                    v, w = (u // G) % 2, u % 2
                    at_least(pe, exped, 2 * p - 3 + bank)
                    if bank == 0:
                        if u % G == 0:
                            pe.wait_ge(planes_in[v], 16 * LOADS * 1 if isinstance(p, int) else
                                       (p - u) * (2 * LOADS) + 16 * LOADS)
                    t0 = (u % G) * P
                    out = st[w][:, bank, :].rearrange("p (h b i) -> p h b i", h=4, b=2)
                    for h in range(4):
                        for b in range(2):
                            hp, t = bank * 4 + h, t0 + b * SEQ
                            pe.matmul(out[:, h, b, :], K[v][:, hp, 2 * t:2 * t + P], Q[v][:, hp, t:t + SEQ],
                                      start=(h == 0 and b == 0), stop=False, skip_group_check=True)
                    q4 = Q[v][:, bank * 4:bank * 4 + 4, t0:t0 + P].rearrange("r h (b i) -> r h b i", b=2)
                    for i in range(0, SEQ, 2):
                        last = pe.matmul(out[:, :, :, i:i + 2], T.Wrel[:, i // 2, :], q4[:, :, :, i:i + 2],
                                         start=False, stop=(i == SEQ - 2), skip_group_check=True)
                    last.then_inc(st_ready, 1)

                def turn(p, u):
                    w = u % 2
                    at_least(pe, shift_ready, p)
                    for bank in range(2):
                        pe.wait_ge(copied, 2 * p + 1 + bank)
                        for h in range(4):
                            c = (bank * 4 + h) * P
                            last = pe.transpose(turned_ps[:, bank, h * P:(h + 1) * P], scores[w][:, c:c + P],
                                                T.identF[:, :])
                        last.then_inc(turned, 1)

                def subtract_max(p, u):
                    w = u % 2
                    pe.wait_ge(shift_ready, p + 1)
                    for hp in range(HP):
                        last = pe.matmul(st[w][:, hp // 4, (hp % 4) * P:(hp % 4 + 1) * P],
                                         T.sel[:, hp, :, :], shift[:, :],
                                         start=False, stop=True, skip_group_check=True)
                    last.then_inc(shifted, 1)

                def weigh(p, u):
                    w = u % 2
                    pe.wait_ge(probs_low, 2 * p + 2)
                    pe.wait_ge(v_ready, 2 * p + 2)
                    at_least(pe, ht_copied, p)
                    for hp in range(HP):
                        for n, (ph, vh) in enumerate(((0, 0), (0, 1), (1, 0))):
                            last = pe.matmul(o_ps[:, hp * 36:hp * 36 + 36], split[w][:, ph, hp * P:(hp + 1) * P],
                                             V[w][:, vh, hp, :, :, :].rearrange("p b h d -> p (b h d)"),
                                             start=(n == 0), stop=(n == 2))
                    last.then_inc(pv_done, 1)

                def values(p, u):
                    pe.wait_ge(cg_ready, p + 1)
                    at_least(pe, v_ready, 2 * p)
                    for b in range(2):
                        last = pe.matmul(v_ps[:, b * P:(b + 1) * P],
                                         cg[u % 2][:, b, :, :], T.WT[:, 2, :], start=True, stop=True)
                    last.then_inc(v_done, 1)

                def step(p, u):
                    u1, u2 = (u - 1) % PAIRS, (u - 2) % PAIRS
                    if live(p - 1):
                        turn(p - 1, u1)
                    if live(p - 3):
                        q = p - 3
                        pe.wait_ge(heads_ready, 2 * q + 2)
                        at_least(pe, x_done, q)
                        pe.transpose(ht_ps, heads[:, :, :, :].rearrange("p a b d -> p (a b d)"), T.identF[:, :])\
                            .then_inc(ht_done, 1)
                    if live(p):
                        score(p, u, 0)
                    if live(p):
                        score(p, u, 1)
                    if live(p - 1):
                        pe.wait_ge(m_copied, p)
                        pe.transpose(mt_ps, maxes[:, :], T.identF[:, :]).then_inc(mt_ready, 1)
                    if live(p - 2):
                        weigh(p - 2, u2)
                    if live(p - 3):
                        pe.wait_ge(ht_copied, p - 2)
                        pe.matmul(y_ps, headsT[:, :], T.WT[:, 3, :], start=True, stop=True).then_inc(y_done, 1)
                    if live(p - 1):
                        subtract_max(p - 1, u1)
                    if live(p):
                        values(p, u)
                steps(pe, step)

            @block.scalar
            def _(act):
                def step(p, u):
                    if live(p - 3):
                        act.wait_ge(ht_done, p - 2)
                        at_least(act, y_done, p - 3)
                        act.copy(headsT[:, :], ht_ps).then_inc(ht_copied, 1)
                    if live(p):
                        at_least(act, turned, 2 * (p - 1))
                        for bank in range(2):
                            act.wait_ge(st_ready, 2 * p + 1 + bank)
                            act.copy(scores[u % 2][:, bank * 512:(bank + 1) * 512], st[u % 2][:, bank, :])\
                                .then_inc(copied, 1)
                    if live(p - 1):
                        q, w = p - 1, (u - 1) % 2
                        act.wait_ge(shifted, q + 1)
                        for bank in range(2):
                            at_least(act, pv_done, q - 1)
                            act.activation(split[w][:, 0, bank * 512:(bank + 1) * 512], st[w][:, bank, :],
                                           ACT.Exp, scale=DK ** -0.5).then_inc(probs_high, 1)
                            at_least(act, probs_low, 2 * q - 1 + bank)
                            act.activation(probs[:, bank, :], st[w][:, bank, :], ACT.Exp, scale=DK ** -0.5)\
                                .then_inc(exped, 1)
                steps(act, step)

            @block.vector
            def _(dve):
                dve.wait_ge(set0, 7)

                def step(p, u):
                    if live(p - 1):
                        q = p - 1
                        at_least(dve, mt_ready, q)
                        for bank in range(2):
                            dve.wait_ge(turned, 2 * q + 1 + bank)
                            dve.tensor_reduce(maxes[:, bank * 8:bank * 8 + 8],
                                              turned_ps[:, bank, :].rearrange("p (h j) -> p h j", j=SEQ),
                                              AX_X, ALU.max).then_inc(maxed, 1)
                        dve.wait_ge(maxed, 2 * q + 2)
                        dve.tensor_copy(maxes[:, 32:48], maxes[:, 0:16]).then_inc(m_copied, 1)
                    if live(p - 1):
                        q, w = p - 1, (u - 1) % 2
                        dve.wait_ge(v_done, q + 1)
                        at_least(dve, pv_done, q - 1)
                        for half, ready in ((0, v_high), (1, v_ready)):
                            if half:
                                dve.wait_ge(v_high, 2 * q + 2)
                            for h2 in range(2):
                                rows = slice(64 * h2, 64 * h2 + 64)
                                out, high = (V[w][rows, n, :, :, h2, 0:DK].rearrange("p hp b d -> p b hp d") for n in (half, 0))
                                full = v_ps[rows, 0:2 * P].rearrange("p (b hp h d) -> p b hp h d", b=2, hp=HP, h=2)[:, :, :, h2, :]
                                if half:
                                    dve.tensor_tensor(out, full, high, ALU.subtract).then_inc(v_ready, 1)
                                else:
                                    dve.tensor_copy(out, full).then_inc(v_high, 1)
                    if live(p - 1):
                        q = p - 1
                        dve.wait_ge(mt_ready, q + 1)
                        at_least(dve, shifted, q)
                        dve.tensor_scalar(shift[:, :], mt_ps[0:48, :], -1.0, None, ALU.mult).then_inc(hi_set, 1)
                        dve.wait_ge(hi_set, q + 1)
                        dve.scalar_tensor_tensor(shift[32:48, :], mt_ps[32:48, :], -1.0, shift[32:48, :],
                                                 ALU.mult, ALU.subtract).then_inc(shift_ready, 1)
                    if live(p - 3):
                        q = p - 3
                        dve.wait_ge(y_done, q + 1)
                        x = flat2(T.X[:, ds(q, 1), :])
                        dve.tensor_tensor(x, y_ps, x, ALU.add).then_inc(x_done, 1)
                    if live(p - 2):
                        q = p - 2
                        dve.wait_ge(pv_done, q + 1)
                        at_least(dve, ht_done, q)
                        o = o_ps.rearrange("p (hp b h d) -> p hp b h d", hp=HP, b=2, h=2)
                        for b in range(2):
                            rows = slice(64 * b, 64 * b + 64)
                            dve.reciprocal(rsum[rows, :, :], o[rows, :, b, :, DK]).then_inc(recip, 1)
                        for b in range(2):
                            rows = slice(64 * b, 64 * b + 64)
                            dve.wait_ge(recip, 2 * q + 1 + b)
                            dve.tensor_tensor(heads[rows, :, :, :], o[rows, :, b, :, 0:DK],
                                              rsum[rows, :, :].unsqueeze(3).to_broadcast([64, HP, 2, DK]), ALU.mult)\
                                .then_inc(heads_ready, 1)
                steps(dve, step)


class Scores:

    def __init__(self, a, T, gate):
        self.T, self.gate = T, gate
        self.ln = Norm(a, T)
        self.SC = a.sb("SC", [P, TILES, E])
        self.xnT = [a.sb(f"xnT{v}", [P, GT]) for v in range(2)]
        self.xt_ps = [a.ps(f"xt_ps{v}", [P, GT]) for v in range(2)]
        self.s_ps = [a.ps(f"s_ps{v}", [P, G * E]) for v in range(2)]
        self.xt_done, self.xt_copied, self.s_done, self.s_ready, self.high, self.low = (
            a.sem(n) for n in ("xt_done", "xt_copied", "s_done", "s_ready", "high", "low"))

    def pool(self, pool):
        def body(it):
            for v in range(2):
                g = 2 * it + v
                self.ln.root(pool, g, v)
                pool.wait_ge(self.ln.xn_ready, g + 1)
                pool.tensor_copy(self.T.XHL[:, ds(g * G, G), 0, :], self.ln.xn[v][:, :, :]).then_inc(self.high, 1)
        rounds(pool, GROUPS // 2, body)

    def vector(self, dve):
        def step(s, v):
            w = 1 - v
            if not isinstance(s, int) or s < GROUPS:
                self.ln.sums(dve, s, v)
            if not isinstance(s, int) or 0 < s <= GROUPS:
                at_least(dve, self.xt_done, s - 2)
                at_least(dve, self.low, s - 2)
                self.ln.apply(dve, s - 1, w)
            if not isinstance(s, int) or s > 1:
                g = s - 2
                dve.wait_ge(self.high, g + 1)
                dve.tensor_tensor(self.T.XHL[:, ds(g * G, G), 1, :], self.ln.xn[v][:, :, :],
                                  self.T.XHL[:, ds(g * G, G), 0, :], ALU.subtract).then_inc(self.low, 1)
                dve.wait_ge(self.s_done, g + 1)
                out = self.SC[:, ds(g * G, G), :]
                sc = self.s_ps[v][:, :].rearrange("p (t e) -> p t e", e=E)
                if self.gate == 0:
                    dve.tensor_tensor(out, sc, self.T.gb0[:, :].unsqueeze(1).to_broadcast([P, G, E]), ALU.add)\
                        .then_inc(self.s_ready, 1)
                else:
                    dve.tensor_copy(out, sc).then_inc(self.s_ready, 1)
        for s in range(4):
            step(s, s % 2)
        with dve.Fori(2, GROUPS // 2) as it:
            for v in range(2):
                step(it * 2 + v, v)
        for v in range(2):
            step(GROUPS + v, v)

    def tensor(self, pe):
        def body(it):
            for v in range(2):
                g = 2 * it + v
                pe.wait_ge(self.ln.xn_ready, g + 1)
                at_least(pe, self.xt_copied, g - 1)
                for t in range(G):
                    last = pe.transpose(self.xt_ps[v][:, t * P:(t + 1) * P], self.ln.xn[v][:, t, :],
                                        self.T.identF[:, :])
                last.then_inc(self.xt_done, 1)
                pe.wait_ge(self.xt_copied, g + 1)
                at_least(pe, self.s_ready, g - 1)
                for t in range(G):
                    last = pe.matmul(self.s_ps[v][:, t * E:(t + 1) * E], self.xnT[v][:, t * P:(t + 1) * P],
                                     self.T.gateT[:, self.gate, :], start=True, stop=True)
                last.then_inc(self.s_done, 1)
        rounds(pe, GROUPS // 2, body)

    def scalar(self, act):
        def body(it):
            for v in range(2):
                g = 2 * it + v
                act.wait_ge(self.xt_done, g + 1)
                at_least(act, self.s_done, g - 1)
                act.copy(self.xnT[v][:, :], self.xt_ps[v][:, :]).then_inc(self.xt_copied, 1)
        rounds(act, GROUPS // 2, body)


class Chain:

    def __init__(self, eng, sem):
        self.eng, self.sem, self.n = eng, sem, 0

    def __call__(self, ins):
        self.n += 1
        ins.then_inc(self.sem, 1)
        self.eng.wait_ge(self.sem, self.n)


def spread(ap, n):
    return ap.unsqueeze(2).to_broadcast([ap.shape[0], ap.shape[1], n])


def softmax_first(dve, chain, sc, SC, peak, shifted_ready):
    dve.wait_ge(sc.s_ready, GROUPS)
    chain(dve.tensor_reduce(peak, SC, AX_X, ALU.max))
    dve.tensor_tensor(SC, SC, spread(peak, E), ALU.subtract).then_inc(shifted_ready, 1)


def softmax_last(dve, chain, PR, total, exp_ready):
    dve.wait_ge(exp_ready, 1)
    chain(dve.tensor_reduce(total, PR, AX_X, ALU.add))
    chain(dve.reciprocal(total, total))
    chain(dve.tensor_tensor(PR, PR, spread(total, E), ALU.mult))


def route0(nc, I, T):
    with ExitStack() as ctx:
        a = Alloc(nc, ctx, "route0")
        sc = Scores(a, T, 0)
        PR, eq, rest, A, one1, one2 = (a.sb(n, [P, TILES, E]) for n in ("PR", "eq", "rest", "A", "one1", "one2"))
        peak, total, p1, p2, top = (a.sb(n, [P, TILES]) for n in ("peak", "total", "p1", "p2", "top"))
        rank8, count, padded, begin, adjust, ones8 = (a.sb(n, [P, E]) for n in ("rank8", "count", "padded", "begin",
                                                                              "adjust", "ones8"))
        padded_i = a.sb("padded_i", [P, E], I32)
        chosen = a.sb("chosen", [P, E, TILES], BF16)
        onesf, csum, pre, tot = (a.sb(n, [P, E * TILES]) for n in ("onesf", "csum", "pre", "tot"))
        slot_f = a.sb("slot_f", [P, TOPK, TILES])
        reach = a.sb("reach", [P, SLOT_TILES, E])
        first = a.sb("first", [P, SLOT_TILES])
        owner = a.sb("owner", [P, SLOT_TILES])
        zeros = a.sb("zeros", [P, 8, 2 * D], BF16)
        pre_ps = a.ps("pre_ps", [P, 512])
        tot_ps = a.ps("tot_ps", [P, 512])
        zset, zero_out, shifted_ready, exp_ready, chosen_ready, counted, step, slots_ready, sent = (
            a.sem(n) for n in ("zset", "zero_out", "shifted_ready", "exp_ready", "chosen_ready", "counted", "step",
                               "slots_ready", "sent"))
        with nc.Block() as block:
            @block.sync
            def _(sp):
                sp.wait_ge(zset, 1)
                for c in range(ST * SLOT_TILES // (8 * P)):
                    sp.dma_start(T.xs_dram[c * 8 * P:(c + 1) * 8 * P, :].rearrange("(n p) d -> p n d", p=P),
                                 zeros[:, :, :]).then_inc(zero_out, 16)
                sp.wait_ge(zero_out, 16 * (ST * SLOT_TILES // (8 * P)))

            @block.gpsimd
            def _(pool):
                pool.memset(zeros[:, :, :], 0.0).then_inc(zset, 1)
                sc.pool(pool)
                pool.wait_ge(zero_out, 16 * (ST * SLOT_TILES // (8 * P)))
                pool.wait_ge(sc.low, GROUPS)
                pool.wait_ge(slots_ready, 1)
                for t in range(TILES):
                    for k in range(TOPK):
                        pool.indirect_dma_start(
                            T.xs_dram[:, :], bass.IndirectOffsetOnAxis(ap=T.slot[:, k, t:t + 1].bitcast(U32), axis=0),
                            T.XHL[:, t, :, :].rearrange("p a d -> p (a d)"), None).then_inc(sent, 16)
                pool.wait_ge(sent, 16 * TILES * TOPK)

            @block.tensor
            def _(pe):
                sc.tensor(pe)
                pe.wait_ge(chosen_ready, 1)
                m = chosen[:, :, :].rearrange("p e t -> p (e t)")
                pe.matmul(pre_ps[:, 0:E * TILES], T.before[:, :], m, start=True, stop=True)
                pe.matmul(tot_ps[:, 0:E * TILES], T.ones[:, :], m, start=True, stop=True).then_inc(counted, 1)

            @block.scalar
            def _(act):
                sc.scalar(act)
                act.wait_ge(shifted_ready, 1)
                act.activation(PR[:, :, :], sc.SC[:, :, :], ACT.Exp).then_inc(exp_ready, 1)

            @block.vector
            def _(dve):
                chain = Chain(dve, step)
                dve.memset(onesf[:, :], 1.0)
                dve.memset(ones8[:, :], 1.0)
                dve.tensor_scalar(first[:, :], T.iotaB[:, 0:SLOT_TILES], float(ST), None, ALU.mult)
                chain(dve.tensor_scalar(rank8[:, :], T.iotaB[:, 0:E], -1.0, float(E), ALU.mult, ALU.add))
                sc.vector(dve)
                softmax_first(dve, chain, sc, sc.SC[:, :, :], peak[:, :], shifted_ready)
                softmax_last(dve, chain, PR[:, :, :], total[:, :], exp_ready)
                ranks = rank8[:, :].unsqueeze(1).to_broadcast([P, TILES, E])
                src = PR
                for value, one in ((p1, one1), (p2, one2)):
                    chain(dve.tensor_reduce(value[:, :], src[:, :, :], AX_X, ALU.max))
                    chain(dve.tensor_tensor(eq[:, :, :], src[:, :, :], spread(value[:, :], E), ALU.is_equal))
                    chain(dve.tensor_tensor(eq[:, :, :], eq[:, :, :], ranks, ALU.mult))
                    chain(dve.tensor_reduce(top[:, :], eq[:, :, :], AX_X, ALU.max))
                    chain(dve.tensor_tensor(one[:, :, :], eq[:, :, :], spread(top[:, :], E), ALU.is_equal))
                    if one is one1:
                        chain(dve.scalar_tensor_tensor(rest[:, :, :], one1[:, :, :], -2.0, PR[:, :, :], ALU.mult, ALU.add))
                    src = rest
                chain(dve.tensor_tensor(chosen[:, :, :].rearrange("p e t -> p t e"), one1[:, :, :], one2[:, :, :], ALU.add))
                dve.sem_inc(chosen_ready, 1)
                chain(dve.tensor_tensor(total[:, :], p1[:, :], p2[:, :], ALU.add))
                chain(dve.tensor_scalar(total[:, :], total[:, :], 1e-20, None, ALU.add))
                chain(dve.reciprocal(total[:, :], total[:, :]))
                dve.tensor_tensor(T.share[:, 0, :], p1[:, :], total[:, :], ALU.mult)
                dve.tensor_tensor(T.share[:, 1, :], p2[:, :], total[:, :], ALU.mult)
                dve.wait_ge(counted, 1)
                chain(dve.tensor_copy(tot[:, :], tot_ps[:, 0:E * TILES]))
                chain(dve.tensor_copy(pre[:, :], pre_ps[:, 0:E * TILES]))
                chain(dve.tensor_reduce(count[:, :], tot[:, :].rearrange("p (e t) -> p e t", e=E), AX_X, ALU.add))
                chain(dve.tensor_scalar(padded[:, :], count[:, :], float(ST - 1), None, ALU.add))
                chain(dve.tensor_copy(padded_i[:, :], padded[:, :]))
                chain(dve.tensor_scalar(padded_i[:, :], padded_i[:, :], -ST, None, ALU.bitwise_and))
                chain(dve.tensor_copy(padded[:, :], padded_i[:, :]))
                chain(dve.tensor_tensor_scan(begin[:, :], ones8[:, :], padded[:, :], 0.0, ALU.mult, ALU.add))
                chain(dve.tensor_tensor(begin[:, :], begin[:, :], padded[:, :], ALU.subtract))
                chain(dve.tensor_tensor_scan(adjust[:, :], ones8[:, :], count[:, :], 0.0, ALU.mult, ALU.add))
                chain(dve.tensor_tensor(adjust[:, :], adjust[:, :], count[:, :], ALU.subtract))
                chain(dve.tensor_tensor(adjust[:, :], begin[:, :], adjust[:, :], ALU.subtract))
                chain(dve.tensor_tensor_scan(csum[:, :], onesf[:, :], tot[:, :], 0.0, ALU.mult, ALU.add))
                chain(dve.tensor_tensor(csum[:, :], csum[:, :], tot[:, :], ALU.subtract))
                chain(dve.tensor_tensor(csum[:, :], csum[:, :], pre[:, :], ALU.add))
                c3 = csum[:, :].rearrange("p (e t) -> p e t", e=E)
                chain(dve.tensor_tensor(c3, c3, spread(adjust[:, :], TILES), ALU.add))
                for k, one in ((0, one1), (1, one2)):
                    chain(dve.tensor_tensor(A[:, :, :], one[:, :, :], c3.rearrange("p e t -> p t e"), ALU.mult))
                    chain(dve.tensor_reduce(slot_f[:, k, :], A[:, :, :], AX_X, ALU.add))
                dve.tensor_copy(T.slot[:, :, :], slot_f[:, :, :]).then_inc(slots_ready, 1)
                chain(dve.tensor_tensor(reach[:, :, :], spread(first[:, :], E),
                                        begin[:, :].unsqueeze(1).to_broadcast([P, SLOT_TILES, E]), ALU.is_ge))
                chain(dve.tensor_reduce(owner[:, :], reach[:, :, :], AX_X, ALU.add))
                chain(dve.tensor_scalar(owner[:, :], owner[:, :], -1.0, None, ALU.add))
                dve.tensor_copy(T.owner[:, :], owner[:, :])


def experts0(nc, I, T):
    with ExitStack() as ctx:
        a = Alloc(nc, ctx, "experts0")
        LAG = 5
        RING = 8
        SUB = ST // P
        HC = C0 // 2
        HW = HC * ST
        xs = [a.sb(f"xs{v}", [P, SUB, 2 * D], BF16) for v in range(RING)]
        xt = [a.sb(f"xt{v}", [P, 2, ST], BF16) for v in range(2)]
        gated = [a.sb(f"gated{v}", [R0, HW]) for v in range(2)]
        z = [a.sb(f"z{v}", [R0, HW]) for v in range(2)]
        hidden = [a.sb(f"hidden{v}", [R0, HW]) for v in range(2)]
        hh = [a.sb(f"hh{v}", [R0, 2, C0, ST], BF16) for v in range(2)]
        ys = [a.sb(f"ys{v}", [P, SUB, D]) for v in range(2)]
        xt_ps = [a.ps(f"xt_ps{v}", [P, 2, ST], BF16) for v in range(2)]
        g_ps = [a.ps(f"g_ps{v}", [P, HW]) for v in range(2)]
        u_ps = [a.ps(f"u_ps{v}", [P, HW]) for v in range(2)]
        y_ps = [a.ps(f"y_ps{v}", [P, SUB, D]) for v in range(2)]
        xs_in = [a.sem(f"xs_in{v}") for v in range(RING)]
        ys_out = [a.sem(f"ys_out{v}") for v in range(2)]
        xt_done, xt_copied, g_done, u_done, gate_ready, z_ready, silu_ready, high, low, y_done, y_ready = (
            a.sem(n) for n in ("xt_done", "xt_copied", "g_done", "u_done", "gate_ready", "z_ready", "silu_ready",
                               "high", "low", "y_done", "y_ready"))

        def live(p):
            return not isinstance(p, int) or 0 <= p < SLOT_TILES

        def owners_from(eng, first, back, count=None):
            count = count or RING + back
            _, values = nc.values_load_multi_w_load_instructions(
                T.owner[0:1, ds(first, count)], engines=[eng.engine], min_val=0, max_val=E - 1)
            return {n - back: value for n, value in enumerate(values)}

        def steps(step, experts=True, tail=2):
            def run(eng):
                owners = owners_from(eng, 0, 0) if experts else None
                for p in range(RING):
                    step(p, p, owners)
                with eng.Fori(1, SLOT_TILES // RING) as it:
                    owners = owners_from(eng, it * RING - 2, 2) if experts else None
                    for u in range(RING):
                        step(it * RING + u, u, owners)
                owners = owners_from(eng, SLOT_TILES - 2, 2, 2) if experts else None
                for u in range(tail):
                    step(SLOT_TILES + u, u % RING, owners)
            return run

        def one(ap):
            return ap.rearrange("p a n -> p (a n)")

        with nc.Block() as block:
            @block.sync
            def _(sp):
                def step(q, u, _):
                    if live(q):
                        at_least(sp, xt_done, q - RING + 1)
                        sp.dma_start(xs[u][:, :, :], T.xs_dram[ds(q * ST, ST), :].rearrange("(s p) d -> p s d", p=P))\
                            .then_inc(xs_in[u], 16)
                    if live(q - LAG):
                        sp.wait_ge(y_ready, q - LAG + 1)
                        w = (u - LAG) % 2
                        sp.dma_start(T.ys_dram[ds((q - LAG) * ST, ST), :].rearrange("(s p) d -> p s d", p=P),
                                     ys[w][:, :, :]).then_inc(ys_out[w], 16)
                steps(step, False, LAG)(sp)
                for v in range(2):
                    sp.wait_ge(ys_out[v], 8 * SLOT_TILES)

            @block.tensor
            def _(pe):
                TERMS = ((0, 0), (0, 1), (1, 0))

                def step(p, ring, owners):
                    u = ring % 2
                    if live(p):
                        pe.wait_ge(xs_in[ring], (p - ring) * (16 // RING) + 16)
                        at_least(pe, xt_copied, p - 1)
                        for half in range(2):
                            for sub in range(SUB):
                                last = pe.transpose(xt_ps[u][:, half, sub * P:(sub + 1) * P],
                                                    xs[ring][:, sub, half * D:(half + 1) * D], T.identB[:, :])
                        last.then_inc(xt_done, 1)
                    if live(p - 1):
                        v = 1 - u
                        e = owners[ring - 1]
                        pe.wait_ge(xt_copied, p)
                        for j in range(2):
                            for ps, W, done, read in ((g_ps, T.WG, g_done, gate_ready), (u_ps, T.WU, u_done, z_ready)):
                                at_least(pe, read, 2 * (p - 2) + j + 1)
                                for c in range(HC):
                                    cc = j * HC + c
                                    for n, (wh, xh) in enumerate(TERMS):
                                        last = pe.matmul(ps[j][0:R0, c * ST:(c + 1) * ST],
                                                         one(W[:, wh, ds(e, 1), cc * R0:(cc + 1) * R0]), xt[v][:, xh, :],
                                                         start=(n == 0), stop=(n == 2))
                                last.then_inc(done, 1)
                    if live(p - 2):
                        e = owners[ring - 2]
                        pe.wait_ge(high, 2 * (p - 1))
                        pe.wait_ge(low, 2 * (p - 1))
                        at_least(pe, y_ready, p - 3)
                        for sub in range(SUB):
                            for c in range(C0):
                                for n, (wh, xh) in enumerate(TERMS):
                                    last = pe.matmul(y_ps[u][:, sub, :], hh[u][:, xh, c, sub * P:(sub + 1) * P],
                                                     one(T.WD[:, wh, ds(e, 1), c * P:(c + 1) * P]),
                                                     start=(c == 0 and n == 0), stop=(c == C0 - 1 and n == 2))
                        last.then_inc(y_done, 1)
                steps(step)(pe)

            @block.scalar
            def _(act):
                def step(p, ring, owners):
                    if live(p - 1):
                        v = 1 - ring % 2
                        e = owners[ring - 1]
                        for j in range(2):
                            act.wait_ge(g_done, 2 * (p - 1) + j + 1)
                            at_least(act, z_ready, 2 * (p - 2) + j + 1)
                            for c in range(HC):
                                last = act.activation(gated[j][:, c * ST:(c + 1) * ST], g_ps[j][0:R0, c * ST:(c + 1) * ST],
                                                      ACT.Identity, bias=one(T.gb[:, ds(e, 1), j * HC + c:j * HC + c + 1]))
                            last.then_inc(gate_ready, 1)
                        for j in range(2):
                            act.wait_ge(z_ready, 2 * (p - 1) + j + 1)
                            at_least(act, y_done, p - 2)
                            act.activation(hh[v][:, 0, j * HC:(j + 1) * HC, :].rearrange("p c t -> p (c t)"), z[j][:, :],
                                           ACT.Silu).then_inc(high, 1)
                            at_least(act, low, 2 * (p - 2) + j + 1)
                            act.activation(hidden[j][:, :], z[j][:, :], ACT.Silu).then_inc(silu_ready, 1)
                steps(step)(act)

            @block.vector
            def _(dve):
                def step(p, ring, owners):
                    u = ring % 2
                    if live(p):
                        dve.wait_ge(xt_done, p + 1)
                        at_least(dve, u_done, 2 * (p - 1))
                        dve.tensor_copy(xt[u][:, :, :], xt_ps[u][:, :, :]).then_inc(xt_copied, 1)
                    if live(p - 2):
                        for j in range(2):
                            dve.wait_ge(silu_ready, 2 * (p - 2) + j + 1)
                            at_least(dve, y_done, p - 3)
                            h = hh[u][:, :, j * HC:(j + 1) * HC, :].rearrange("p h c t -> p h (c t)")
                            dve.tensor_tensor(h[:, 1, :], hidden[j][:, :], h[:, 0, :], ALU.subtract).then_inc(low, 1)
                    if live(p - 1):
                        e = owners[ring - 1]
                        for j in range(2):
                            dve.wait_ge(u_done, 2 * (p - 1) + j + 1)
                            dve.wait_ge(gate_ready, 2 * (p - 1) + j + 1)
                            at_least(dve, silu_ready, 2 * (p - 2) + j + 1)
                            for c in range(HC):
                                last = dve.scalar_tensor_tensor(
                                    z[j][:, c * ST:(c + 1) * ST], u_ps[j][0:R0, c * ST:(c + 1) * ST],
                                    one(T.ub[:, ds(e, 1), j * HC + c:j * HC + c + 1]), gated[j][:, c * ST:(c + 1) * ST],
                                    ALU.add, ALU.mult)
                            last.then_inc(z_ready, 1)
                    if live(p - 2):
                        e = owners[ring - 2]
                        dve.wait_ge(y_done, p - 1)
                        at_least(dve, ys_out[u], 8 * (p - u) - 16)
                        dve.tensor_tensor(ys[u][:, :, :], y_ps[u][:, :, :],
                                          T.db0[:, ds(e, 1), :].to_broadcast([P, SUB, D]), ALU.add).then_inc(y_ready, 1)
                steps(step)(dve)


def combine0(nc, I, T):
    with ExitStack() as ctx:
        a = Alloc(nc, ctx, "combine0")
        rows = a.sb("rows", [P, TILES, TOPK, D])
        rows_in = [a.sem(f"rows_in{t}") for t in range(GROUPS)]
        added = a.sem("added")
        with nc.Block() as block:
            @block.gpsimd
            def _(pool):
                for t in range(TILES):
                    for k in range(TOPK):
                        pool.indirect_dma_start(
                            rows[:, t, k, :], None, T.ys_dram[:, :],
                            bass.IndirectOffsetOnAxis(ap=T.slot[:, k, t:t + 1].bitcast(U32), axis=0))\
                            .then_inc(rows_in[t // G], 16)

            @block.vector
            def _(dve):
                for t in range(TILES):
                    dve.wait_ge(rows_in[t // G], 16 * TOPK * G)
                    for k in range(TOPK):
                        dve.scalar_tensor_tensor(T.X[:, t, :], rows[:, t, k, :], T.share[:, k, t:t + 1], T.X[:, t, :],
                                                 ALU.mult, ALU.add).then_inc(added, 1)
                        dve.wait_ge(added, 2 * t + k + 1)


def attend1(nc, I, T):
    with ExitStack() as ctx:
        a = Alloc(nc, ctx, "attend1")
        SCALE = D ** -0.5
        ln = Norm(a, T)
        cg, qT, kT, V = ([a.sb(f"{n}{v}", [P, GT]) for v in range(2)] for n in ("cg", "qT", "kT", "V"))
        xnT, sm, probs, pT, oT = (a.sb(n, [P, GT]) for n in ("xnT", "sm", "probs", "pT", "oT"))
        peak, nmax, total, inverse = (a.sb(n, [P, G]) for n in ("peak", "nmax", "total", "inverse"))
        xt_ps, q_ps, k_ps, v_ps, s_ps, p_ps, o_ps, y_ps = (
            a.ps(n, [P, GT]) for n in ("xt_ps", "q_ps", "k_ps", "v_ps", "s_ps", "p_ps", "o_ps", "y_ps"))
        (cg_ready, xt_done, xt_copied, q_done, q_ready, k_done, k_ready, v_done, v_ready, s_done, masked, peaked,
         nmax_ready, exped, p_done, p_copied, o_done, o_copied, y_done, inverted, x_done, biased) = (
            a.sem(n) for n in ("cg_ready", "xt_done", "xt_copied", "q_done", "q_ready", "k_done", "k_ready", "v_done",
                               "v_ready", "s_done", "masked", "peaked", "nmax_ready", "exped", "p_done", "p_copied",
                               "o_done", "o_copied", "y_done", "inverted", "x_done", "biased"))

        def tile(t):
            return slice(t * P, (t + 1) * P)

        def live(g):
            return not isinstance(g, int) or 0 <= g < GROUPS

        def steps(eng, step):
            for g in range(2):
                step(g, g)
            with eng.Fori(1, GROUPS // 2) as it:
                for v in range(2):
                    step(it * 2 + v, v)
            step(GROUPS, 0)

        with nc.Block() as block:
            @block.gpsimd
            def _(pool):
                def body(it):
                    for v in range(2):
                        g = 2 * it + v
                        at_least(pool, v_done, g - 1)
                        pool.tensor_copy(cg[v][:, :], T.ctxT[:, ds(g * GT, GT)]).then_inc(cg_ready, 1)
                        ln.root(pool, g, v)
                        pool.wait_ge(ln.xn_ready, g + 1)
                        pool.tensor_tensor(T.X[:, ds(g * G, G), :], T.X[:, ds(g * G, G), :],
                                           T.bo1[:, :].unsqueeze(1).to_broadcast([P, G, D]), ALU.add).then_inc(biased, 1)
                rounds(pool, GROUPS // 2, body)

            @block.tensor
            def _(pe):
                def step(g, v):
                    w, b = 1 - v, g - 1
                    if live(g):
                        pe.wait_ge(ln.xn_ready, g + 1)
                        at_least(pe, xt_copied, g)
                        for t in range(G):
                            last = pe.transpose(xt_ps[:, tile(t)], ln.xn[v][:, t, :], T.identF[:, :])
                        last.then_inc(xt_done, 1)
                    if live(b):
                        pe.wait_ge(q_ready, b + 1)
                        pe.wait_ge(k_ready, b + 1)
                        at_least(pe, masked, b)
                        for t in range(G):
                            last = pe.matmul(s_ps[:, tile(t)], qT[w][:, tile(t)], kT[w][:, tile(t)],
                                             start=True, stop=True)
                        last.then_inc(s_done, 1)
                    if live(g):
                        pe.wait_ge(cg_ready, g + 1)
                        at_least(pe, k_ready, g)
                        pe.matmul(k_ps[:, :], T.WT[:, 5, :], cg[v][:, :], start=True, stop=True).then_inc(k_done, 1)
                        at_least(pe, v_ready, g)
                        for t in range(G):
                            last = pe.matmul(v_ps[:, tile(t)], cg[v][:, tile(t)], T.WT[:, 6, :], start=True, stop=True)
                        last.then_inc(v_done, 1)
                    if live(b):
                        pe.wait_ge(exped, b + 1)
                        at_least(pe, p_copied, b)
                        for t in range(G):
                            last = pe.transpose(p_ps[:, tile(t)], probs[:, tile(t)], T.identF[:, :])
                        last.then_inc(p_done, 1)
                    if live(g):
                        pe.wait_ge(xt_copied, g + 1)
                        at_least(pe, q_ready, g)
                        pe.matmul(q_ps[:, :], T.WT[:, 4, :], xnT[:, :], start=True, stop=True).then_inc(q_done, 1)
                    if live(b):
                        pe.wait_ge(p_copied, b + 1)
                        at_least(pe, o_copied, b)
                        for t in range(G):
                            last = pe.matmul(o_ps[:, tile(t)], V[w][:, tile(t)], pT[:, tile(t)], start=True, stop=True)
                        last.then_inc(o_done, 1)
                        pe.wait_ge(o_copied, b + 1)
                        at_least(pe, x_done, b)
                        for t in range(G):
                            last = pe.matmul(y_ps[:, tile(t)], oT[:, tile(t)], T.WT[:, 7, :], start=True, stop=True)
                        last.then_inc(y_done, 1)
                steps(pe, step)

            @block.scalar
            def _(act):
                def step(g, v):
                    b = g - 1
                    if live(b):
                        act.wait_ge(nmax_ready, b + 1)
                        at_least(act, p_done, b)
                        at_least(act, inverted, b)
                        for t in range(G):
                            last = act.activation(probs[:, tile(t)], sm[:, tile(t)], ACT.Exp, bias=nmax[:, t:t + 1],
                                                  scale=SCALE, accum_out=total[:, t:t + 1])
                        last.then_inc(exped, 1)
                    if live(g):
                        act.wait_ge(xt_done, g + 1)
                        at_least(act, q_done, g)
                        act.copy(xnT[:, :], xt_ps[:, :]).then_inc(xt_copied, 1)
                        act.wait_ge(k_done, g + 1)
                        at_least(act, s_done, g - 1)
                        act.copy(kT[v][:, :], k_ps[:, :]).then_inc(k_ready, 1)
                    if live(b):
                        act.wait_ge(p_done, b + 1)
                        at_least(act, o_done, b)
                        act.copy(pT[:, :], p_ps[:, :]).then_inc(p_copied, 1)
                    if live(g):
                        act.wait_ge(q_done, g + 1)
                        act.activation(qT[v][:, :], q_ps[:, :], ACT.Identity, bias=T.bcol[:, 2:3]).then_inc(q_ready, 1)
                steps(act, step)

            @block.vector
            def _(dve):
                def norm(g, v):
                    ln.sums(dve, g, v)
                    at_least(dve, xt_done, g - 1)
                    ln.apply(dve, g, v)

                def step(g, v):
                    b = g - 1
                    if live(g):
                        norm(g, v)
                    if live(b):
                        dve.wait_ge(s_done, b + 1)
                        at_least(dve, exped, b)
                        s4 = sm[:, :].rearrange("p (t n) -> p t n", t=G)
                        dve.tensor_tensor(s4, s_ps[:, :].rearrange("p (t n) -> p t n", t=G),
                                          T.mask[:, :].unsqueeze(1).to_broadcast([P, G, P]), ALU.add).then_inc(masked, 1)
                        dve.wait_ge(masked, b + 1)
                        dve.tensor_reduce(peak[:, :], s4, AX_X, ALU.max).then_inc(peaked, 1)
                        dve.wait_ge(peaked, b + 1)
                        dve.tensor_scalar(nmax[:, :], peak[:, :], -SCALE, None, ALU.mult).then_inc(nmax_ready, 1)
                    if live(g):
                        dve.wait_ge(v_done, g + 1)
                        at_least(dve, o_done, g - 1)
                        dve.tensor_tensor(V[v][:, :].rearrange("p (t n) -> p t n", t=G),
                                          v_ps[:, :].rearrange("p (t n) -> p t n", t=G),
                                          T.bv1[:, :].unsqueeze(1).to_broadcast([P, G, P]), ALU.add).then_inc(v_ready, 1)
                    if live(b):
                        dve.wait_ge(exped, b + 1)
                        dve.reciprocal(inverse[:, :], total[:, :]).then_inc(inverted, 1)
                        dve.wait_ge(o_done, b + 1)
                        at_least(dve, y_done, b)
                        dve.tensor_copy(oT[:, :], o_ps[:, :]).then_inc(o_copied, 1)
                        dve.wait_ge(y_done, b + 1)
                        dve.wait_ge(biased, b + 1)
                        dve.wait_ge(inverted, b + 1)
                        for t in range(G):
                            x = flat2(T.X[:, ds(b * G + t, 1), :])
                            last = dve.scalar_tensor_tensor(x, y_ps[:, tile(t)], inverse[:, t:t + 1], x, ALU.mult, ALU.add)
                        last.then_inc(x_done, 1)
                steps(dve, step)


def route1(nc, I, T):
    with ExitStack() as ctx:
        a = Alloc(nc, ctx, "route1")
        sc = Scores(a, T, 1)
        PR = a.sb("PR", [P, TILES, E])
        peak, total = (a.sb(n, [P, TILES]) for n in ("peak", "total"))
        byexp = a.sb("byexp", [P, 4, SEQ])
        rest = a.sb("rest", [P, 4, SEQ])
        best = a.sb("best", [P, 4, CAP])
        where = a.sb("where", [P, 4, CAP], U32)
        where_f = a.sb("where_f", [P, 4, CAP])
        rows_i = a.sb("rows_i", [64, 1], I32)
        b2_i = a.sb("b2_i", [64, 1], I32)
        b2 = a.sb("b2", [64, 1])
        tile_i = a.sb("tile_i", [64, 16, E], I32)
        in4 = a.sb("in4", [64, 16, E])
        in_pair = a.sb("in_pair", [64, P], BF16)
        in_eight = a.sb("in_eight", [64, P])
        gain = a.sb("gain", [64, P])
        w1 = [a.sb(f"w1{v}", [P, F1]) for v in range(2)]
        w2 = [a.sb(f"w2{v}", [P, C1, P]) for v in range(2)]
        e_ps = a.ps("e_ps", [P, 2, P])
        i_ps = a.ps("i_ps", [64, P])
        v_ps = a.ps("v_ps", [64, P])
        w_in = [a.sem(f"w_in{v}") for v in range(2)]
        (shifted_ready, exp_ready, probs_ready, turned, step, found, back, cols_ready, sent, loaded, iotas, whigh, wlow,
         fenced) = (
            a.sem(n) for n in ("shifted_ready", "exp_ready", "probs_ready", "turned", "step", "found", "back",
                               "cols_ready", "sent", "loaded", "iotas", "whigh", "wlow", "fenced"))
        w1_d = I["L1_ffn_w1"]
        w2_d = I["L1_ffn_w2"].rearrange("e (c p) d -> e p c d", p=P)
        with nc.Block() as block:
            @block.sync
            def _(sp):
                for e in range(E):
                    at_least(sp, wlow, 2 * (e - 1))
                    at_least(sp, w_in[e % 2], 32 * (e // 2))
                    sp.dma_start(w1[e % 2][:, :], w1_d[e, :, :]).then_inc(w_in[e % 2], 16)
                    sp.dma_start(w2[e % 2][:, :, :], w2_d[e, :, :, :]).then_inc(w_in[e % 2], 16)
                sp.wait_ge(cols_ready, 1)
                for d, src in ((T.pair_dram, in_pair), (T.eight_dram, in_eight), (T.gain_dram, gain)):
                    to = d.rearrange("(q p b k e) -> q b k p e", q=2, p=16, b=2, k=CAP)
                    for q in range(2):
                        for b in range(2):
                            r = (q * 2 + b) * CAP
                            sp.dma_start(to[q, b, :, :, :], src[r:r + CAP, :].rearrange("k (p e) -> k p e", e=E))\
                                .then_inc(sent, 16)
                sp.wait_ge(sent, 12 * 16)
                sp.dma_start(T.pair_row[:, :], T.pair_dram.partition_broadcast(P)).then_inc(loaded, 16)
                for d, dst in ((T.eight_dram, T.eight_col), (T.gain_dram, T.gain_col)):
                    sp.dma_start(dst[:, :, :], d.rearrange("(g q e) -> q g e", q=P, e=E)).then_inc(loaded, 16)
                sp.wait_ge(loaded, 48)

            @block.gpsimd
            def _(pool):
                pool.iota(rows_i[:, :], pattern=[[0, 1]], base=0, channel_multiplier=1).then_inc(iotas, 1)
                pool.iota(tile_i[:, :, :], pattern=[[0, 4], [P, 4], [0, E]], base=0, channel_multiplier=0)\
                    .then_inc(iotas, 1)
                sc.pool(pool)
                for e in range(E):
                    pool.wait_ge(whigh, 2 * e + 2)
                    pool.tensor_tensor(T.W1[:, 1, e, :], w1[e % 2][:, :], T.W1[:, 0, e, :], ALU.subtract).then_inc(wlow, 1)
                    pool.tensor_tensor(T.W2[:, 1, e, :], flat2(w2[e % 2][:, :, :]), T.W2[:, 0, e, :], ALU.subtract)\
                        .then_inc(wlow, 1)

            @block.tensor
            def _(pe):
                sc.tensor(pe)
                pe.wait_ge(probs_ready, 1)
                for q in range(2):
                    last = pe.transpose(e_ps[:, q, :], PR[:, q * 16:(q + 1) * 16, :].rearrange("p t e -> p (t e)"),
                                        T.identF[:, :])
                last.then_inc(turned, 1)
                pe.wait_ge(found, 1)
                pe.transpose(i_ps[:, :], where_f[:, :, :].rearrange("p s k -> p (s k)"), T.identF[:, :])
                pe.transpose(v_ps[:, :], best[:, :, :].rearrange("p s k -> p (s k)"), T.identF[:, :]).then_inc(back, 1)

            @block.scalar
            def _(act):
                sc.scalar(act)
                act.wait_ge(shifted_ready, 1)
                act.activation(PR[:, :, :], sc.SC[:, :, :], ACT.Exp).then_inc(exp_ready, 1)
                for e in range(E):
                    act.wait_ge(w_in[e % 2], 32 * (e // 2 + 1))
                    act.copy(T.W1[:, 0, e, :], w1[e % 2][:, :]).then_inc(whigh, 1)
                    act.copy(T.W2[:, 0, e, :], flat2(w2[e % 2][:, :, :])).then_inc(whigh, 1)

            @block.vector
            def _(dve):
                chain = Chain(dve, step)
                sc.vector(dve)
                softmax_first(dve, chain, sc, sc.SC[:, :, :], peak[:, :], shifted_ready)
                softmax_last(dve, chain, PR[:, :, :], total[:, :], exp_ready)
                dve.sem_inc(probs_ready, 1)
                dve.wait_ge(turned, 1)
                chain(dve.tensor_copy(byexp[:, :, :].rearrange("p s t -> p (s t)"), e_ps[:, :, :].rearrange("p q t -> p (q t)")))
                for s in range(4):
                    chain(dve.max(best[:, s, 0:8], byexp[:, s, :]))
                    chain(dve.max_index(where[:, s, 0:8], best[:, s, 0:8], byexp[:, s, :]))
                    chain(dve.match_replace(rest[:, s, :], best[:, s, 0:8], byexp[:, s, :], -1.0))
                    chain(dve.max(best[:, s, 8:16], rest[:, s, :]))
                    chain(dve.max_index(where[:, s, 8:16], best[:, s, 8:16], rest[:, s, :]))
                chain(dve.tensor_copy(where_f[:, :, :], where[:, :, :]))
                dve.sem_inc(found, 1)
                dve.wait_ge(iotas, 2)
                chain(dve.tensor_scalar(b2_i[:, :], rows_i[:, :], CAP, None, ALU.bitwise_and))
                chain(dve.tensor_copy(b2[:, :], b2_i[:, :]))
                chain(dve.tensor_scalar(b2[:, :], b2[:, :], float(SEQ // CAP), None, ALU.mult))
                chain(dve.tensor_copy(in4[:, :, :], tile_i[:, :, :]))
                dve.wait_ge(back, 1)
                chain(dve.tensor_scalar(in_pair[:, :], i_ps[:, :], b2[:, 0:1], None, ALU.add))
                chain(dve.scalar_tensor_tensor(in_eight[:, :], i_ps[:, :], b2[:, 0:1],
                                               in4[:, :, :].rearrange("p t e -> p (t e)"), ALU.add, ALU.add))
                chain(dve.tensor_copy(gain[:, :], v_ps[:, :]))
                dve.sem_inc(cols_ready, 1)


def experts1(nc, I, T):
    with ExitStack() as ctx:
        a = Alloc(nc, ctx, "experts1")
        XG = [a.sb(f"XG{h}", [P, E, BATCH, CAP], BF16) for h in range(2)]
        Y = a.sb("Y", [P, 2, GROUPS, E, D], BF16)
        pick = [a.sb(f"pick{v}", [P, 2 * P], BF16) for v in range(2)]
        place = [a.sb(f"place{v}", [P, GT], BF16) for v in range(2)]
        hidden = [a.sb(f"hidden{v}", [P, GT]) for v in range(2)]
        hh = [a.sb(f"hh{v}", [P, 2, C1, GT], BF16) for v in range(2)]
        bank = [a.ps(f"bank{i}", [P, 512]) for i in range(8)]
        out_d = T.out.rearrange("b s d -> (b s) d").rearrange("(n p) d -> p n d", p=P)
        (picked, g_done, g_high, g_low) = (a.sem(n) for n in ("picked", "g_done", "g_high", "g_low"))
        (h_done, gelu_ready, high, low, y_done, y_high, y_low) = (
            a.sem(n) for n in ("h_done", "gelu_ready", "high", "low", "y_done", "y_high", "y_low"))
        placed, sum_done, x_done, stored = (a.sem(n) for n in ("placed", "sum_done", "x_done", "stored"))
        TERMS = ((0, 0), (0, 1), (1, 0))
        STEPS = 2 * E

        def flat3(ap):
            return ap.rearrange("p a b c -> p (a b c)")

        def live(s):
            return not isinstance(s, int) or 0 <= s < STEPS

        def steps(eng, step):
            for s in range(2):
                step(s, 0, s)
            with eng.Fori(1, E) as e:
                for j in range(2):
                    step(2 * e + j, e, j)
            step(STEPS, E, 0)

        with nc.Block() as block:
            @block.sync
            def _(sp):
                def body(g):
                    sp.wait_ge(x_done, g + 1)
                    sp.dma_start(out_d[:, ds(g * G, G), :], T.X[:, ds(g * G, G), :]).then_inc(stored, 16)
                rounds(sp, GROUPS, body)
                sp.wait_ge(stored, 16 * GROUPS)

            @block.tensor
            def _(pe):
                def gather(it):
                    for v in range(2):
                        p = 2 * it + v
                        pe.wait_ge(picked, p + 1)
                        at_least(pe, g_high, p - 1)
                        at_least(pe, g_low, p - 1)
                        for h in range(2):
                            last = pe.matmul(bank[2 * v + h][:, 0:2 * P], T.XHL[:, ds(p, 1), h, :].rearrange("p a d -> p (a d)"),
                                             pick[v][:, :], start=True, stop=True)
                        last.then_inc(g_done, 1)
                rounds(pe, TILES // 2, gather)

                def step(s, e, j):
                    if live(s):
                        if isinstance(s, int) and s == 0:
                            pe.wait_ge(g_high, TILES)
                            pe.wait_ge(g_low, TILES)
                        for c in range(C1):
                            at_least(pe, gelu_ready, 4 * (s - 1) + c + 1)
                            for n, (wh, xh) in enumerate(TERMS):
                                last = pe.matmul(bank[c][:, :],
                                                 flat2(T.W1[:, wh, ds(e, 1), c * P:(c + 1) * P]),
                                                 flat3(XG[xh][:, ds(e, 1), 32 * j:32 * j + 32, :]),
                                                 start=(n == 0), stop=(n == 2))
                            last.then_inc(h_done, 1)
                    if live(s - 1):
                        r, w = s - 1, 1 - j
                        ee = e if j else e - 1
                        pe.wait_ge(high, 4 * r + 4)
                        pe.wait_ge(low, 4 * r + 4)
                        at_least(pe, y_low, r - 1)
                        for m in range(4):
                            for c in range(C1):
                                for n, (wh, xh) in enumerate(TERMS):
                                    last = pe.matmul(bank[4 + w][:, m * P:(m + 1) * P], hh[w][:, xh, c, m * P:(m + 1) * P],
                                                     flat2(T.W2[:, wh, ds(ee, 1), c * P:(c + 1) * P]),
                                                     start=(c == 0 and n == 0), stop=(c == C1 - 1 and n == 2))
                        last.then_inc(y_done, 1)
                steps(pe, step)

                def scatter(g):
                    b = bank[6]
                    at_least(pe, x_done, g)
                    for e in range(E):
                        pe.wait_ge(placed, g * E + e + 1)
                        for t in range(G):
                            for h in range(2):
                                last = pe.matmul(b[:, t * P:(t + 1) * P], place[e % 2][:, t * P:(t + 1) * P],
                                                 flat2(Y[:, h, ds(g, 1), e, :]),
                                                 start=(e == 0 and t == 0 and h == 0), stop=(e == E - 1 and h == 1),
                                                 skip_group_check=True)
                        last.then_inc(sum_done, 1)
                pe.wait_ge(y_low, STEPS)
                rounds(pe, GROUPS, scatter)

            @block.scalar
            def _(act):
                def gather(it):
                    for v in range(2):
                        p = 2 * it + v
                        act.wait_ge(g_done, p + 1)
                        act.copy(XG[0][:, :, ds(2 * p, 2), :].rearrange("p e b k -> p b k e"),
                                 bank[2 * v][:, 0:2 * P].rearrange("p (b k e) -> p b k e", b=2, e=E)).then_inc(g_high, 1)
                rounds(act, TILES // 2, gather)

                def step(s, e, j):
                    if live(s):
                        for c in range(C1):
                            act.wait_ge(h_done, 4 * s + c + 1)
                            at_least(act, low, 4 * s + c - 1)
                            act.activation(hidden[c % 2][:, :], bank[c][:, :], ACT.Gelu).then_inc(gelu_ready, 1)
                            at_least(act, y_done, s - 1)
                            act.wait_ge(gelu_ready, 4 * s + c + 1)
                            act.copy(hh[j][:, 0, c, :], hidden[c % 2][:, :]).then_inc(high, 1)
                    if live(s - 1):
                        r, w = s - 1, 1 - j
                        ee = e if j else e - 1
                        act.wait_ge(y_done, r + 1)
                        for m in range(4):
                            last = act.activation(flat2(Y[:, 0, 4 * w + m, ds(ee, 1), :]),
                                                  bank[4 + w][:, m * P:(m + 1) * P], ACT.Identity,
                                                  scale=T.gain_col[:, 4 * w + m, ds(ee, 1)])
                        last.then_inc(y_high, 1)
                steps(act, step)

            @block.vector
            def _(dve):
                def gather(it):
                    for v in range(2):
                        p = 2 * it + v
                        at_least(dve, g_done, p - 1)
                        dve.tensor_scalar(pick[v][:, :], T.pair_row[:, ds(p * 2 * P, 2 * P)], T.iotaP[:, 0:1], None,
                                          ALU.is_equal).then_inc(picked, 1)
                        dve.wait_ge(g_done, p + 1)
                        dve.tensor_copy(XG[1][:, :, ds(2 * p, 2), :].rearrange("p e b k -> p b k e"),
                                        bank[2 * v + 1][:, 0:2 * P].rearrange("p (b k e) -> p b k e", b=2, e=E))\
                            .then_inc(g_low, 1)
                rounds(dve, TILES // 2, gather)

                def step(s, e, j):
                    if live(s):
                        for c in range(C1):
                            dve.wait_ge(high, 4 * s + c + 1)
                            dve.tensor_tensor(hh[j][:, 1, c, :], hidden[c % 2][:, :], hh[j][:, 0, c, :], ALU.subtract)\
                                .then_inc(low, 1)
                    if live(s - 1):
                        r, w = s - 1, 1 - j
                        ee = e if j else e - 1
                        dve.wait_ge(y_high, r + 1)
                        for m in range(4):
                            last = dve.scalar_tensor_tensor(flat2(Y[:, 1, 4 * w + m, ds(ee, 1), :]),
                                                            bank[4 + w][:, m * P:(m + 1) * P],
                                                            T.gain_col[:, 4 * w + m, ds(ee, 1)],
                                                            flat2(Y[:, 0, 4 * w + m, ds(ee, 1), :]),
                                                            ALU.mult, ALU.subtract)
                        last.then_inc(y_low, 1)
                steps(dve, step)

                def scatter(g):
                    for e in range(E):
                        at_least(dve, sum_done, g * E + e - 1)
                        dve.tensor_scalar(place[e % 2][:, :], T.iotaB[:, :], flat2(T.eight_col[:, ds(g, 1), e:e + 1]), None,
                                          ALU.is_equal).then_inc(placed, 1)
                    dve.wait_ge(sum_done, g * E + E)
                    x = T.X[:, ds(g * G, G), :]
                    dve.tensor_tensor(x, bank[6][:, :].rearrange("p (t d) -> p t d", t=G), x, ALU.add).then_inc(x_done, 1)
                rounds(dve, GROUPS, scatter)


def build(nc, I, out, stages):
    HELD.clear()
    with ExitStack() as ctx:
        a = Alloc(nc, ctx, "build")
        T = Tensors()
        T.X = a.sb("X", [P, TILES, D])
        T.ctxT = a.sb("ctxT", [P, NT])
        T.WT = a.sb("WT", [P, 8, P])
        T.gateT = a.sb("gateT", [P, 2, E])
        T.owns = a.sb("owns", [P, 2])
        T.row_i = a.sb("row_i", [P, 2], I32)
        T.bv0, T.bo0, T.bv1, T.bo1 = (a.sb(n, [P, D]) for n in ("bv0", "bo0", "bv1", "bo1"))
        T.gb0 = a.sb("gb0", [P, E])
        T.bcol = a.sb("bcol", [P, 3])
        T.identF = a.sb("identF", [P, P])
        T.identB = a.sb("identB", [P, P], BF16)
        T.before = a.sb("before", [P, P], BF16)
        T.ones = a.sb("ones", [P, P], BF16)
        T.half = a.sb("half", [P, 8])
        T.eps = a.sb("eps", [P, 8])
        T.mask = a.sb("mask", [P, P])
        T.iota_i = a.sb("iota_i", [P, 512], I32)
        T.iota_p = a.sb("iota_p", [P, 1], I32)
        T.iotaB = a.sb("iotaB", [P, 512])
        T.iotaP = a.sb("iotaP", [P, 1])
        T.q_dram = nc.dram_tensor("q_dram", [4, P, NT], BF16, kind="Internal").ap()
        T.k_dram = nc.dram_tensor("k_dram", [2, P, 2 * NT], BF16, kind="Internal").ap()
        T.xs_dram = nc.dram_tensor("xs_dram", [SLOT_TILES * ST, 2 * D], BF16, kind="Internal").ap()
        T.ys_dram = nc.dram_tensor("ys_dram", [SLOT_TILES * ST, D], F32, kind="Internal").ap()
        with ExitStack() as first:
            b = Alloc(nc, first, "layer0")
            T.WU = b.sb("WU", [P, 2, E, F0], BF16)
            T.WG = b.sb("WG", [P, 2, E, F0], BF16)
            T.WD = b.sb("WD", [R0, 2, E, C0 * P], BF16)
            T.Wrel = b.sb("Wrel", [QROWS, SEQ // 2, P], BF16)
            T.sel = b.sb("sel", [48, HP, 2, SEQ], BF16)
            T.XHL = b.sb("XHL", [P, TILES, 2, D], BF16)
            T.slot = b.sb("slot", [P, TOPK, TILES], I32)
            T.share = b.sb("share", [P, TOPK, TILES])
            T.owner = b.sb("owner", [P, SLOT_TILES], I32)
            T.db0 = b.sb("db0", [P, E, D])
            T.ub = b.sb("ub", [R0, E, C0])
            T.gb = b.sb("gb", [R0, E, C0])
            for stage in stages[0]:
                stage(nc, I, T)
        clear_semaphores(nc)
        T.W1 = a.sb("W1", [P, 2, E, F1], BF16)
        T.W2 = a.sb("W2", [P, 2, E, C1 * P], BF16)
        T.XHL = a.sb("XHL1", [P, TILES, 2, D], BF16)
        T.pair_row = a.sb("pair_row", [P, BATCH * CAP * E], BF16)
        T.eight_col = a.sb("eight_col", [P, GROUPS, E])
        T.gain_col = a.sb("gain_col", [P, GROUPS, E])
        T.pair_dram = nc.dram_tensor("pair_dram", [BATCH * CAP * E], BF16, kind="Internal").ap()
        T.eight_dram = nc.dram_tensor("eight_dram", [BATCH * CAP * E], F32, kind="Internal").ap()
        T.gain_dram = nc.dram_tensor("gain_dram", [BATCH * CAP * E], F32, kind="Internal").ap()
        T.out = out
        for stage in stages[1]:
            stage(nc, I, T)


STAGES = ((prepare, project0, attend0, route0, experts0, combine0),
          (attend1, route1, experts1))

_INS = ["x", "ctx_1024", "L0_xattn_Wq", "L0_xattn_bq", "L0_xattn_Wk", "L0_xattn_bk", "L0_xattn_Wv", "L0_xattn_bv",
        "L0_xattn_Wo", "L0_xattn_bo", "L0_xattn_w_rel", "L0_ffn_gate_w", "L0_ffn_gate_b", "L0_ffn_up_w",
        "L0_ffn_up_b", "L0_ffn_gp_w", "L0_ffn_gp_b", "L0_ffn_down_w", "L0_ffn_down_b", "L1_xattn_Wk",
        "L1_xattn_Wv", "L1_xattn_bv", "L1_xattn_Wq", "L1_xattn_bq", "L1_xattn_Wo", "L1_xattn_bo",
        "L1_ffn_gate_w", "L1_ffn_w1", "L1_ffn_w2"]


def kernel(**inputs):
    import numpy as _np
    import concourse.bacc as _bacc
    from concourse import mybir as _mybir
    from concourse.bass_utils import run_bass_kernel_spmd as _run

    nc = _bacc.Bacc("TRN2", target_bir_lowering=False, num_devices=1)
    arrays, args = {}, {}
    for name in _INS:
        a = _np.ascontiguousarray(inputs[name])
        arrays[f"in_{name}_dram"] = a
        args[name] = nc.dram_tensor(f"in_{name}_dram", a.shape, _mybir.dt.from_np(a.dtype), kind="ExternalInput").ap()
    out = nc.dram_tensor("out_0_dram", (BATCH, SEQ, D), _mybir.dt.float32, kind="ExternalOutput").ap()
    build(nc, args, out, STAGES)
    r = _run(nc, [arrays], core_ids=[0])
    return r.results[0]["out_0_dram"]
```

```python
from contextlib import ExitStack

import concourse.bass as bass
from concourse import mybir

F32 = mybir.dt.float32
BF16 = mybir.dt.bfloat16
I32 = mybir.dt.int32
U32 = mybir.dt.uint32
ALU = mybir.AluOpType
ACT = mybir.ActivationFunctionType
AX_X = mybir.AxisListType.X
ds = bass.ds

P = 128
BATCH, SEQ, D = 64, 64, 128
NT = BATCH * SEQ
TILES = NT // P
H, DK = 16, 8
HP = H // 2
E = 8
F0, C0 = 408, 4
R0 = F0 // C0
F1, C1 = 512, 4
R1 = F1 // C1
TOPK = 2
ST = 2 * P
SLOT_TILES = -(-(NT * TOPK + E * (ST - 1)) // ST)
CAP = 2 * SEQ // E
G = 4
GT = G * P
GROUPS = NT // GT
LN_EPS = 1e-5
NEG = -1e38
TERM_HIGH = (0, 1, 0)
TERM_W = (0, 0, 1)
QROWS = 2 * 3 * 16


class Tensors:
    pass


def at_least(eng, sem, value):
    if not (isinstance(value, int) and value <= 0):
        eng.wait_ge(sem, value)


def rounds(eng, count, body):
    body(0)
    with eng.Fori(1, count) as it:
        body(it)


def groups(eng, step, peeled, tail):
    for s in range(peeled):
        step(s, s % 2)
    with eng.Fori(peeled // 2, GROUPS // 2) as it:
        for v in range(2):
            step(it * 2 + v, v)
    for s in range(GROUPS, GROUPS + tail):
        step(s, s % 2)


def is_group(g):
    return not isinstance(g, int) or 0 <= g < GROUPS


def flat2(ap):
    return ap.rearrange("p a d -> p (a d)")


class Alloc:

    def __init__(self, nc, ctx, stage):
        self.nc, self.ctx, self.stage = nc, ctx, stage

    def sb(self, name, shape, dt=F32):
        return self.ctx.enter_context(self.nc.sbuf_tensor(f"{self.stage}_{name}", shape, dt))

    def ps(self, name, shape, dt=F32):
        return self.ctx.enter_context(self.nc.psum_tensor(f"{self.stage}_{name}", shape, dt))

    def sem(self, name):
        sem = self.nc.alloc_semaphore(f"{self.stage}_{name}")
        HELD.append(sem)
        return sem


HELD = []


def clear_semaphores(nc):
    nc.clear_and_free_semaphores(list(HELD))
    HELD.clear()
    nc.all_engine_barrier()


def windows(row):
    return bass.AP(tensor=row.tensor, offset=row.offset, ap=[row.ap[0], (2, SEQ // 2), (1, SEQ)])


def prepare(nc, I, T):
    with ExitStack() as ctx:
        a = Alloc(nc, ctx, "prepare")
        small = a.sb("small", [P, 8, P])
        gates = a.sb("gates", [E, 2, P])
        wrel = a.sb("wrel", [P, DK])
        wrel_t = T.wrel_t
        bv_t = a.sb("bv_t", [P, 2, P])
        ring = [a.ps(f"ring{i}", [P, 512]) for i in range(4)]
        fold = [a.ps(f"fold{i}", [P, 512]) for i in range(2)]
        small_in, rel_in, row_in = (a.sem(n) for n in ("small_in", "rel_in", "row_in"))
        ident_set, ident_ready, iotas, rel_zero = (
            a.sem(n) for n in ("ident_set", "ident_ready", "iotas", "rel_zero"))
        T.bias_in = a.sem("bias_in")
        T.rel_out = a.sem("rel_out")
        turned, high_done, low_done, owned, fold_turned, fold_copied, folded = (
            a.sem(n) for n in ("turned", "high_done", "low_done", "owned", "fold_turned", "fold_copied", "folded"))

        jobs = []
        for h in range(2):
            jobs.append((small_in, 160, [small[:, 4 * h + j, :] for j in range(4)], "small", h))
        jobs.append((small_in, 160, [gates[:, j, :] for j in range(2)], "gates", 0))
        jobs.append((rel_in, 16, [wrel[:, :]], "wrel", 0))

        def result(kind, bank, e, half):
            if kind == "small":
                return T.WT[:, 4 * e:4 * e + 4, :], bank[:, :].rearrange("p (j d) -> p j d", j=4)
            if kind == "gates":
                return T.gateT[:, :, :], bank[:, 0:2 * E].rearrange("p (j e) -> p j e", j=2)
            return wrel_t[:, half, :], bank[0:DK, 0:P]

        with nc.Block() as block:
            @block.sync
            def _(sp):
                sp.dma_start(wrel[:, :], I["L0_xattn_w_rel"][0:P, :]).then_inc(rel_in, 16)
                for j, n in enumerate(("L0_xattn_Wq", "L0_xattn_Wk", "L0_xattn_Wv", "L0_xattn_Wo",
                                       "L1_xattn_Wq", "L1_xattn_Wk", "L1_xattn_Wv", "L1_xattn_Wo")):
                    sp.dma_start(small[:, j, :], I[n]).then_inc(small_in, 16)
                sp.dma_start(gates[:, 0, :], I["L0_ffn_gate_w"]).then_inc(small_in, 16)
                sp.dma_start(gates[:, 1, :], I["L1_ffn_gate_w"]).then_inc(small_in, 16)
                sp.wait_ge(low_done, 1)
                sp.wait_ge(rel_zero, 1)
                for par in range(2):
                    for s in range(3):
                        for h2 in range(2):
                            row = par * 48 + s * 16 + h2 * DK
                            sp.dma_start(T.Wrel[row:row + DK, :, h2 * SEQ:(h2 + 1) * SEQ],
                                         windows(wrel_t[:, TERM_W[s], par:P])).then_inc(T.rel_out, 16)

            @block.gpsimd
            def _(pool):
                pool.memset(T.identF[:, :], 0.0).then_inc(ident_set, 1)
                pool.memset(T.identB[:, :], 0.0).then_inc(ident_set, 1)
                pool.memset(T.sel[:, :, :, :], 0.0).then_inc(ident_set, 1)
                pool.memset(T.before[:, :], 0.0).then_inc(ident_set, 1)
                pool.wait_ge(ident_set, 4)
                for m in (T.identF, T.identB):
                    pool.affine_select(out=m[:, :], in_=m[:, :], compare_op=ALU.not_equal, fill=1.0, base=0,
                                       pattern=[[-1, P]], channel_multiplier=1).then_inc(ident_ready, 1)
                pool.affine_select(out=T.before[:, :], in_=T.before[:, :], compare_op=ALU.is_ge, fill=1.0, base=0,
                                   pattern=[[-1, P]], channel_multiplier=1).then_inc(ident_ready, 1)
                for base in (0, -32):
                    pool.affine_select(out=T.sel[:, :, :, :], in_=T.sel[:, :, :, :], compare_op=ALU.not_equal,
                                       fill=1.0, base=base, pattern=[[-2, HP], [-1, 2], [0, SEQ]],
                                       channel_multiplier=1).then_inc(ident_ready, 1)
                    pool.wait_ge(ident_ready, 4 if base == 0 else 5)
                pool.iota(T.row_i[:, :], pattern=[[0, 2]], base=0, channel_multiplier=1).then_inc(iotas, 1)
                pool.iota(T.iota_i[:, :], pattern=[[1, 512]], base=0, channel_multiplier=0).then_inc(iotas, 1)
                pool.iota(T.iota_p[:, :], pattern=[[0, 1]], base=0, channel_multiplier=1).then_inc(iotas, 1)
                pool.dma_start(T.gb0[:, :], I["L0_ffn_gate_b"].partition_broadcast(P)).then_inc(T.bias_in, 16)
                pool.dma_start(T.db0[:, :, :], I["L0_ffn_down_b"].partition_broadcast(P)).then_inc(T.bias_in, 16)
                for out, n in ((T.ub, "L0_ffn_up_b"), (T.gb, "L0_ffn_gp_b")):
                    for c in range(C0):
                        pool.dma_start(out[:, :, c], I[n][:, c * R0:(c + 1) * R0].rearrange("e r -> r e"),
                                       allow_slow_non_contiguous=True).then_inc(T.bias_in, 16)

            @block.tensor
            def _(pe):
                pe.wait_ge(ident_ready, 2)
                for n, (load, count, sources, kind, e) in enumerate(jobs):
                    pe.wait_ge(load, count)
                    for j, src in enumerate(sources):
                        k, m = src.shape
                        w = E if kind == "gates" else P
                        last = pe.transpose(ring[n % 4][0:m, j * w:j * w + k], src, T.identF[0:k, 0:k])
                    last.then_inc(turned, 1)
                pe.wait_ge(row_in, 16 * 7)
                for n, (bv, w) in enumerate(((T.bv0, 3), (T.bv1, 7))):
                    pe.transpose(fold[n][:, 0:P], bv[:, :], T.identF[:, :]).then_inc(fold_turned, 1)
                    pe.wait_ge(fold_copied, n + 1)
                    pe.matmul(fold[n][:, P:2 * P], bv_t[:, n, :], T.WT[:, w, :], start=True, stop=True).then_inc(folded, 1)

            @block.scalar
            def _(act):
                for out, name in ((T.bv0, "L0_xattn_bv"), (T.bo0, "L0_xattn_bo"), (T.bv1, "L1_xattn_bv"),
                                  (T.bo1, "L1_xattn_bo")):
                    act.dma_start(out[:, :], I[name].partition_broadcast(P)).then_inc(row_in, 16)
                for j, n in enumerate(("L0_xattn_bq", "L0_xattn_bk", "L1_xattn_bq")):
                    act.dma_start(T.bcol[:, j:j + 1], I[n].rearrange("(p a) -> p a", a=1)).then_inc(row_in, 16)
                for n, (_, _, _, kind, e) in enumerate(jobs):
                    act.wait_ge(turned, n + 1)
                    out, src = result(kind, ring[n % 4], e, 0)
                    act.copy(out, src).then_inc(high_done, 1)

            @block.vector
            def _(dve):
                dve.memset(T.Wrel[:, :, :], 0.0).then_inc(rel_zero, 1)
                dve.memset(T.ones[:, :], 1.0)
                dve.memset(T.half[:, :], -0.5).then_inc(owned, 1)
                dve.wait_ge(owned, 1)
                dve.memset(T.eps[:, :], LN_EPS)
                for a0, b0 in ((0, 0), (0, 64), (64, 0), (64, 64)):
                    dve.memset(T.mask[a0:a0 + 64, b0:b0 + 64], 0.0 if a0 == b0 else NEG)
                for n, (_, _, _, kind, e) in enumerate(jobs):
                    if kind in ("small", "gates"):
                        continue
                    dve.wait_ge(high_done, n + 1)
                    out, src = result(kind, ring[n % 4], e, 1)
                    high, _ = result(kind, ring[n % 4], e, 0)
                    dve.tensor_tensor(out, src, high, ALU.subtract).then_inc(low_done, 1)
                dve.wait_ge(iotas, 3)
                dve.tensor_scalar(T.row_i[:, :], T.row_i[:, :], DK, None, ALU.bitwise_and).then_inc(owned, 1)
                dve.wait_ge(owned, 2)
                dve.tensor_scalar(T.owns[:, 0:1], T.row_i[:, 0:1], 0.0, None, ALU.is_equal)
                dve.tensor_scalar(T.owns[:, 1:2], T.row_i[:, 1:2], 0.0, None, ALU.is_gt)
                dve.tensor_copy(T.iotaB[:, :], T.iota_i[:, :])
                dve.tensor_copy(T.iotaP[:, :], T.iota_p[:, :])
                for n, bo in enumerate((T.bo0, T.bo1)):
                    dve.wait_ge(fold_turned, n + 1)
                    dve.tensor_copy(bv_t[:, n, :], fold[n][:, 0:P]).then_inc(fold_copied, 1)
                    dve.wait_ge(folded, n + 1)
                    dve.tensor_tensor(bo[:, :], bo[:, :], fold[n][:, P:2 * P], ALU.add)


class Norm:

    def __init__(self, a, T, name="ln"):
        self.T = T
        self.scratch = a.sb(f"{name}_scratch", [P, 1])
        self.stats = [a.sb(f"{name}_stats{v}", [P, G, 6]) for v in range(2)]
        self.mv = [a.sb(f"{name}_mv{v}", [P, G, 2]) for v in range(2)]
        self.var = [a.sb(f"{name}_var{v}", [P, G]) for v in range(2)]
        self.rstd = [a.sb(f"{name}_rstd{v}", [P, G]) for v in range(2)]
        self.xn = [a.sb(f"{name}_xn{v}", [P, G, D]) for v in range(2)]
        self.summed, self.mv_ready, self.var_ready, self.rstd_ready, self.xn_ready = (
            a.sem(f"{name}_{n}") for n in ("summed", "mv_ready", "var_ready", "rstd_ready", "xn_ready"))

    def sums(self, dve, g, v):
        for t in range(G):
            last = dve.bn_stats(self.stats[v][:, t, :], flat2(self.T.X[:, ds(g * G + t, 1), :]))
        last.then_inc(self.summed, 1)
        dve.wait_ge(self.summed, g + 1)
        dve.tensor_copy(self.scratch[:, 0:1], self.stats[v][:, G - 1, 0:1])
        for t in range(G):
            last = dve.bn_aggr(self.mv[v][:, t, :], self.stats[v][:, t, :])
        last.then_inc(self.mv_ready, 1)

    def root(self, pool, g, v):
        pool.wait_ge(self.mv_ready, g + 1)
        pool.tensor_tensor(self.var[v][:, :], self.mv[v][:, :, 1], self.T.eps[:, 0:G], ALU.add)\
            .then_inc(self.var_ready, 1)
        pool.wait_ge(self.var_ready, g + 1)
        pool.tensor_tensor(self.rstd[v][:, :], self.var[v][:, :], self.T.half[:, 0:G], ALU.pow)\
            .then_inc(self.rstd_ready, 1)

    def apply(self, dve, g, v):
        dve.wait_ge(self.rstd_ready, g + 1)
        for t in range(G):
            last = dve.tensor_scalar(self.xn[v][:, t, :], flat2(self.T.X[:, ds(g * G + t, 1), :]),
                                     self.mv[v][:, t, 0:1], self.rstd[v][:, t:t + 1], ALU.subtract, ALU.mult)
        last.then_inc(self.xn_ready, 1)


LOADS = 6 + 6


def load_planes(sp, T, g, v):
    for par in range(2):
        for s in range(3):
            row = par * 48 + s * 16
            sp.dma_start(T.Q[v][row:row + 16, :, :],
                         T.q_dram[2 * TERM_HIGH[s] + par, :, ds(g * GT, GT)]
                         .rearrange("(hp r) t -> r hp t", r=16)).then_inc(T.planes_in[v], 16)
            sp.dma_start(T.K[v][row:row + 16, :, :],
                         T.k_dram[TERM_W[s], :, ds(g * 2 * GT, 2 * GT)]
                         .rearrange("(hp r) t -> r hp t", r=16)).then_inc(T.planes_in[v], 16)


def project0(nc, I, T):
    with ExitStack() as ctx:
        a = Alloc(nc, ctx, "project0")
        ln = Norm(a, T)
        cx = [a.sb(f"cx{v}", [P, G, D]) for v in range(2)]
        xnT = [a.sb(f"xnT{v}", [P, GT]) for v in range(2)]
        q_split = [a.sb(f"q_split{v}", [P, 4, GT], BF16) for v in range(2)]
        k_full = [a.sb(f"k_full{v}", [P, GT]) for v in range(2)]
        k_split = [a.sb(f"k_split{v}", [P, 2, 2 * G, 2, SEQ], BF16) for v in range(2)]
        xt_ps = [a.ps(f"xt_ps{v}", [P, GT]) for v in range(2)]
        ct_ps = [a.ps(f"ct_ps{v}", [P, GT]) for v in range(2)]
        q_ps = [a.ps(f"q_ps{v}", [P, GT]) for v in range(2)]
        k_ps = [a.ps(f"k_ps{v}", [P, GT]) for v in range(2)]
        x_in = [a.sem(f"x_in{v}") for v in range(2)]
        c_in = [a.sem(f"c_in{v}") for v in range(2)]
        planes_out = [a.sem(f"planes_out{v}") for v in range(2)]
        T.planes_in = [a.sem(f"planes_in{v}") for v in range(2)]
        zeroed, xt_done, ct_done, xt_copied, ct_copied, q_done, k_done, q_high, k_high, low, biased = (
            a.sem(n) for n in ("zeroed", "xt_done", "ct_done", "xt_copied", "ct_copied", "q_done", "k_done",
                               "q_high", "k_high", "low", "biased"))
        k_copied = a.sem("k_copied")
        x_d = I["x"].rearrange("b s d -> (b s) d").rearrange("(n p) d -> p n d", p=P)
        c_d = I["ctx_1024"].rearrange("b s d -> (b s) d").rearrange("(n p) d -> p n d", p=P)

        with nc.Block() as block:
            @block.sync
            def _(sp):
                def step(s, v):
                    if is_group(s):
                        at_least(sp, ct_done, s - 1)
                        sp.dma_start(T.X[:, ds(s * G, G), :], x_d[:, ds(s * G, G), :]).then_inc(x_in[v], 16)
                        sp.dma_start(cx[v][:, :, :], c_d[:, ds(s * G, G), :]).then_inc(c_in[v], 16)
                    if is_group(s - 3):
                        g, w = s - 3, 1 - v
                        sp.wait_ge(low, g + 1)
                        sp.dma_start(T.q_dram[:, :, ds(g * GT, GT)].rearrange("n p t -> p n t"), q_split[w][:, :, :])\
                            .then_inc(planes_out[w], 16)
                        sp.dma_start(T.k_dram[:, :, ds(g * 2 * GT, 2 * GT)].rearrange("n p t -> p n t"),
                                     k_split[w][:, :, :, :, :].rearrange("p n b h j -> p n (b h j)"))\
                            .then_inc(planes_out[w], 16)
                for s in range(4):
                    step(s, s % 2)
                with sp.Fori(2, GROUPS // 2) as it:
                    for v in range(2):
                        step(it * 2 + v, v)
                sp.wait_ge(planes_out[0], 32)
                load_planes(sp, T, 0, 0)
                for s in range(GROUPS, GROUPS + 3):
                    step(s, s % 2)
                for v in range(2):
                    sp.wait_ge(planes_out[v], 16 * GROUPS)

            @block.gpsimd
            def _(pool):
                for v in range(2):
                    pool.memset(q_split[v][:, :, :], 0.0).then_inc(zeroed, 1)

                def body(it):
                    for v in range(2):
                        g = 2 * it + v
                        ln.root(pool, g, v)
                        pool.wait_ge(ln.xn_ready, g + 1)
                        pool.tensor_tensor(T.X[:, ds(g * G, G), :], T.X[:, ds(g * G, G), :],
                                           T.bo0[:, :].unsqueeze(1).to_broadcast([P, G, D]), ALU.add).then_inc(biased, 1)
                rounds(pool, GROUPS // 2, body)

            @block.vector
            def _(dve):
                dve.wait_ge(zeroed, 2)

                def step(s, v):
                    if is_group(s - 1):
                        at_least(dve, xt_done, s - 2)
                        ln.apply(dve, s - 1, 1 - v)
                    if is_group(s):
                        dve.wait_ge(x_in[v], (s - v) * 8 + 16)
                        ln.sums(dve, s, v)
                    if is_group(s - 2):
                        g = s - 2
                        dve.wait_ge(q_high, 2 * g + 2)
                        at_least(dve, planes_out[v], 16 * (g - v))
                        for par in range(2):
                            dve.scalar_tensor_tensor(q_split[v][:, 2 + par, par::2], q_ps[v][:, par::2], T.bcol[:, 0:1],
                                                     q_split[v][:, par, par::2], ALU.add, ALU.subtract)
                        dve.wait_ge(k_high, 2 * g + 2)
                        for h2 in range(2):
                            last = dve.scalar_tensor_tensor(
                                k_split[v][:, 1, :, h2, :], k_full[v][:, :].rearrange("p (b j) -> p b j", j=SEQ),
                                T.owns[:, h2:h2 + 1], k_split[v][:, 0, :, h2, :], ALU.mult, ALU.subtract)
                        last.then_inc(low, 1)
                groups(dve, step, 4, 2)

            @block.tensor
            def _(pe):
                def step(s, v):
                    if is_group(s):
                        pe.wait_ge(c_in[v], (s - v) * 8 + 16)
                        at_least(pe, ct_copied, s - 1)
                        for t in range(G):
                            last = pe.transpose(ct_ps[v][:, t * P:(t + 1) * P], cx[v][:, t, :], T.identF[:, :])
                        last.then_inc(ct_done, 1)
                    if is_group(s - 1):
                        g, w = s - 1, 1 - v
                        pe.wait_ge(ln.xn_ready, g + 1)
                        at_least(pe, xt_copied, g - 1)
                        for t in range(G):
                            last = pe.transpose(xt_ps[w][:, t * P:(t + 1) * P], ln.xn[w][:, t, :], T.identF[:, :])
                        last.then_inc(xt_done, 1)
                        at_least(pe, low, g - 1)
                        pe.wait_ge(ct_copied, g + 1)
                        pe.matmul(k_ps[w][:, :], T.WT[:, 1, :], T.ctxT[:, ds(g * GT, GT)], start=True, stop=True)\
                            .then_inc(k_done, 1)
                        pe.wait_ge(xt_copied, g + 1)
                        pe.matmul(q_ps[w][:, :], T.WT[:, 0, :], xnT[w][:, :], start=True, stop=True).then_inc(q_done, 1)
                groups(pe, step, 4, 1)

            @block.scalar
            def _(act):
                act.wait_ge(zeroed, 2)

                def step(s, v):
                    if is_group(s):
                        act.wait_ge(ct_done, s + 1)
                        act.copy(T.ctxT[:, ds(s * GT, GT)], ct_ps[v][:, :]).then_inc(ct_copied, 1)
                    if is_group(s - 1):
                        g, w = s - 1, 1 - v
                        act.wait_ge(xt_done, g + 1)
                        at_least(act, q_done, g - 1)
                        act.copy(xnT[w][:, :], xt_ps[w][:, :]).then_inc(xt_copied, 1)
                        act.wait_ge(k_done, g + 1)
                        at_least(act, low, g - 1)
                        act.activation(k_full[w][:, :], k_ps[w][:, :], ACT.Identity, bias=T.bcol[:, 1:2])\
                            .then_inc(k_copied, 1)
                        act.wait_ge(k_copied, g + 1)
                        at_least(act, planes_out[w], 16 * (g - w))
                        for h2 in range(2):
                            act.activation(k_split[w][:, 0, :, h2, :],
                                           k_full[w][:, :].rearrange("p (b j) -> p b j", j=SEQ),
                                           ACT.Identity, scale=T.owns[:, h2:h2 + 1]).then_inc(k_high, 1)
                        act.wait_ge(q_done, g + 1)
                        for par in range(2):
                            act.activation(q_split[w][:, par, par::2], q_ps[w][:, par::2], ACT.Identity,
                                           bias=T.bcol[:, 0:1]).then_inc(q_high, 1)
                groups(act, step, 4, 1)


def attend0(nc, I, T):
    with ExitStack() as ctx:
        a = Alloc(nc, ctx, "attend0")
        Q, K, planes_in = T.Q, T.K, T.planes_in
        cg = [a.sb(f"cg{v}", [P, 2, 2, SEQ]) for v in range(2)]
        scores = [a.sb(f"scores{v}", [P, HP * P]) for v in range(2)]
        probs = a.sb("probs", [P, 2, 512])
        split = [a.sb(f"split{v}", [P, 2, HP * P], BF16) for v in range(2)]
        V = [a.sb(f"V{v}", [P, 2, HP, 2, 2, DK + 1], BF16) for v in range(2)]
        maxes = a.sb("maxes", [P, P])
        shift = a.sb("shift", [48, P], BF16)
        rsum = a.sb("rsum", [P, HP, 2])
        heads = a.sb("heads", [P, HP, 2, DK])
        headsT = a.sb("headsT", [P, P])
        st = [a.ps(f"st{v}", [P, 2, 512]) for v in range(2)]
        turned_ps = a.ps("turned_ps", [P, 2, 512])
        v_ps = a.ps("v_ps", [P, 512])
        outp = a.ps("outp", [P, 512])
        mt_ps, o_ps, ht_ps, y_ps = turned_ps[:, 0, 0:P], outp[:, 0:HP * 36], outp[:, 384:512], outp[:, 384:512]
        (set0, cg_ready, st_ready, copied, turned, maxed, m_copied, mt_ready, hi_set, shift_ready, shifted,
         exped, probs_low, v_done, v_high, v_ready, pv_done, recip, heads_ready, ht_done, ht_copied, y_done, x_done) = (
            a.sem(n) for n in ("set0", "cg_ready", "st_ready", "copied", "turned", "maxed", "m_copied", "mt_ready",
                               "hi_set", "shift_ready", "shifted", "exped", "probs_low", "v_done", "v_high", "v_ready", "pv_done", "recip",
                               "heads_ready", "ht_done", "ht_copied", "y_done", "x_done"))
        BEFORE = 3 * SEQ // 8
        PAIRS = 2 * G

        def steps(eng, step):
            for u in range(PAIRS):
                step(u, u)
            with eng.Fori(1, TILES // PAIRS) as it:
                for u in range(PAIRS):
                    step(it * PAIRS + u, u)
            for u in range(3):
                step(TILES + u, u)

        def live(p):
            return not isinstance(p, int) or 0 <= p < TILES

        def value(w, half, h2):
            return V[w][64 * h2:64 * h2 + 64, half, :, :, h2, 0:DK].rearrange("p hp b d -> p b hp d")

        def made(h2):
            return v_ps[64 * h2:64 * h2 + 64, 0:2 * P]\
                .rearrange("p (b hp h d) -> p b hp h d", b=2, hp=HP, h=2)[:, :, :, h2, :]

        def half(ap, bank):
            return ap[..., bank * SEQ // 2:(bank + 1) * SEQ // 2]

        def by_half(row, bank):
            return half(row.rearrange("p (n i) -> p n i", i=SEQ), bank)

        def by_bank(row):
            return row.rearrange("p (n i) -> p n i", i=SEQ // 2)

        with nc.Block() as block:
            @block.sync
            def _(sp):
                def load(it):
                    for v in range(2):
                        g = 2 * it + v
                        at_least(sp, st_ready, 2 * G * (g - 1))
                        if not isinstance(g, int) or g > 0:
                            load_planes(sp, T, g, v)
                rounds(sp, GROUPS // 2, load)

            @block.gpsimd
            def _(pool):
                for v in range(2):
                    pool.memset(V[v][:, :, :, :, :, :], 0.0).then_inc(set0, 1)
                pool.memset(maxes[:, :], 0.0).then_inc(set0, 1)
                pool.wait_ge(set0, 3)
                for v in range(2):
                    pool.memset(V[v][0:64, 0, :, :, 0, DK:DK + 1], 1.0).then_inc(set0, 1)
                    pool.memset(V[v][64:P, 0, :, :, 1, DK:DK + 1], 1.0).then_inc(set0, 1)
                pool.wait_ge(set0, 7)

                def step(p, u):
                    if live(p):
                        at_least(pool, v_done, p - 1)
                        pool.tensor_copy(cg[u % 2][:, :, :, :],
                                         T.ctxT[:, ds(p * P, P)].rearrange("p (b t) -> p b t", t=SEQ).unsqueeze(2)
                                         .to_broadcast([P, 2, 2, SEQ])).then_inc(cg_ready, 1)
                    if live(p - 2):
                        q, w = p - 2, u % 2
                        for bank in range(2):
                            pool.wait_ge(exped, 2 * q + 1 + bank)
                            at_least(pool, pv_done, q - 1)
                            pool.tensor_tensor(by_half(split[w][:, 1, :], bank), by_bank(probs[:, bank, :]),
                                               by_half(split[w][:, 0, :], bank), ALU.subtract).then_inc(probs_low, 1)
                steps(pool, step)

            @block.tensor
            def _(pe):
                pe.wait_ge(T.rel_out, 12 * 16)

                def by_pair(u, bank):
                    return st[u % 2][:, bank, :].rearrange("p (h b i) -> p h b i", h=HP, b=2)

                def keys(p, u, bank):
                    v = (u // G) % 2
                    at_least(pe, exped, 2 * p - 3 + bank)
                    if bank == 0 and u % G == 0:
                        pe.wait_ge(planes_in[v], (p - u) * 2 * LOADS + 16 * LOADS)
                    for hp in range(HP):
                        for b in range(2):
                            t = (u % G) * P + b * SEQ
                            i = t + bank * SEQ // 2
                            pe.matmul(by_pair(u, bank)[:, hp, b, :], K[v][:, hp, 2 * t:2 * t + P],
                                      Q[v][:, hp, i:i + SEQ // 2],
                                      start=(hp == 0 and b == 0), stop=False, skip_group_check=True)

                def positions(u, bank, first, end):
                    t = (u % G) * P
                    q4 = half(Q[(u // G) % 2][:, :, t:t + P].rearrange("r h (b i) -> r h b i", b=2), bank)
                    for i in range(first, end, 2):
                        last = pe.matmul(by_pair(u, bank)[:, :, :, i:i + 2], T.Wrel[:, (bank * SEQ // 2 + i) // 2, :],
                                         q4[:, :, :, i:i + 2],
                                         start=False, stop=(i == SEQ // 2 - 2), skip_group_check=True)
                    if end == SEQ // 2:
                        last.then_inc(st_ready, 1)

                def turn(p, u):
                    w = u % 2
                    at_least(pe, shift_ready, p)
                    pe.wait_ge(copied, 2 * p + 2)
                    for bank in range(2):
                        for h in range(4):
                            c = (bank * 4 + h) * P
                            last = pe.transpose(turned_ps[:, bank, h * P:(h + 1) * P], scores[w][:, c:c + P],
                                                T.identF[:, :])
                        last.then_inc(turned, 1)

                def subtract_max(p, u):
                    w = u % 2
                    pe.wait_ge(shift_ready, p + 1)
                    for bank in range(2):
                        for hp in range(HP):
                            last = pe.matmul(st[w][:, bank, hp * SEQ:(hp + 1) * SEQ].rearrange("p (b i) -> p b i", b=2),
                                             T.sel[:, hp, :, :],
                                             half(shift[:, :].rearrange("p (b i) -> p b i", b=2), bank),
                                             start=False, stop=True, skip_group_check=True)
                    last.then_inc(shifted, 1)

                def weigh(p, u):
                    w = u % 2
                    pe.wait_ge(probs_low, 2 * p + 2)
                    pe.wait_ge(v_ready, 2 * p + 2)
                    at_least(pe, x_done, p)
                    for hp in range(HP):
                        for n, (ph, vh) in enumerate(((0, 0), (0, 1), (1, 0))):
                            last = pe.matmul(o_ps[:, hp * 36:hp * 36 + 36], split[w][:, ph, hp * P:(hp + 1) * P],
                                             V[w][:, vh, hp, :, :, :].rearrange("p b h d -> p (b h d)"),
                                             start=(n == 0), stop=(n == 2))
                    last.then_inc(pv_done, 1)

                def values(p, u):
                    pe.wait_ge(cg_ready, p + 1)
                    at_least(pe, v_ready, 2 * p)
                    for b in range(2):
                        last = pe.matmul(v_ps[:, b * P:(b + 1) * P],
                                         cg[u % 2][:, b, :, :], T.WT[:, 2, :], start=True, stop=True)
                    last.then_inc(v_done, 1)

                def step(p, u):
                    u1, u2 = (u - 1) % PAIRS, (u - 2) % PAIRS
                    if live(p - 1):
                        turn(p - 1, u1)
                    if live(p):
                        keys(p, u, 0)
                        positions(u, 0, 0, SEQ // 2)
                    if live(p - 3):
                        q = p - 3
                        pe.wait_ge(heads_ready, 2 * q + 2)
                        pe.transpose(ht_ps, heads[:, :, :, :].rearrange("p a b d -> p (a b d)"), T.identF[:, :])\
                            .then_inc(ht_done, 1)
                    if live(p):
                        keys(p, u, 1)
                        positions(u, 1, 0, BEFORE)
                    if live(p - 1):
                        pe.wait_ge(m_copied, p)
                        pe.transpose(mt_ps, maxes[:, :], T.identF[:, :]).then_inc(mt_ready, 1)
                    if live(p):
                        positions(u, 1, BEFORE, SEQ // 2)
                    if live(p - 3):
                        pe.wait_ge(ht_copied, p - 2)
                        pe.matmul(y_ps, headsT[:, :], T.WT[:, 3, :], start=True, stop=True).then_inc(y_done, 1)
                    if live(p):
                        values(p, u)
                    if live(p - 1):
                        subtract_max(p - 1, u1)
                    if live(p - 2):
                        weigh(p - 2, u2)
                steps(pe, step)

            @block.scalar
            def _(act):
                act.wait_ge(set0, 7)

                def step(p, u):
                    if live(p - 1):
                        q, w = p - 1, (u - 1) % 2
                        act.wait_ge(v_done, q + 1)
                        at_least(act, pv_done, q - 1)
                        for h2 in range(2):
                            act.copy(value(w, 0, h2), made(h2)).then_inc(v_high, 1)
                    if live(p - 3):
                        act.wait_ge(ht_done, p - 2)
                        at_least(act, y_done, p - 3)
                        act.copy(headsT[:, :], ht_ps).then_inc(ht_copied, 1)
                    if live(p):
                        at_least(act, turned, 2 * (p - 1))
                        for bank in range(2):
                            act.wait_ge(st_ready, 2 * p + 1 + bank)
                            act.copy(by_half(scores[u % 2][:, :], bank), by_bank(st[u % 2][:, bank, :]))\
                                .then_inc(copied, 1)
                    if live(p - 1):
                        q, w = p - 1, (u - 1) % 2
                        act.wait_ge(shifted, q + 1)
                        for bank in range(2):
                            at_least(act, pv_done, q - 1)
                            act.activation(by_half(split[w][:, 0, :], bank), by_bank(st[w][:, bank, :]),
                                           ACT.Exp, scale=DK ** -0.5)
                            at_least(act, probs_low, 2 * q - 1 + bank)
                            act.activation(probs[:, bank, :], st[w][:, bank, :], ACT.Exp, scale=DK ** -0.5)\
                                .then_inc(exped, 1)
                steps(act, step)

            @block.vector
            def _(dve):
                dve.wait_ge(set0, 7)

                def step(p, u):
                    if live(p - 1):
                        q = p - 1
                        at_least(dve, mt_ready, q)
                        for bank in range(2):
                            dve.wait_ge(turned, 2 * q + 1 + bank)
                            dve.tensor_reduce(maxes[:, bank * 8:bank * 8 + 8],
                                              turned_ps[:, bank, :].rearrange("p (h j) -> p h j", j=SEQ),
                                              AX_X, ALU.max).then_inc(maxed, 1)
                        dve.wait_ge(maxed, 2 * q + 2)
                        dve.tensor_copy(maxes[:, 32:48], maxes[:, 0:16]).then_inc(m_copied, 1)
                    if live(p - 1):
                        q, w = p - 1, (u - 1) % 2
                        dve.wait_ge(v_high, 2 * q + 2)
                        at_least(dve, pv_done, q - 1)
                        for h2 in range(2):
                            dve.tensor_tensor(value(w, 1, h2), made(h2), value(w, 0, h2), ALU.subtract).then_inc(v_ready, 1)
                    if live(p - 1):
                        q = p - 1
                        dve.wait_ge(mt_ready, q + 1)
                        at_least(dve, shifted, q)
                        dve.tensor_scalar(shift[:, :], mt_ps[0:48, :], -1.0, None, ALU.mult).then_inc(hi_set, 1)
                        dve.wait_ge(hi_set, q + 1)
                        dve.scalar_tensor_tensor(shift[32:48, :], mt_ps[32:48, :], -1.0, shift[32:48, :],
                                                 ALU.mult, ALU.subtract).then_inc(shift_ready, 1)
                    if live(p - 3):
                        q = p - 3
                        dve.wait_ge(y_done, q + 1)
                        x = flat2(T.X[:, ds(q, 1), :])
                        dve.tensor_tensor(x, y_ps, x, ALU.add).then_inc(x_done, 1)
                    if live(p - 2):
                        q = p - 2
                        dve.wait_ge(pv_done, q + 1)
                        at_least(dve, ht_done, q)
                        o = o_ps.rearrange("p (hp b h d) -> p hp b h d", hp=HP, b=2, h=2)
                        for b in range(2):
                            rows = slice(64 * b, 64 * b + 64)
                            dve.reciprocal(rsum[rows, :, :], o[rows, :, b, :, DK]).then_inc(recip, 1)
                        for b in range(2):
                            rows = slice(64 * b, 64 * b + 64)
                            dve.wait_ge(recip, 2 * q + 1 + b)
                            dve.tensor_tensor(heads[rows, :, :, :], o[rows, :, b, :, 0:DK],
                                              rsum[rows, :, :].unsqueeze(3).to_broadcast([64, HP, 2, DK]), ALU.mult)\
                                .then_inc(heads_ready, 1)
                steps(dve, step)


class Scores:

    def __init__(self, a, T, gate):
        self.T, self.gate = T, gate
        self.ln = Norm(a, T)
        self.SC = a.sb("SC", [P, TILES, E])
        self.xnT = [a.sb(f"xnT{v}", [P, GT]) for v in range(2)]
        self.xt_ps = [a.ps(f"xt_ps{v}", [P, GT]) for v in range(2)]
        self.s_ps = [a.ps(f"s_ps{v}", [P, G * E]) for v in range(2)]
        self.xt_done, self.xt_copied, self.s_done, self.s_ready, self.high, self.low = (
            a.sem(n) for n in ("xt_done", "xt_copied", "s_done", "s_ready", "high", "low"))

    def pool(self, pool):
        def low_half(g, v):
            pool.wait_ge(self.high, g + 1)
            pool.tensor_tensor(self.T.XHL[:, ds(g * G, G), 1, :], self.ln.xn[v][:, :, :],
                               self.T.XHL[:, ds(g * G, G), 0, :], ALU.subtract).then_inc(self.low, 1)

        def body(it):
            for v in range(2):
                g = 2 * it + v
                self.ln.root(pool, g, v)
                if not isinstance(g, int) or g > 1:
                    low_half(g - 2, v)
        rounds(pool, GROUPS // 2, body)
        for v in range(2):
            low_half(GROUPS - 2 + v, v)

    def vector(self, dve):
        def step(s, v):
            w = 1 - v
            if is_group(s):
                self.ln.sums(dve, s, v)
            if is_group(s - 1):
                at_least(dve, self.xt_done, s - 2)
                at_least(dve, self.low, s - 2)
                self.ln.apply(dve, s - 1, w)
            if is_group(s - 3):
                g = s - 3
                dve.wait_ge(self.s_done, g + 1)
                out = self.SC[:, ds(g * G, G), :]
                sc = self.s_ps[w][:, :].rearrange("p (t e) -> p t e", e=E)
                if self.gate == 0:
                    dve.tensor_tensor(out, sc, self.T.gb0[:, :].unsqueeze(1).to_broadcast([P, G, E]), ALU.add)\
                        .then_inc(self.s_ready, 1)
                else:
                    dve.tensor_copy(out, sc).then_inc(self.s_ready, 1)
        groups(dve, step, 4, 3)

    def tensor(self, pe):
        def step(s, v):
            if is_group(s):
                pe.wait_ge(self.ln.xn_ready, s + 1)
                at_least(pe, self.xt_copied, s - 1)
                for t in range(G):
                    last = pe.transpose(self.xt_ps[v][:, t * P:(t + 1) * P], self.ln.xn[v][:, t, :],
                                        self.T.identF[:, :])
                last.then_inc(self.xt_done, 1)
            if is_group(s - 1):
                g, w = s - 1, 1 - v
                pe.wait_ge(self.xt_copied, g + 1)
                at_least(pe, self.s_ready, g - 1)
                for t in range(G):
                    last = pe.matmul(self.s_ps[w][:, t * E:(t + 1) * E], self.xnT[w][:, t * P:(t + 1) * P],
                                     self.T.gateT[:, self.gate, :], start=True, stop=True)
                last.then_inc(self.s_done, 1)
        groups(pe, step, 4, 1)

    def scalar(self, act):
        def body(it):
            for v in range(2):
                g = 2 * it + v
                act.wait_ge(self.xt_done, g + 1)
                at_least(act, self.s_done, g - 1)
                act.copy(self.xnT[v][:, :], self.xt_ps[v][:, :]).then_inc(self.xt_copied, 1)
                act.copy(self.T.XHL[:, ds(g * G, G), 0, :], self.ln.xn[v][:, :, :]).then_inc(self.high, 1)
        rounds(act, GROUPS // 2, body)


class Chain:

    def __init__(self, eng, sem):
        self.eng, self.sem, self.n = eng, sem, 0

    def __call__(self, ins):
        self.n += 1
        ins.then_inc(self.sem, 1)
        self.eng.wait_ge(self.sem, self.n)


def spread(ap, n):
    return ap.unsqueeze(2).to_broadcast([ap.shape[0], ap.shape[1], n])


def softmax_first(dve, chain, sc, SC, peak, shifted_ready):
    dve.wait_ge(sc.s_ready, GROUPS)
    chain(dve.tensor_reduce(peak, SC, AX_X, ALU.max))
    dve.tensor_tensor(SC, SC, spread(peak, E), ALU.subtract).then_inc(shifted_ready, 1)


def softmax_last(dve, chain, PR, total, exp_ready):
    dve.wait_ge(exp_ready, 1)
    chain(dve.tensor_reduce(total, PR, AX_X, ALU.add))
    chain(dve.reciprocal(total, total))
    chain(dve.tensor_tensor(PR, PR, spread(total, E), ALU.mult))


def route0(nc, I, T):
    with ExitStack() as ctx:
        a = Alloc(nc, ctx, "route0")
        sc = Scores(a, T, 0)
        PR, eq, rest, A, one1, one2 = (a.sb(n, [P, TILES, E]) for n in ("PR", "eq", "rest", "A", "one1", "one2"))
        peak, total, p1, p2, top = (a.sb(n, [P, TILES]) for n in ("peak", "total", "p1", "p2", "top"))
        rank8, count, padded, begin, adjust, ones8 = (a.sb(n, [P, E]) for n in ("rank8", "count", "padded", "begin",
                                                                              "adjust", "ones8"))
        padded_i = a.sb("padded_i", [P, E], I32)
        chosen = a.sb("chosen", [P, E, TILES], BF16)
        onesf, csum, pre, tot = (a.sb(n, [P, E * TILES]) for n in ("onesf", "csum", "pre", "tot"))
        slot_f = a.sb("slot_f", [P, TOPK, TILES])
        reach = a.sb("reach", [P, SLOT_TILES, E])
        first = a.sb("first", [P, SLOT_TILES])
        owner = a.sb("owner", [P, SLOT_TILES])
        zeros = a.sb("zeros", [P, 8, 2 * D], BF16)
        pre_ps = a.ps("pre_ps", [P, 512])
        tot_ps = a.ps("tot_ps", [P, 512])
        up, gp = ([a.sb(f"{n}{v}", [R0, C0, P]) for v in range(2)] for n in ("up", "gp"))
        down = [a.sb(f"down{v}", [P, F0]) for v in range(2)]
        ring = [*sc.xt_ps, *(a.ps(f"ring{v}", [P, 512]) for v in range(2))]
        w_in = [a.sem(f"w_in{v}") for v in range(2)]
        w_turned, w_high, w_low = (a.sem(n) for n in ("w_turned", "w_high", "w_low"))

        def weights(n, half):
            e, bank = n // 3, ring[n % 4]
            if n % 3 == 2:
                return T.WD[:, half, e, :], bank[0:R0, :]
            return (T.WU, T.WG)[n % 3][:, half, e, :], bank[:, 0:F0]
        zset, zero_out, shifted_ready, exp_ready, chosen_ready, counted, step, slots_ready, sent = (
            a.sem(n) for n in ("zset", "zero_out", "shifted_ready", "exp_ready", "chosen_ready", "counted", "step",
                               "slots_ready", "sent"))
        with nc.Block() as block:
            @block.sync
            def _(sp):
                sp.wait_ge(zset, 1)
                for c in range(ST * SLOT_TILES // (8 * P)):
                    sp.dma_start(T.xs_dram[c * 8 * P:(c + 1) * 8 * P, :].rearrange("(n p) d -> p n d", p=P),
                                 zeros[:, :, :]).then_inc(zero_out, 16)
                for e in range(E):
                    v = e % 2
                    at_least(sp, w_turned, 3 * (e - 1))
                    rows = slice(e * C0, (e + 1) * C0)
                    for name, out in (("L0_ffn_up_w", up[v]), ("L0_ffn_gp_w", gp[v])):
                        sp.dma_start(out[:, :, :], I[name].rearrange("e (c r) d -> r (e c) d", r=R0)[:, rows, :])\
                            .then_inc(w_in[v], 16)
                    sp.dma_start(down[v][:, :], I["L0_ffn_down_w"][e, :, :]).then_inc(w_in[v], 16)
                sp.wait_ge(zero_out, 16 * (ST * SLOT_TILES // (8 * P)))

            @block.gpsimd
            def _(pool):
                pool.memset(zeros[:, :, :], 0.0).then_inc(zset, 1)
                sc.pool(pool)
                pool.wait_ge(zero_out, 16 * (ST * SLOT_TILES // (8 * P)))
                pool.wait_ge(sc.low, GROUPS)
                for k in range(TOPK):
                    pool.wait_ge(slots_ready, k + 1)
                    for t in range(TILES):
                        pool.indirect_dma_start(
                            T.xs_dram[:, :], bass.IndirectOffsetOnAxis(ap=T.slot[:, k, t:t + 1].bitcast(U32), axis=0),
                            T.XHL[:, t, :, :].rearrange("p a d -> p (a d)"), None).then_inc(sent, 16)
                pool.wait_ge(sent, 16 * TILES * TOPK)

            @block.tensor
            def _(pe):
                sc.tensor(pe)
                pe.wait_ge(chosen_ready, 1)
                m = chosen[:, :, :].rearrange("p e t -> p (e t)")
                pe.matmul(pre_ps[:, 0:E * TILES], T.before[:, :], m, start=True, stop=True)
                pe.matmul(tot_ps[:, 0:E * TILES], T.ones[:, :], m, start=True, stop=True).then_inc(counted, 1)
                for n in range(3 * E):
                    e = n // 3
                    v = e % 2
                    pe.wait_ge(w_in[v], 48 * (e // 2 + 1))
                    if n >= 4:
                        pe.wait_ge(w_low, n - 3)
                    for c in range(C0):
                        if n % 3 == 2:
                            last = pe.transpose(ring[n % 4][0:R0, c * P:(c + 1) * P], down[v][:, c * R0:(c + 1) * R0],
                                                T.identF[:, :])
                        else:
                            last = pe.transpose(ring[n % 4][:, c * R0:(c + 1) * R0], (up, gp)[n % 3][v][:, c, :],
                                                T.identF[0:R0, 0:R0])
                    last.then_inc(w_turned, 1)

            @block.scalar
            def _(act):
                act.wait_ge(T.bias_in, 16 * (2 + 2 * C0))
                sc.scalar(act)
                act.wait_ge(shifted_ready, 1)
                act.activation(PR[:, :, :], sc.SC[:, :, :], ACT.Exp).then_inc(exp_ready, 1)
                for n in range(3 * E):
                    act.wait_ge(w_turned, n + 1)
                    out, src = weights(n, 0)
                    act.copy(out, src).then_inc(w_high, 1)

            @block.vector
            def _(dve):
                chain = Chain(dve, step)
                dve.memset(onesf[:, :], 1.0)
                dve.memset(ones8[:, :], 1.0)
                dve.tensor_scalar(first[:, :], T.iotaB[:, 0:SLOT_TILES], float(ST), None, ALU.mult)
                chain(dve.tensor_scalar(rank8[:, :], T.iotaB[:, 0:E], -1.0, float(E), ALU.mult, ALU.add))
                dve.wait_ge(T.bias_in, 16 * (2 + 2 * C0))
                sc.vector(dve)
                softmax_first(dve, chain, sc, sc.SC[:, :, :], peak[:, :], shifted_ready)
                softmax_last(dve, chain, PR[:, :, :], total[:, :], exp_ready)
                ranks = rank8[:, :].unsqueeze(1).to_broadcast([P, TILES, E])
                src = PR
                for value, one in ((p1, one1), (p2, one2)):
                    chain(dve.tensor_reduce(value[:, :], src[:, :, :], AX_X, ALU.max))
                    chain(dve.tensor_tensor(eq[:, :, :], src[:, :, :], spread(value[:, :], E), ALU.is_equal))
                    chain(dve.tensor_tensor(eq[:, :, :], eq[:, :, :], ranks, ALU.mult))
                    chain(dve.tensor_reduce(top[:, :], eq[:, :, :], AX_X, ALU.max))
                    chain(dve.tensor_tensor(one[:, :, :], eq[:, :, :], spread(top[:, :], E), ALU.is_equal))
                    if one is one1:
                        chain(dve.scalar_tensor_tensor(rest[:, :, :], one1[:, :, :], -2.0, PR[:, :, :], ALU.mult, ALU.add))
                    src = rest
                chain(dve.tensor_tensor(chosen[:, :, :].rearrange("p e t -> p t e"), one1[:, :, :], one2[:, :, :], ALU.add))
                dve.sem_inc(chosen_ready, 1)
                chain(dve.tensor_tensor(total[:, :], p1[:, :], p2[:, :], ALU.add))
                chain(dve.tensor_scalar(total[:, :], total[:, :], 1e-20, None, ALU.add))
                chain(dve.reciprocal(total[:, :], total[:, :]))
                dve.tensor_tensor(T.share[:, 0, :], p1[:, :], total[:, :], ALU.mult)
                dve.tensor_tensor(T.share[:, 1, :], p2[:, :], total[:, :], ALU.mult)
                dve.wait_ge(counted, 1)
                dve.tensor_copy(tot[:, :], tot_ps[:, 0:E * TILES])
                chain(dve.tensor_copy(pre[:, :], pre_ps[:, 0:E * TILES]))
                dve.tensor_tensor_scan(csum[:, :], onesf[:, :], tot[:, :], 0.0, ALU.mult, ALU.add)
                chain(dve.tensor_reduce(count[:, :], tot[:, :].rearrange("p (e t) -> p e t", e=E), AX_X, ALU.add))
                dve.tensor_tensor_scan(adjust[:, :], ones8[:, :], count[:, :], 0.0, ALU.mult, ALU.add)
                chain(dve.tensor_scalar(padded[:, :], count[:, :], float(ST - 1), None, ALU.add))
                dve.tensor_tensor(csum[:, :], csum[:, :], tot[:, :], ALU.subtract)
                chain(dve.tensor_copy(padded_i[:, :], padded[:, :]))
                dve.tensor_tensor(adjust[:, :], adjust[:, :], count[:, :], ALU.subtract)
                chain(dve.tensor_scalar(padded_i[:, :], padded_i[:, :], -ST, None, ALU.bitwise_and))
                dve.tensor_tensor(csum[:, :], csum[:, :], pre[:, :], ALU.add)
                chain(dve.tensor_copy(padded[:, :], padded_i[:, :]))
                chain(dve.tensor_tensor_scan(begin[:, :], ones8[:, :], padded[:, :], 0.0, ALU.mult, ALU.add))
                chain(dve.tensor_tensor(begin[:, :], begin[:, :], padded[:, :], ALU.subtract))
                chain(dve.tensor_tensor(adjust[:, :], begin[:, :], adjust[:, :], ALU.subtract))
                c3 = csum[:, :].rearrange("p (e t) -> p e t", e=E)
                chain(dve.tensor_tensor(c3, c3, spread(adjust[:, :], TILES), ALU.add))
                for k, one in ((0, one1), (1, one2)):
                    chain(dve.tensor_tensor(A[:, :, :], one[:, :, :], c3.rearrange("p e t -> p t e"), ALU.mult))
                    chain(dve.tensor_reduce(slot_f[:, k, :], A[:, :, :], AX_X, ALU.add))
                    dve.tensor_copy(T.slot[:, k, :], slot_f[:, k, :]).then_inc(slots_ready, 1)
                chain(dve.tensor_tensor(reach[:, :, :], spread(first[:, :], E),
                                        begin[:, :].unsqueeze(1).to_broadcast([P, SLOT_TILES, E]), ALU.is_ge))
                chain(dve.tensor_reduce(owner[:, :], reach[:, :, :], AX_X, ALU.add))
                chain(dve.tensor_scalar(owner[:, :], owner[:, :], -1.0, None, ALU.add))
                dve.tensor_copy(T.owner[:, :], owner[:, :])
                for n in range(3 * E):
                    dve.wait_ge(w_high, n + 1)
                    out, src = weights(n, 1)
                    dve.tensor_tensor(out, src, weights(n, 0)[0], ALU.subtract).then_inc(w_low, 1)


def experts0(nc, I, T):
    with ExitStack() as ctx:
        a = Alloc(nc, ctx, "experts0")
        LAG = 5
        RING = 8
        BODY = 2 * RING
        SUB = ST // P
        HC = C0 // 2
        HW = HC * ST
        xs = [a.sb(f"xs{v}", [P, SUB, 2 * D], BF16) for v in range(RING)]
        xt = [a.sb(f"xt{v}", [P, 2, ST], BF16) for v in range(2)]
        gated = [a.sb(f"gated{v}", [R0, HW]) for v in range(2)]
        z = [a.sb(f"z{v}", [R0, HW]) for v in range(2)]
        hidden = [a.sb(f"hidden{v}", [R0, HW]) for v in range(2)]
        hh = [a.sb(f"hh{v}", [R0, 2, C0, ST], BF16) for v in range(2)]
        ys = [a.sb(f"ys{v}", [P, SUB, D]) for v in range(2)]
        xt_ps = [a.ps(f"xt_ps{v}", [P, 2, ST], BF16) for v in range(2)]
        g_ps = [a.ps(f"g_ps{v}", [P, HW]) for v in range(2)]
        u_ps = [a.ps(f"u_ps{v}", [P, HW]) for v in range(2)]
        y_ps = [a.ps(f"y_ps{v}", [P, SUB, D]) for v in range(2)]
        w1 = [a.sb(f"w1{v}", [P, F1]) for v in range(2)]
        w2 = [a.sb(f"w2{v}", [P, C1, P]) for v in range(2)]
        w_in = [a.sem(f"w_in{v}") for v in range(2)]
        w_high, w_low = a.sem("w_high"), a.sem("w_low")
        w1_d = I["L1_ffn_w1"]
        w2_d = I["L1_ffn_w2"].rearrange("e (c p) d -> e p c d", p=P)
        xs_in = [a.sem(f"xs_in{v}") for v in range(RING)]
        ys_out = [a.sem(f"ys_out{v}") for v in range(2)]
        xt_done, xt_copied, g_done, u_done, gate_ready, z_ready, silu_ready, high, low, y_done, y_ready = (
            a.sem(n) for n in ("xt_done", "xt_copied", "g_done", "u_done", "gate_ready", "z_ready", "silu_ready",
                               "high", "low", "y_done", "y_ready"))

        def live(p):
            return not isinstance(p, int) or 0 <= p < SLOT_TILES

        def owners_from(eng, first, back, count):
            _, values = nc.values_load_multi_w_load_instructions(
                T.owner[0:1, ds(first, count + back)], engines=[eng.engine], min_val=0, max_val=E - 1)
            return lambda n: values[n + back]

        def steps(step, experts=True, tail=2):
            def run(eng):
                def some(first, back, count, tile):
                    owner = owners_from(eng, first, back, count) if experts else None
                    for n in range(count):
                        step(tile(n), n % RING, lambda ago, n=n: owner(n - ago))
                some(0, 0, RING, lambda n: n)
                with eng.Fori(0, (SLOT_TILES - RING) // BODY) as it:
                    some(it * BODY + (RING - 2), 2, BODY, lambda n: it * BODY + (RING + n))
                if experts:
                    owner = owners_from(eng, SLOT_TILES - 2, 2, 0)
                for n in range(tail):
                    step(SLOT_TILES + n, n % RING, lambda ago, n=n: owner(n - ago))
            return run

        def one(ap):
            return ap.rearrange("p a n -> p (a n)")

        with nc.Block() as block:
            @block.sync
            def _(sp):
                def step(q, u, _):
                    if live(q):
                        at_least(sp, xt_done, q - RING + 1)
                        sp.dma_start(xs[u][:, :, :], T.xs_dram[ds(q * ST, ST), :].rearrange("(s p) d -> p s d", p=P))\
                            .then_inc(xs_in[u], 16)
                    if live(q - LAG):
                        sp.wait_ge(y_ready, q - LAG + 1)
                        w = (u - LAG) % 2
                        sp.dma_start(T.ys_dram[ds((q - LAG) * ST, ST), :].rearrange("(s p) d -> p s d", p=P),
                                     ys[w][:, :, :]).then_inc(ys_out[w], 16)
                steps(step, False, LAG)(sp)
                for v in range(2):
                    sp.wait_ge(ys_out[v], 8 * SLOT_TILES)

            @block.gpsimd
            def _(pool):
                def load(e):
                    pool.dma_start(w1[e % 2][:, :], w1_d[e, :, :]).then_inc(w_in[e % 2], 16)
                    pool.dma_start(w2[e % 2][:, :, :], w2_d[e, :, :, :]).then_inc(w_in[e % 2], 16)
                load(0)
                for e in range(E):
                    if e + 1 < E:
                        at_least(pool, w_low, 2 * e)
                        load(e + 1)
                    pool.wait_ge(w_in[e % 2], 32 * (e // 2 + 1))
                    pool.tensor_copy(T.W1[:, 0, e, :], w1[e % 2][:, :]).then_inc(w_high, 1)
                    pool.tensor_copy(T.W2[:, 0, e, :], one(w2[e % 2][:, :, :])).then_inc(w_high, 1)
                    pool.wait_ge(w_high, 2 * e + 2)
                    pool.tensor_tensor(T.W1[:, 1, e, :], w1[e % 2][:, :], T.W1[:, 0, e, :], ALU.subtract).then_inc(w_low, 1)
                    pool.tensor_tensor(T.W2[:, 1, e, :], one(w2[e % 2][:, :, :]), T.W2[:, 0, e, :], ALU.subtract)\
                        .then_inc(w_low, 1)

            @block.tensor
            def _(pe):
                TERMS = ((0, 0), (0, 1), (1, 0))

                def step(p, ring, owner):
                    u = ring % 2
                    if live(p):
                        pe.wait_ge(xs_in[ring], (p - ring) * (16 // RING) + 16)
                        at_least(pe, xt_copied, p - 1)
                        for half in range(2):
                            for sub in range(SUB):
                                last = pe.transpose(xt_ps[u][:, half, sub * P:(sub + 1) * P],
                                                    xs[ring][:, sub, half * D:(half + 1) * D], T.identB[:, :])
                        last.then_inc(xt_done, 1)
                    if live(p - 1):
                        v = 1 - u
                        e = owner(1)
                        pe.wait_ge(xt_copied, p)
                        for j in range(2):
                            for ps, W, done, read in ((g_ps, T.WG, g_done, gate_ready), (u_ps, T.WU, u_done, z_ready)):
                                at_least(pe, read, 2 * (p - 2) + j + 1)
                                for c in range(HC):
                                    cc = j * HC + c
                                    for n, (wh, xh) in enumerate(TERMS):
                                        last = pe.matmul(ps[j][0:R0, c * ST:(c + 1) * ST],
                                                         one(W[:, wh, ds(e, 1), cc * R0:(cc + 1) * R0]), xt[v][:, xh, :],
                                                         start=(n == 0), stop=(n == 2))
                                last.then_inc(done, 1)
                    if live(p - 2):
                        e = owner(2)
                        pe.wait_ge(high, 2 * (p - 1))
                        pe.wait_ge(low, 2 * (p - 1))
                        at_least(pe, y_ready, p - 3)
                        for sub in range(SUB):
                            for c in range(C0):
                                for n, (wh, xh) in enumerate(TERMS):
                                    last = pe.matmul(y_ps[u][:, sub, :], hh[u][:, xh, c, sub * P:(sub + 1) * P],
                                                     one(T.WD[:, wh, ds(e, 1), c * P:(c + 1) * P]),
                                                     start=(c == 0 and n == 0), stop=(c == C0 - 1 and n == 2))
                        last.then_inc(y_done, 1)
                steps(step)(pe)

            @block.scalar
            def _(act):
                def step(p, ring, owner):
                    if live(p - 1):
                        v = 1 - ring % 2
                        e = owner(1)
                        for j in range(2):
                            act.wait_ge(g_done, 2 * (p - 1) + j + 1)
                            at_least(act, z_ready, 2 * (p - 2) + j + 1)
                            for c in range(HC):
                                last = act.activation(gated[j][:, c * ST:(c + 1) * ST], g_ps[j][0:R0, c * ST:(c + 1) * ST],
                                                      ACT.Identity, bias=one(T.gb[:, ds(e, 1), j * HC + c:j * HC + c + 1]))
                            last.then_inc(gate_ready, 1)
                        for j in range(2):
                            act.wait_ge(z_ready, 2 * (p - 1) + j + 1)
                            at_least(act, y_done, p - 2)
                            act.activation(hh[v][:, 0, j * HC:(j + 1) * HC, :].rearrange("p c t -> p (c t)"), z[j][:, :],
                                           ACT.Silu).then_inc(high, 1)
                            at_least(act, low, 2 * (p - 2) + j + 1)
                            act.activation(hidden[j][:, :], z[j][:, :], ACT.Silu).then_inc(silu_ready, 1)
                steps(step)(act)

            @block.vector
            def _(dve):
                def step(p, ring, owner):
                    u = ring % 2
                    if live(p):
                        dve.wait_ge(xt_done, p + 1)
                        at_least(dve, u_done, 2 * (p - 1))
                        dve.tensor_copy(xt[u][:, :, :], xt_ps[u][:, :, :]).then_inc(xt_copied, 1)
                    if live(p - 2):
                        for j in range(2):
                            dve.wait_ge(silu_ready, 2 * (p - 2) + j + 1)
                            at_least(dve, y_done, p - 3)
                            h = hh[u][:, :, j * HC:(j + 1) * HC, :].rearrange("p h c t -> p h (c t)")
                            dve.tensor_tensor(h[:, 1, :], hidden[j][:, :], h[:, 0, :], ALU.subtract).then_inc(low, 1)
                    if live(p - 1):
                        e = owner(1)
                        for j in range(2):
                            dve.wait_ge(u_done, 2 * (p - 1) + j + 1)
                            dve.wait_ge(gate_ready, 2 * (p - 1) + j + 1)
                            at_least(dve, silu_ready, 2 * (p - 2) + j + 1)
                            for c in range(HC):
                                last = dve.scalar_tensor_tensor(
                                    z[j][:, c * ST:(c + 1) * ST], u_ps[j][0:R0, c * ST:(c + 1) * ST],
                                    one(T.ub[:, ds(e, 1), j * HC + c:j * HC + c + 1]), gated[j][:, c * ST:(c + 1) * ST],
                                    ALU.add, ALU.mult)
                            last.then_inc(z_ready, 1)
                    if live(p - 2):
                        e = owner(2)
                        dve.wait_ge(y_done, p - 1)
                        at_least(dve, ys_out[u], 8 * (p - u) - 16)
                        dve.tensor_tensor(ys[u][:, :, :], y_ps[u][:, :, :],
                                          T.db0[:, ds(e, 1), :].to_broadcast([P, SUB, D]), ALU.add).then_inc(y_ready, 1)
                steps(step)(dve)


def attend1(nc, I, T):
    with ExitStack() as ctx:
        a = Alloc(nc, ctx, "attend1")
        SCALE = D ** -0.5
        ln = Norm(a, T)
        rows = [a.sb(f"rows{v}", [P, G, TOPK, D]) for v in range(2)]
        cg, qT, kT, V = ([a.sb(f"{n}{v}", [P, GT]) for v in range(2)] for n in ("cg", "qT", "kT", "V"))
        xnT, sm, probs, pT, oT = (a.sb(n, [P, GT]) for n in ("xnT", "sm", "probs", "pT", "oT"))
        peak, nmax = (a.sb(n, [P, G]) for n in ("peak", "nmax"))
        total, inverse = ([a.sb(f"{n}{v}", [P, G]) for v in range(2)] for n in ("total", "inverse"))
        xt_ps, q_ps, k_ps, v_ps, s_ps, p_ps, o_ps, y_ps = (
            a.ps(n, [P, GT]) for n in ("xt_ps", "q_ps", "k_ps", "v_ps", "s_ps", "p_ps", "o_ps", "y_ps"))
        rows_in = [a.sem(f"rows_in{v}") for v in range(2)]
        cg_in = [a.sem(f"cg_in{v}") for v in range(2)]
        (first_added, combined, xt_done, xt_copied, q_done, q_ready, k_done, k_ready, v_done, v_ready, s_done, masked,
         peaked, nmax_ready, exped, p_done, p_copied, o_done, o_copied, y_done, inverted, x_done, biased) = (
            a.sem(n) for n in ("first_added", "combined", "xt_done", "xt_copied", "q_done", "q_ready", "k_done",
                               "k_ready", "v_done", "v_ready", "s_done", "masked", "peaked", "nmax_ready", "exped",
                               "p_done", "p_copied", "o_done", "o_copied", "y_done", "inverted", "x_done", "biased"))

        def tile(t):
            return slice(t * P, (t + 1) * P)

        with nc.Block() as block:
            @block.sync
            def _(sp):
                def body(it):
                    for v in range(2):
                        g = 2 * it + v
                        at_least(sp, v_done, g - 1)
                        at_least(sp, k_done, g - 1)
                        sp.dma_start(cg[v][:, :], T.ctxT[:, ds(g * GT, GT)]).then_inc(cg_in[v], 16)
                rounds(sp, GROUPS // 2, body)

            @block.gpsimd
            def _(pool):
                for g in range(GROUPS + 1):
                    if g < GROUPS:
                        at_least(pool, combined, g - 1)
                        for t in range(G):
                            for k in range(TOPK):
                                pool.indirect_dma_start(
                                    rows[g % 2][:, t, k, :], None, T.ys_dram[:, :],
                                    bass.IndirectOffsetOnAxis(ap=T.slot[:, k, g * G + t:g * G + t + 1].bitcast(U32), axis=0))\
                                    .then_inc(rows_in[g % 2], 16)
                    if g:
                        ln.root(pool, g - 1, (g - 1) % 2)

            @block.tensor
            def _(pe):
                def step(g, v):
                    b, w, c = g - 1, 1 - v, g - 2
                    if is_group(b):
                        pe.wait_ge(q_ready, b + 1)
                        pe.wait_ge(k_ready, b + 1)
                        at_least(pe, masked, b)
                        for t in range(G):
                            last = pe.matmul(s_ps[:, tile(t)], qT[w][:, tile(t)], kT[w][:, tile(t)],
                                             start=True, stop=True)
                        last.then_inc(s_done, 1)
                    if is_group(g):
                        pe.wait_ge(ln.xn_ready, g + 1)
                        at_least(pe, xt_copied, g)
                        for t in range(G):
                            last = pe.transpose(xt_ps[:, tile(t)], ln.xn[v][:, t, :], T.identF[:, :])
                        last.then_inc(xt_done, 1)
                        pe.wait_ge(cg_in[v], 8 * (g - v) + 16)
                        at_least(pe, v_ready, g)
                        for t in range(G):
                            last = pe.matmul(v_ps[:, tile(t)], cg[v][:, tile(t)], T.WT[:, 6, :], start=True, stop=True)
                        last.then_inc(v_done, 1)
                    if is_group(c):
                        pe.wait_ge(o_copied, c + 1)
                        at_least(pe, x_done, c)
                        for t in range(G):
                            last = pe.matmul(y_ps[:, tile(t)], oT[:, tile(t)], T.WT[:, 7, :], start=True, stop=True)
                        last.then_inc(y_done, 1)
                    if is_group(g):
                        pe.wait_ge(xt_copied, g + 1)
                        at_least(pe, q_ready, g)
                        pe.matmul(q_ps[:, :], T.WT[:, 4, :], xnT[:, :], start=True, stop=True).then_inc(q_done, 1)
                    if is_group(b):
                        pe.wait_ge(exped, b + 1)
                        at_least(pe, p_copied, b)
                        for t in range(G):
                            last = pe.transpose(p_ps[:, tile(t)], probs[:, tile(t)], T.identF[:, :])
                        last.then_inc(p_done, 1)
                    if is_group(g):
                        at_least(pe, k_ready, g)
                        pe.matmul(k_ps[:, :], T.WT[:, 5, :], cg[v][:, :], start=True, stop=True).then_inc(k_done, 1)
                    if is_group(b):
                        pe.wait_ge(v_ready, b + 1)
                        pe.wait_ge(p_copied, b + 1)
                        at_least(pe, o_copied, b)
                        for t in range(G):
                            last = pe.matmul(o_ps[:, tile(t)], V[w][:, tile(t)], pT[:, tile(t)], start=True, stop=True)
                        last.then_inc(o_done, 1)
                groups(pe, step, 4, 2)

            @block.scalar
            def _(act):
                def step(g, v):
                    b, w = g - 1, 1 - v
                    if is_group(g):
                        act.wait_ge(xt_done, g + 1)
                        at_least(act, q_done, g)
                        act.copy(xnT[:, :], xt_ps[:, :]).then_inc(xt_copied, 1)
                        act.wait_ge(v_done, g + 1)
                        at_least(act, o_done, g - 1)
                        act.copy(V[v][:, :], v_ps[:, :]).then_inc(v_ready, 1)
                    if is_group(b):
                        act.wait_ge(nmax_ready, b + 1)
                        at_least(act, p_done, b)
                        at_least(act, inverted, b - 1)
                        for t in range(G):
                            last = act.activation(probs[:, tile(t)], sm[:, tile(t)], ACT.Exp, bias=nmax[:, t:t + 1],
                                                  scale=SCALE, accum_out=total[w][:, t:t + 1])
                        last.then_inc(exped, 1)
                    if is_group(g):
                        act.wait_ge(q_done, g + 1)
                        at_least(act, s_done, g - 1)
                        act.activation(qT[v][:, :], q_ps[:, :], ACT.Identity, bias=T.bcol[:, 2:3]).then_inc(q_ready, 1)
                    if is_group(b):
                        act.wait_ge(p_done, b + 1)
                        at_least(act, o_done, b)
                        act.copy(pT[:, :], p_ps[:, :]).then_inc(p_copied, 1)
                    if is_group(g):
                        act.wait_ge(k_done, g + 1)
                        act.copy(kT[v][:, :], k_ps[:, :]).then_inc(k_ready, 1)
                    if is_group(b):
                        act.wait_ge(o_done, b + 1)
                        at_least(act, y_done, b)
                        act.copy(oT[:, :], o_ps[:, :]).then_inc(o_copied, 1)
                groups(act, step, 4, 1)

            @block.vector
            def _(dve):
                def step(s, v):
                    w = 1 - v
                    if is_group(s - 1):
                        g = s - 1
                        at_least(dve, xt_done, g - 1)
                        ln.apply(dve, g, w)
                        dve.wait_ge(ln.xn_ready, g + 1)
                        x = T.X[:, ds(g * G, G), :]
                        dve.tensor_tensor(x, x, T.bo1[:, :].unsqueeze(1).to_broadcast([P, G, D]), ALU.add)\
                            .then_inc(biased, 1)
                    if is_group(s - 2):
                        b = s - 2
                        dve.wait_ge(s_done, b + 1)
                        at_least(dve, exped, b)
                        s4 = sm[:, :].rearrange("p (t n) -> p t n", t=G)
                        dve.tensor_tensor(s4, s_ps[:, :].rearrange("p (t n) -> p t n", t=G),
                                          T.mask[:, :].unsqueeze(1).to_broadcast([P, G, P]), ALU.add).then_inc(masked, 1)
                        dve.wait_ge(masked, b + 1)
                        dve.tensor_reduce(peak[:, :], s4, AX_X, ALU.max).then_inc(peaked, 1)
                        dve.wait_ge(peaked, b + 1)
                        dve.tensor_scalar(nmax[:, :], peak[:, :], -SCALE, None, ALU.mult).then_inc(nmax_ready, 1)
                    if is_group(s):
                        dve.wait_ge(rows_in[v], (s - v) * 8 * TOPK * G + 16 * TOPK * G)
                        for k, done in enumerate((first_added, combined)):
                            for t in range(G):
                                x = flat2(T.X[:, ds(s * G + t, 1), :])
                                last = dve.scalar_tensor_tensor(x, rows[v][:, t, k, :], flat2(T.share[:, k:k + 1, ds(s * G + t, 1)]),
                                                                x, ALU.mult, ALU.add)
                            last.then_inc(done, 1)
                            dve.wait_ge(done, s + 1)
                        dve.tensor_copy(ln.scratch[:, 0:1], rows[v][:, 0, 0, 0:1])
                        ln.sums(dve, s, v)
                    if is_group(s - 2):
                        b = s - 2
                        dve.wait_ge(exped, b + 1)
                        at_least(dve, x_done, b - 1)
                        dve.reciprocal(inverse[v][:, :], total[v][:, :]).then_inc(inverted, 1)
                    if is_group(s - 3):
                        c = s - 3
                        dve.wait_ge(y_done, c + 1)
                        dve.wait_ge(biased, c + 1)
                        dve.wait_ge(inverted, c + 1)
                        for t in range(G):
                            x = flat2(T.X[:, ds(c * G + t, 1), :])
                            last = dve.scalar_tensor_tensor(x, y_ps[:, tile(t)], inverse[w][:, t:t + 1], x, ALU.mult, ALU.add)
                        last.then_inc(x_done, 1)
                groups(dve, step, 4, 3)


def route1(nc, I, T):
    with ExitStack() as ctx:
        a = Alloc(nc, ctx, "route1")
        sc = Scores(a, T, 1)
        PR = a.sb("PR", [P, TILES, E])
        peak, total = (a.sb(n, [P, TILES]) for n in ("peak", "total"))
        byexp = a.sb("byexp", [P, 4, SEQ])
        rest = a.sb("rest", [P, 4, SEQ])
        best = a.sb("best", [P, 4, CAP])
        where = a.sb("where", [P, 4, CAP], U32)
        where_f = a.sb("where_f", [P, 4, CAP])
        rows_i = a.sb("rows_i", [64, 1], I32)
        b2_i = a.sb("b2_i", [64, 1], I32)
        b2 = a.sb("b2", [64, 1])
        tile_i = a.sb("tile_i", [64, 16, E], I32)
        in4 = a.sb("in4", [64, 16, E])
        in_pair = a.sb("in_pair", [64, P], BF16)
        T.sent, T.rest_loaded = a.sem("sent"), a.sem("rest_loaded")
        e_ps = a.ps("e_ps", [P, 2, P])
        i_ps = a.ps("i_ps", [64, P])
        v_ps = a.ps("v_ps", [64, P])
        (shifted_ready, exp_ready, probs_ready, turned, step, found, back, cols_ready, loaded, iotas, pair_ready) = (
            a.sem(n) for n in ("shifted_ready", "exp_ready", "probs_ready", "turned", "step", "found", "back",
                               "cols_ready", "loaded", "iotas", "pair_ready"))
        with nc.Block() as block:
            @block.sync
            def _(sp):
                def send(d, src):
                    to = d.rearrange("(q p b k e) -> q b k p e", q=2, p=16, b=2, k=CAP)
                    for q in range(2):
                        for b in range(2):
                            r = (q * 2 + b) * CAP
                            sp.dma_start(to[q, b, :, :, :], src[r:r + CAP, :].rearrange("k (p e) -> k p e", e=E))\
                                .then_inc(T.sent, 16)
                sp.wait_ge(pair_ready, 1)
                send(T.pair_dram, in_pair)
                sp.wait_ge(T.sent, 4 * 16)
                first = 4 * 4 * P
                sp.dma_start(T.pair_row[:, 0:first], T.pair_dram[0:first].partition_broadcast(P)).then_inc(loaded, 16)
                sp.wait_ge(cols_ready, 1)
                send(T.eight_dram, T.in_eight)
                send(T.gain_dram, T.gain)
                sp.dma_start(T.pair_row[:, first:], T.pair_dram[first:].partition_broadcast(P)).then_inc(T.rest_loaded, 16)
                sp.wait_ge(loaded, 16)

            @block.gpsimd
            def _(pool):
                pool.iota(rows_i[:, :], pattern=[[0, 1]], base=0, channel_multiplier=1).then_inc(iotas, 1)
                pool.iota(tile_i[:, :, :], pattern=[[0, 4], [P, 4], [0, E]], base=0, channel_multiplier=0)\
                    .then_inc(iotas, 1)
                sc.pool(pool)

            @block.tensor
            def _(pe):
                sc.tensor(pe)
                pe.wait_ge(probs_ready, 1)
                for q in range(2):
                    last = pe.transpose(e_ps[:, q, :], PR[:, q * 16:(q + 1) * 16, :].rearrange("p t e -> p (t e)"),
                                        T.identF[:, :])
                last.then_inc(turned, 1)
                pe.wait_ge(found, 1)
                pe.transpose(i_ps[:, :], where_f[:, :, :].rearrange("p s k -> p (s k)"), T.identF[:, :])
                pe.transpose(v_ps[:, :], best[:, :, :].rearrange("p s k -> p (s k)"), T.identF[:, :]).then_inc(back, 1)

            @block.scalar
            def _(act):
                sc.scalar(act)
                act.wait_ge(shifted_ready, 1)
                act.activation(PR[:, :, :], sc.SC[:, :, :], ACT.Exp).then_inc(exp_ready, 1)

            @block.vector
            def _(dve):
                chain = Chain(dve, step)
                dve.wait_ge(iotas, 2)
                chain(dve.tensor_scalar(b2_i[:, :], rows_i[:, :], CAP, None, ALU.bitwise_and))
                chain(dve.tensor_copy(b2[:, :], b2_i[:, :]))
                chain(dve.tensor_scalar(b2[:, :], b2[:, :], float(SEQ // CAP), None, ALU.mult))
                chain(dve.tensor_copy(in4[:, :, :], tile_i[:, :, :]))
                sc.vector(dve)
                softmax_first(dve, chain, sc, sc.SC[:, :, :], peak[:, :], shifted_ready)
                softmax_last(dve, chain, PR[:, :, :], total[:, :], exp_ready)
                dve.sem_inc(probs_ready, 1)
                dve.wait_ge(turned, 1)
                chain(dve.tensor_copy(byexp[:, :, :].rearrange("p s t -> p (s t)"), e_ps[:, :, :].rearrange("p q t -> p (q t)")))
                for find in (lambda s: dve.max(best[:, s, 0:8], byexp[:, s, :]),
                             lambda s: dve.max_index(where[:, s, 0:8], best[:, s, 0:8], byexp[:, s, :]),
                             lambda s: dve.match_replace(rest[:, s, :], best[:, s, 0:8], byexp[:, s, :], -1.0),
                             lambda s: dve.max(best[:, s, 8:16], rest[:, s, :]),
                             lambda s: dve.max_index(where[:, s, 8:16], best[:, s, 8:16], rest[:, s, :])):
                    for s in range(3):
                        find(s)
                    chain(find(3))
                chain(dve.tensor_copy(where_f[:, :, :], where[:, :, :]))
                dve.sem_inc(found, 1)
                dve.wait_ge(back, 1)
                dve.tensor_scalar(in_pair[:, :], i_ps[:, :], b2[:, 0:1], None, ALU.add).then_inc(pair_ready, 1)
                chain(dve.scalar_tensor_tensor(T.in_eight[:, :], i_ps[:, :], b2[:, 0:1],
                                               in4[:, :, :].rearrange("p t e -> p (t e)"), ALU.add, ALU.add))
                chain(dve.tensor_copy(T.gain[:, :], v_ps[:, :]))
                dve.sem_inc(cols_ready, 1)


def experts1(nc, I, T):
    with ExitStack() as ctx:
        a = Alloc(nc, ctx, "experts1")
        XG = [a.sb(f"XG{h}", [P, E, BATCH, CAP], BF16) for h in range(2)]
        eight_col, gain_col = (a.sb(n, [P, GROUPS, E]) for n in ("eight_col", "gain_col"))
        cols_in = a.sem("cols_in")
        Y = a.sb("Y", [P, GROUPS, E, 2, D], BF16)
        pick = [a.sb(f"pick{v}", [P, 4 * P], BF16) for v in range(4)]
        BY_DVE, RING = 6, 4
        ring = pick
        others = [a.sb(f"place_too{v}", [P, GT], BF16) for v in range(2 * (E - BY_DVE))]
        hidden = [a.sb(f"hidden{v}", [P, GT]) for v in range(2)]
        hh = [a.sb(f"hh{v}", [P, 2, C1, GT], BF16) for v in range(2)]
        banks = a.ps("banks", [P, 8, 512])
        bank = [banks[:, i, :] for i in range(8)]
        out_d = T.out.rearrange("b s d -> (b s) d").rearrange("(n p) d -> p n d", p=P)
        (picked, g_done, g_high, g_low) = (a.sem(n) for n in ("picked", "g_done", "g_high", "g_low"))
        (h_done, gelu_ready, high, low, y_done, y_high, y_low) = (
            a.sem(n) for n in ("h_done", "gelu_ready", "high", "low", "y_done", "y_high", "y_low"))
        distance = hidden[0]
        measured = a.sem("measured")
        placed, placed_too, sum_done, low_added, x_done, stored = (
            a.sem(n) for n in ("placed", "placed_too", "sum_done", "low_added", "x_done", "stored"))
        TERMS = ((0, 0), (0, 1), (1, 0))
        STEPS = 2 * E

        def gathers(eng, gather, tail):
            for r in range(4):
                gather(r, r)
            with eng.Fori(1, TILES // 8) as it:
                for v in range(4):
                    gather(it * 4 + v, v)
            for v in range(tail):
                gather(TILES // 2 + v, v)

        def gathered(v, h):
            return bank[2 * v + h][:, :].rearrange("p (b k e) -> p b k e", b=4, e=E)

        def place(v, e):
            if e < BY_DVE:
                return ring[(BY_DVE * v + e) % RING][:, :]
            return others[v * (E - BY_DVE) + e - BY_DVE][:, :]

        def flat3(ap):
            return ap.rearrange("p a b c -> p (a b c)")

        def live(s):
            return not isinstance(s, int) or 0 <= s < STEPS

        def steps(eng, step, tail):
            for s in range(2):
                step(s, 0, s)
            with eng.Fori(1, E) as e:
                for j in range(2):
                    step(2 * e + j, e, j)
            for j in range(tail):
                step(STEPS + j, E, j)

        with nc.Block() as block:
            @block.sync
            def _(sp):
                sp.wait_ge(T.sent, 12 * 16)
                for d, dst in ((T.gain_dram, gain_col), (T.eight_dram, eight_col)):
                    sp.dma_start(dst[:, :, :], d.rearrange("(g q e) -> q g e", q=P, e=E)).then_inc(cols_in, 16)

                def body(g):
                    sp.wait_ge(x_done, g + 1)
                    sp.dma_start(out_d[:, ds(g * G, G), :], T.X[:, ds(g * G, G), :]).then_inc(stored, 16)
                rounds(sp, GROUPS, body)
                sp.wait_ge(stored, 16 * GROUPS)

            @block.tensor
            def _(pe):
                def gather(r, v):
                    pe.wait_ge(picked, r + 1)
                    at_least(pe, g_high, r - 3)
                    at_least(pe, g_low, r - 3)
                    for h in range(2):
                        for t in range(2):
                            last = pe.matmul(bank[2 * v + h][:, t * 2 * P:(t + 1) * 2 * P],
                                             T.XHL[:, ds(2 * r + t, 1), h, :].rearrange("p a d -> p (a d)"),
                                             pick[v][:, t * 2 * P:(t + 1) * 2 * P], start=True, stop=True)
                    last.then_inc(g_done, 1)
                gathers(pe, gather, 0)

                def step(s, e, j):
                    if live(s):
                        if isinstance(s, int) and s == 0:
                            pe.wait_ge(g_high, TILES // 2)
                            pe.wait_ge(g_low, TILES // 2)
                        for c in range(C1):
                            at_least(pe, gelu_ready, 4 * (s - 1) + c + 1)
                            for n, (wh, xh) in enumerate(TERMS):
                                last = pe.matmul(bank[c][:, :],
                                                 flat2(T.W1[:, wh, ds(e, 1), c * P:(c + 1) * P]),
                                                 flat3(XG[xh][:, ds(e, 1), 32 * j:32 * j + 32, :]),
                                                 start=(n == 0), stop=(n == 2))
                            last.then_inc(h_done, 1)
                    if live(s - 1):
                        r, w = s - 1, 1 - j
                        ee = e if j else e - 1
                        pe.wait_ge(high, 4 * r + 4)
                        pe.wait_ge(low, 4 * r + 4)
                        at_least(pe, y_low, r - 1)
                        for m in range(4):
                            for c in range(C1):
                                for n, (wh, xh) in enumerate(TERMS):
                                    last = pe.matmul(bank[4 + w][:, m * P:(m + 1) * P], hh[w][:, xh, c, m * P:(m + 1) * P],
                                                     flat2(T.W2[:, wh, ds(ee, 1), c * P:(c + 1) * P]),
                                                     start=(c == 0 and n == 0), stop=(c == C1 - 1 and n == 2))
                        last.then_inc(y_done, 1)
                steps(pe, step, 1)

                pe.wait_ge(y_low, STEPS)

                def scatter(it):
                    for v in range(2):
                        g = 2 * it + v
                        at_least(pe, x_done, g - 1)
                        for e in range(E):
                            if e < BY_DVE:
                                pe.wait_ge(placed, BY_DVE * g + e + 1)
                            else:
                                pe.wait_ge(placed_too, (E - BY_DVE) * g + e - BY_DVE + 1)
                            for t in range(G):
                                last = pe.matmul(bank[2 * v + t // 2][:, t % 2 * 2 * D:(t % 2 + 1) * 2 * D],
                                                 place(v, e)[:, t * P:(t + 1) * P],
                                                 Y[:, ds(g, 1), e, :, :].rearrange("p a h d -> p (a h d)"),
                                                 start=(e == 0 and t % 2 == 0), stop=(e == E - 1), skip_group_check=True)
                            last.then_inc(sum_done, 1)
                rounds(pe, GROUPS // 2, scatter)

            @block.scalar
            def _(act):
                def gather(r, v):
                    act.wait_ge(g_done, r + 1)
                    act.copy(XG[0][:, :, ds(4 * r, 4), :].rearrange("p e b k -> p b k e"), gathered(v, 0)).then_inc(g_high, 1)
                gathers(act, gather, 0)

                def step(s, e, j):
                    if live(s):
                        for c in range(C1):
                            act.wait_ge(h_done, 4 * s + c + 1)
                            at_least(act, low, 4 * s + c - 1)
                            act.activation(hidden[c % 2][:, :], bank[c][:, :], ACT.Gelu).then_inc(gelu_ready, 1)
                            at_least(act, y_done, s - 1)
                            act.wait_ge(gelu_ready, 4 * s + c + 1)
                            act.copy(hh[j][:, 0, c, :], hidden[c % 2][:, :]).then_inc(high, 1)
                steps(act, step, 0)

                act.wait_ge(cols_in, 32)
                act.wait_ge(low, C1 * STEPS)

                def scatter(it):
                    for v in range(2):
                        g = 2 * it + v
                        for e in range(BY_DVE, E):
                            at_least(act, placed_too, (E - BY_DVE) * g + e - BY_DVE)
                            act.activation(distance[:, :], T.iotaB[:, :], ACT.Abs, scale=-1.0,
                                           bias=flat2(eight_col[:, ds(g, 1), e:e + 1])).then_inc(measured, 1)
                            act.wait_ge(measured, (E - BY_DVE) * g + e - BY_DVE + 1)
                            at_least(act, sum_done, E * (g - 2) + e + 1)
                            act.activation(place(v, e), distance[:, :], ACT.Relu, scale=-1.0, bias=T.iotaB[:, 1:2])\
                                .then_inc(placed_too, 1)
                rounds(act, GROUPS // 2, scatter)

            @block.vector
            def _(dve):
                def gather(r, v):
                    if not isinstance(r, int) or r < TILES // 2:
                        if isinstance(r, int) and r == 3:
                            dve.wait_ge(T.rest_loaded, 16)
                        at_least(dve, g_done, r - 3)
                        dve.tensor_scalar(pick[v][:, :], T.pair_row[:, ds(r * 4 * P, 4 * P)], T.iotaP[:, 0:1], None,
                                          ALU.is_equal).then_inc(picked, 1)
                    if not isinstance(r, int) or r > 1:
                        q = r - 2
                        dve.wait_ge(g_done, q + 1)
                        dve.tensor_copy(XG[1][:, :, ds(4 * q, 4), :].rearrange("p e b k -> p b k e"),
                                        gathered((v - 2) % 4, 1)).then_inc(g_low, 1)
                gathers(dve, gather, 2)

                dve.wait_ge(cols_in, 32)

                def step(s, e, j):
                    r = s - 2

                    def result(m, half):
                        out, high = (flat2(Y[:, 4 * j + m, ds(e - 1, 1), n, :]) for n in (half, 0))
                        made, gain = bank[4 + j][:, m * P:(m + 1) * P], gain_col[:, 4 * j + m, ds(e - 1, 1)]
                        if half:
                            dve.wait_ge(y_high, 4 * r + m + 1)
                            return dve.scalar_tensor_tensor(out, made, gain, high, ALU.mult, ALU.subtract)
                        return dve.tensor_scalar(out, made, gain, None, ALU.mult).then_inc(y_high, 1)
                    for c in range(C1):
                        if live(s):
                            dve.wait_ge(high, 4 * s + c + 1)
                            dve.tensor_tensor(hh[j][:, 1, c, :], hidden[c % 2][:, :], hh[j][:, 0, c, :], ALU.subtract)\
                                .then_inc(low, 1)
                        if live(r):
                            if c == 0:
                                dve.wait_ge(y_done, r + 1)
                            else:
                                result(c - 1, 1)
                            result(c, 0)
                    if live(r):
                        result(C1 - 1, 1).then_inc(y_low, 1)
                steps(dve, step, 2)

                def scatter(it):
                    for v in range(2):
                        g = 2 * it + v
                        for e in range(BY_DVE):
                            at_least(dve, sum_done, E * g + e - RING + 1 if e >= RING
                                     else E * (g - 1) + BY_DVE + e - RING + 1)
                            dve.tensor_scalar(place(v, e), T.iotaB[:, :], flat2(eight_col[:, ds(g, 1), e:e + 1]), None,
                                              ALU.is_equal).then_inc(placed, 1)
                            if e == RING - 1 and (not isinstance(g, int) or g > 0):
                                add(g - 1, 1 - v)

                def add(g, v):
                    dve.wait_ge(sum_done, E * (g + 1))
                    x = T.X[:, ds(g * G, G), :]
                    sums = banks[:, 2 * v:2 * v + 2, :].rearrange("p b (t h d) -> p (b t) h d", t=2, h=2)
                    dve.tensor_tensor(x, sums[:, :, 1, :], x, ALU.add).then_inc(low_added, 1)
                    dve.wait_ge(low_added, g + 1)
                    dve.tensor_tensor(x, sums[:, :, 0, :], x, ALU.add).then_inc(x_done, 1)
                rounds(dve, GROUPS // 2, scatter)
                add(GROUPS - 1, 1)


def build(nc, I, out, stages):
    HELD.clear()
    with ExitStack() as ctx:
        a = Alloc(nc, ctx, "build")
        T = Tensors()
        T.X = a.sb("X", [P, TILES, D])
        T.ctxT = a.sb("ctxT", [P, NT])
        T.WT = a.sb("WT", [P, 8, P])
        T.gateT = a.sb("gateT", [P, 2, E])
        T.owns = a.sb("owns", [P, 2])
        T.row_i = a.sb("row_i", [P, 2], I32)
        T.bv0, T.bo0, T.bv1, T.bo1 = (a.sb(n, [P, D]) for n in ("bv0", "bo0", "bv1", "bo1"))
        T.gb0 = a.sb("gb0", [P, E])
        T.bcol = a.sb("bcol", [P, 3])
        T.identF = a.sb("identF", [P, P])
        T.identB = a.sb("identB", [P, P], BF16)
        T.before = a.sb("before", [P, P], BF16)
        T.ones = a.sb("ones", [P, P], BF16)
        T.half = a.sb("half", [P, 8])
        T.eps = a.sb("eps", [P, 8])
        T.mask = a.sb("mask", [P, P])
        T.iota_i = a.sb("iota_i", [P, 512], I32)
        T.iota_p = a.sb("iota_p", [P, 1], I32)
        T.iotaB = a.sb("iotaB", [P, 512])
        T.iotaP = a.sb("iotaP", [P, 1])
        T.slot = a.sb("slot", [P, TOPK, TILES], I32)
        T.share = a.sb("share", [P, TOPK, TILES])
        T.q_dram = nc.dram_tensor("q_dram", [4, P, NT], BF16, kind="Internal").ap()
        T.k_dram = nc.dram_tensor("k_dram", [2, P, 2 * NT], BF16, kind="Internal").ap()
        T.xs_dram = nc.dram_tensor("xs_dram", [SLOT_TILES * ST, 2 * D], BF16, kind="Internal").ap()
        T.ys_dram = nc.dram_tensor("ys_dram", [SLOT_TILES * ST, D], F32, kind="Internal").ap()
        T.owner = a.sb("owner", [P, SLOT_TILES], I32)
        T.db0 = a.sb("db0", [P, E, D])
        T.ub = a.sb("ub", [R0, E, C0])
        T.gb = a.sb("gb", [R0, E, C0])
        with ExitStack() as scope:
            b = Alloc(nc, scope, "part0")
            T.Wrel = b.sb("Wrel", [QROWS, SEQ // 2, P], BF16)
            T.wrel_t = b.sb("wrel_t", [DK, 2, P], BF16)
            T.Q = [b.sb(f"Q{v}", [QROWS, HP, GT], BF16) for v in range(2)]
            T.K = [b.sb(f"K{v}", [QROWS, HP, 2 * GT], BF16) for v in range(2)]
            T.sel = b.sb("sel", [48, HP, 2, SEQ], BF16)
            for stage in stages[0]:
                stage(nc, I, T)
        T.W1 = a.sb("W1", [P, 2, E, F1], BF16)
        T.W2 = a.sb("W2", [P, 2, E, C1 * P], BF16)
        T.XHL = a.sb("XHL", [P, TILES, 2, D], BF16)
        with ExitStack() as scope:
            b = Alloc(nc, scope, "part1")
            T.WU = b.sb("WU", [P, 2, E, F0], BF16)
            T.WG = b.sb("WG", [P, 2, E, F0], BF16)
            T.WD = b.sb("WD", [R0, 2, E, C0 * P], BF16)
            for stage in stages[1]:
                stage(nc, I, T)
        clear_semaphores(nc)
        T.pair_row = a.sb("pair_row", [P, BATCH * CAP * E], BF16)
        T.pair_dram = nc.dram_tensor("pair_dram", [BATCH * CAP * E], BF16, kind="Internal").ap()
        T.eight_dram = nc.dram_tensor("eight_dram", [BATCH * CAP * E], F32, kind="Internal").ap()
        T.gain_dram = nc.dram_tensor("gain_dram", [BATCH * CAP * E], F32, kind="Internal").ap()
        T.in_eight = a.sb("in_eight", [BATCH, P])
        T.gain = a.sb("gain", [BATCH, P])
        T.out = out
        for stage in stages[2]:
            stage(nc, I, T)


STAGES = ((prepare, project0, attend0),
          (route0, experts0),
          (attend1, route1, experts1))

_INS = ["x", "ctx_1024", "L0_xattn_Wq", "L0_xattn_bq", "L0_xattn_Wk", "L0_xattn_bk", "L0_xattn_Wv", "L0_xattn_bv",
        "L0_xattn_Wo", "L0_xattn_bo", "L0_xattn_w_rel", "L0_ffn_gate_w", "L0_ffn_gate_b", "L0_ffn_up_w",
        "L0_ffn_up_b", "L0_ffn_gp_w", "L0_ffn_gp_b", "L0_ffn_down_w", "L0_ffn_down_b", "L1_xattn_Wk",
        "L1_xattn_Wv", "L1_xattn_bv", "L1_xattn_Wq", "L1_xattn_bq", "L1_xattn_Wo", "L1_xattn_bo",
        "L1_ffn_gate_w", "L1_ffn_w1", "L1_ffn_w2"]


def kernel(**inputs):
    import numpy as _np
    import concourse.bacc as _bacc
    from concourse import mybir as _mybir
    from concourse.bass_utils import run_bass_kernel_spmd as _run

    nc = _bacc.Bacc("TRN2", target_bir_lowering=False, num_devices=1)
    arrays, args = {}, {}
    for name in _INS:
        a = _np.ascontiguousarray(inputs[name])
        arrays[f"in_{name}_dram"] = a
        args[name] = nc.dram_tensor(f"in_{name}_dram", a.shape, _mybir.dt.from_np(a.dtype), kind="ExternalInput").ap()
    out = nc.dram_tensor("out_0_dram", (BATCH, SEQ, D), _mybir.dt.float32, kind="ExternalOutput").ap()
    build(nc, args, out, STAGES)
    r = _run(nc, [arrays], core_ids=[0])
    return r.results[0]["out_0_dram"]
```
